# Optimizing a Trainium2 kernel written in Bass

```python
import numpy as np
import jax
import jax.numpy as jnp

def _softmax(x, axis=-1):
    return jax.nn.softmax(x, axis=axis)

def _gelu(x):
    return jax.nn.gelu(x, approximate=True)

def _silu(x):
    return jax.nn.silu(x)

def _sigmoid(x):
    return jax.nn.sigmoid(x)

def _layernorm(x, axis=-1, eps=1e-05):
    m = jnp.mean(x, axis=axis, keepdims=True)
    v = jnp.var(x, axis=axis, keepdims=True)
    return (x - m) / jnp.sqrt(v + eps)

def _scatter_add(tgt, idx, src, axis=0):
    return tgt.at[idx].add(src)

def _segment_sum(src, seg, n):
    return jax.ops.segment_sum(src, seg, n)
kernel_name = 'mk_seq_preln_d2_jaxref_r8_7962af'

def setup_inputs(seed: int=0):
    np.random.seed(seed)
    _w = jnp.asarray

    def _L0_attn_setup():
        import jax, jax.numpy as jnp
        import numpy as np
        HID = 256
        H = 16
        D = HID // H
        THETA = 10000.0

        def _rope(q, k):
            T = q.shape[1]
            half = D // 2
            inv_freq = 1.0 / THETA ** (jnp.arange(half, dtype=jnp.float32) / half)
            ang = jnp.arange(T, dtype=jnp.float32)[:, None] * inv_freq[None, :]
            cos = jnp.cos(ang)[None, :, None, :]
            sin = jnp.sin(ang)[None, :, None, :]

            def rot(x):
                x1, x2 = (x[..., :half], x[..., half:])
                return jnp.concatenate([x1 * cos - x2 * sin, x2 * cos + x1 * sin], axis=-1)
            return (rot(q), rot(k))
        key = jax.random.key(seed)
        ks = jax.random.split(key, 7)
        B, T = (1, 256)
        s = 1.0 / np.sqrt(HID)
        return {'hidden_states': jax.random.normal(ks[0], (B, T, HID), dtype=jnp.float32), 'Wq': jax.random.normal(ks[1], (HID, HID), dtype=jnp.float32) * s, 'Wk': jax.random.normal(ks[2], (HID, HID), dtype=jnp.float32) * s, 'Wv': jax.random.normal(ks[3], (HID, HID), dtype=jnp.float32) * s, 'Wb': jax.random.normal(ks[4], (HID, H), dtype=jnp.float32) * s, 'bb': jnp.zeros((H,), dtype=jnp.float32), 'Wo': jax.random.normal(ks[5], (HID, HID), dtype=jnp.float32) * s}
    _L0_attn_in = _L0_attn_setup()

    def _L0_ffn_setup():
        import jax, jax.numpy as jnp
        import numpy as np
        NUM_EXPERTS = 64
        TOP_K = 8
        HIDDEN = 256
        FFN = 96
        BATCH, SEQ = (1, 256)
        CAP_FACTOR = 2

        def _moe_forward(hidden_states, gate_w, w_gate, w_up, w_down):
            B, S, D = hidden_states.shape
            E = gate_w.shape[0]
            x = hidden_states.reshape(-1, D)
            N = x.shape[0]
            P = N * TOP_K
            C = CAP_FACTOR * P // E
            logits = x @ gate_w.T
            probs = jax.nn.softmax(logits, axis=-1)
            scores, idx = jax.lax.top_k(probs, TOP_K)
            flat_e = idx.reshape(-1)
            order = jnp.argsort(flat_e)
            e_sorted = flat_e[order]
            tok_sorted = order // TOP_K
            s_sorted = scores.reshape(-1)[order]
            counts = jnp.bincount(e_sorted, length=E)
            starts = jnp.cumsum(counts) - counts
            pos = jnp.arange(P) - starts[e_sorted]
            valid = pos < C
            safe_pos = jnp.minimum(pos, C - 1)
            xbuf = jnp.zeros((E, C, D), dtype=x.dtype).at[e_sorted, pos].set(x[tok_sorted], mode='drop')
            g = jnp.einsum('ecd,efd->ecf', xbuf, w_gate)
            u = jnp.einsum('ecd,efd->ecf', xbuf, w_up)
            y = jnp.einsum('ecf,edf->ecd', jax.nn.silu(g) * u, w_down)
            y_pair = y[e_sorted, safe_pos] * (s_sorted * valid)[:, None]
            out = jnp.zeros((N, D), dtype=x.dtype).at[tok_sorted].add(y_pair)
            return out.reshape(B, S, D)
        key = jax.random.key(seed)
        k1, k2, k3, k4, k5 = jax.random.split(key, 5)
        hidden_states = jax.random.normal(k1, (BATCH, SEQ, HIDDEN), dtype=jnp.float32)
        gate_w = jax.random.normal(k2, (NUM_EXPERTS, HIDDEN), dtype=jnp.float32) * 0.02
        w_gate = jax.random.normal(k3, (NUM_EXPERTS, FFN, HIDDEN), dtype=jnp.float32) * 0.02
        w_up = jax.random.normal(k4, (NUM_EXPERTS, FFN, HIDDEN), dtype=jnp.float32) * 0.02
        w_down = jax.random.normal(k5, (NUM_EXPERTS, HIDDEN, FFN), dtype=jnp.float32) * 0.02
        return {'hidden_states': hidden_states, 'gate_w': gate_w, 'w_gate': w_gate, 'w_up': w_up, 'w_down': w_down}
    _L0_ffn_in = _L0_ffn_setup()

    def _L1_attn_setup():
        import jax, jax.numpy as jnp
        import numpy as np
        D_MODEL = 256
        N_HEADS = 16
        HEAD_DIM = D_MODEL // N_HEADS
        SCALE = HEAD_DIM ** (-0.5)
        key = jax.random.key(seed)
        ks = jax.random.split(key, 9)
        B, L, D = (4, 512, D_MODEL)
        s = 1.0 / np.sqrt(D)
        inp = {'x': jax.random.normal(ks[0], (B, L, D), dtype=jnp.float32)}
        inp['Wq'] = jax.random.normal(ks[1], (D, D), dtype=jnp.float32) * s
        inp['bq'] = jnp.zeros((D,), dtype=jnp.float32)
        inp['Wk'] = jax.random.normal(ks[2], (D, D), dtype=jnp.float32) * s
        inp['bk'] = jnp.zeros((D,), dtype=jnp.float32)
        inp['Wv'] = jax.random.normal(ks[3], (D, D), dtype=jnp.float32) * s
        inp['bv'] = jnp.zeros((D,), dtype=jnp.float32)
        inp['Wo'] = jax.random.normal(ks[4], (D, D), dtype=jnp.float32) * s
        inp['bo'] = jnp.zeros((D,), dtype=jnp.float32)
        return inp
    _L1_attn_in = _L1_attn_setup()

    def _L1_ffn_setup():
        import jax, jax.numpy as jnp
        import numpy as np
        TOP_K = 2
        key = jax.random.key(seed)
        ks = jax.random.split(key, 5)
        B, S, H, F, E = (2, 512, 256, 512, 8)
        scale = 1.0 / np.sqrt(H)
        return {'hidden_states': jax.random.normal(ks[0], (B, S, H), dtype=jnp.float32), 'gate_w': jax.random.normal(ks[1], (E, H), dtype=jnp.float32) * scale, 'w1': jax.random.normal(ks[2], (E, F, H), dtype=jnp.float32) * scale, 'w2': jax.random.normal(ks[3], (E, H, F), dtype=jnp.float32) * (1.0 / np.sqrt(F)), 'w3': jax.random.normal(ks[4], (E, F, H), dtype=jnp.float32) * scale}
    _L1_ffn_in = _L1_ffn_setup()
    _d = {'L0_attn_hidden_states': _L0_attn_in['hidden_states'], 'L0_attn_Wq': _L0_attn_in['Wq'], 'L0_attn_Wk': _L0_attn_in['Wk'], 'L0_attn_Wv': _L0_attn_in['Wv'], 'L0_attn_Wb': _L0_attn_in['Wb'], 'L0_attn_bb': _L0_attn_in['bb'], 'L0_attn_Wo': _L0_attn_in['Wo'], 'L0_ffn_gate_w': _L0_ffn_in['gate_w'], 'L0_ffn_w_gate': _L0_ffn_in['w_gate'], 'L0_ffn_w_up': _L0_ffn_in['w_up'], 'L0_ffn_w_down': _L0_ffn_in['w_down'], 'L1_attn_Wq': _L1_attn_in['Wq'], 'L1_attn_bq': _L1_attn_in['bq'], 'L1_attn_Wk': _L1_attn_in['Wk'], 'L1_attn_bk': _L1_attn_in['bk'], 'L1_attn_Wv': _L1_attn_in['Wv'], 'L1_attn_bv': _L1_attn_in['bv'], 'L1_attn_Wo': _L1_attn_in['Wo'], 'L1_attn_bo': _L1_attn_in['bo'], 'L1_ffn_gate_w': _L1_ffn_in['gate_w'], 'L1_ffn_w1': _L1_ffn_in['w1'], 'L1_ffn_w2': _L1_ffn_in['w2'], 'L1_ffn_w3': _L1_ffn_in['w3']}
    _x0 = _d['L0_attn_hidden_states']
    _d['L0_attn_hidden_states'] = jax.random.normal(jax.random.fold_in(jax.random.key(seed), 1), (2, 512, 256), dtype=_x0.dtype)
    del _x0
    return _d

def reference(L0_attn_hidden_states, L0_attn_Wq, L0_attn_Wk, L0_attn_Wv, L0_attn_Wb, L0_attn_bb, L0_attn_Wo, L0_ffn_gate_w, L0_ffn_w_gate, L0_ffn_w_up, L0_ffn_w_down, L1_attn_Wq, L1_attn_bq, L1_attn_Wk, L1_attn_bk, L1_attn_Wv, L1_attn_bv, L1_attn_Wo, L1_attn_bo, L1_ffn_gate_w, L1_ffn_w1, L1_ffn_w2, L1_ffn_w3):

    def _L0_attn_ref(hidden_states, Wq, Wk, Wv, Wb, bb, Wo):
        import jax, jax.numpy as jnp
        import numpy as np
        HID = 256
        H = 16
        D = HID // H
        THETA = 10000.0

        def _rope(q, k):
            T = q.shape[1]
            half = D // 2
            inv_freq = 1.0 / THETA ** (jnp.arange(half, dtype=jnp.float32) / half)
            ang = jnp.arange(T, dtype=jnp.float32)[:, None] * inv_freq[None, :]
            cos = jnp.cos(ang)[None, :, None, :]
            sin = jnp.sin(ang)[None, :, None, :]

            def rot(x):
                x1, x2 = (x[..., :half], x[..., half:])
                return jnp.concatenate([x1 * cos - x2 * sin, x2 * cos + x1 * sin], axis=-1)
            return (rot(q), rot(k))
        B, T, _ = hidden_states.shape
        scale = 1.0 / np.sqrt(D)
        q = (hidden_states @ Wq).reshape(B, T, H, D)
        k = (hidden_states @ Wk).reshape(B, T, H, D)
        v = (hidden_states @ Wv).reshape(B, T, H, D)
        beta = hidden_states @ Wb + bb
        q, k = _rope(q, k)
        s = jnp.einsum('bihd,bjhd->bhij', k, k) * scale
        idx = jnp.arange(T)
        strict = idx[:, None] > idx[None, :]
        s = jnp.where(strict, s, -jnp.inf)
        m = jnp.max(s, axis=-1, keepdims=True)
        e = jnp.exp(s - jnp.where(jnp.isfinite(m), m, 0.0))
        e = jnp.where(strict, e, 0.0)
        denom = jnp.sum(e, axis=-1, keepdims=True)
        p = e / jnp.where(denom == 0, 1.0, denom)
        L = p * beta.transpose(0, 2, 1)[..., None]
        A = L + jnp.eye(T, dtype=L.dtype)[None, None]
        u = jax.scipy.linalg.solve_triangular(A, v.transpose(0, 2, 1, 3), lower=True)
        sc = jnp.einsum('bihd,bjhd->bhij', q, k) * scale
        causal = idx[:, None] >= idx[None, :]
        sc = jnp.where(causal, sc, -jnp.inf)
        attn = jax.nn.softmax(sc, axis=-1)
        o = jnp.einsum('bhij,bhjd->bihd', attn, u).reshape(B, T, HID)
        return o @ Wo

    def _L0_ffn_ref(hidden_states, gate_w, w_gate, w_up, w_down):
        import jax, jax.numpy as jnp
        import numpy as np
        NUM_EXPERTS = 64
        TOP_K = 8
        HIDDEN = 256
        FFN = 96
        BATCH, SEQ = (1, 256)
        CAP_FACTOR = 2

        def _moe_forward(hidden_states, gate_w, w_gate, w_up, w_down):
            B, S, D = hidden_states.shape
            E = gate_w.shape[0]
            x = hidden_states.reshape(-1, D)
            N = x.shape[0]
            P = N * TOP_K
            C = CAP_FACTOR * P // E
            logits = x @ gate_w.T
            probs = jax.nn.softmax(logits, axis=-1)
            scores, idx = jax.lax.top_k(probs, TOP_K)
            flat_e = idx.reshape(-1)
            order = jnp.argsort(flat_e)
            e_sorted = flat_e[order]
            tok_sorted = order // TOP_K
            s_sorted = scores.reshape(-1)[order]
            counts = jnp.bincount(e_sorted, length=E)
            starts = jnp.cumsum(counts) - counts
            pos = jnp.arange(P) - starts[e_sorted]
            valid = pos < C
            safe_pos = jnp.minimum(pos, C - 1)
            xbuf = jnp.zeros((E, C, D), dtype=x.dtype).at[e_sorted, pos].set(x[tok_sorted], mode='drop')
            g = jnp.einsum('ecd,efd->ecf', xbuf, w_gate)
            u = jnp.einsum('ecd,efd->ecf', xbuf, w_up)
            y = jnp.einsum('ecf,edf->ecd', jax.nn.silu(g) * u, w_down)
            y_pair = y[e_sorted, safe_pos] * (s_sorted * valid)[:, None]
            out = jnp.zeros((N, D), dtype=x.dtype).at[tok_sorted].add(y_pair)
            return out.reshape(B, S, D)
        return _moe_forward(hidden_states, gate_w, w_gate, w_up, w_down)

    def _L1_attn_ref(x, Wq, bq, Wk, bk, Wv, bv, Wo, bo):
        import jax, jax.numpy as jnp
        import numpy as np
        D_MODEL = 256
        N_HEADS = 16
        HEAD_DIM = D_MODEL // N_HEADS
        SCALE = HEAD_DIM ** (-0.5)
        B, L, D = x.shape
        H, Hd = (N_HEADS, HEAD_DIM)
        q = jnp.einsum('bld,ed->ble', x, Wq) + bq
        k = jnp.einsum('bld,ed->ble', x, Wk) + bk
        v = jnp.einsum('bld,ed->ble', x, Wv) + bv
        phi_q = jax.nn.elu(q) + 1.0
        phi_k = jax.nn.elu(k) + 1.0
        phi_q = phi_q.reshape(B, L, H, Hd)
        phi_k = phi_k.reshape(B, L, H, Hd)
        v = v.reshape(B, L, H, Hd)
        kv_sum = jnp.cumsum(phi_k * v, axis=1)
        context = (phi_q * kv_sum).reshape(B, L, D) * SCALE
        return jnp.einsum('bld,ed->ble', context, Wo) + bo

    def _L1_ffn_ref(hidden_states, gate_w, w1, w2, w3):
        import jax, jax.numpy as jnp
        import numpy as np
        TOP_K = 2
        B, S, H = hidden_states.shape
        E = gate_w.shape[0]
        x = hidden_states.reshape(-1, H)
        T = x.shape[0]
        logits = x @ gate_w.T
        probs = jax.nn.softmax(logits.astype(jnp.float32), axis=-1)
        top_w, top_idx = jax.lax.top_k(probs, TOP_K)
        top_w = top_w / jnp.sum(top_w, axis=-1, keepdims=True)
        combine = jnp.zeros((T, E), jnp.float32).at[jnp.arange(T)[:, None], top_idx].add(top_w)
        out = jnp.zeros_like(x)
        for e in range(E):
            h = jax.nn.silu(x @ w1[e].T) * (x @ w3[e].T)
            y = h @ w2[e].T
            out = out + combine[:, e:e + 1] * y
        return out.reshape(B, S, H)
    x = L0_attn_hidden_states
    x = x + _L0_attn_ref(_layernorm(x, axis=-1), L0_attn_Wq, L0_attn_Wk, L0_attn_Wv, L0_attn_Wb, L0_attn_bb, L0_attn_Wo)
    x = x + _L0_ffn_ref(_layernorm(x, axis=-1), L0_ffn_gate_w, L0_ffn_w_gate, L0_ffn_w_up, L0_ffn_w_down)
    x = x + _L1_attn_ref(_layernorm(x, axis=-1), L1_attn_Wq, L1_attn_bq, L1_attn_Wk, L1_attn_bk, L1_attn_Wv, L1_attn_bv, L1_attn_Wo, L1_attn_bo)
    x = x + _L1_ffn_ref(_layernorm(x, axis=-1), L1_ffn_gate_w, L1_ffn_w1, L1_ffn_w2, L1_ffn_w3)
    return x

_drawn_inputs = setup_inputs


def setup_inputs(seed=0):
    import zlib

    import numpy as np

    out = dict(_drawn_inputs(seed))
    spreads = {'L0_attn_bb': (0.0, 0.1),
     'L1_attn_bq': (0.0, 0.1),
     'L1_attn_bk': (0.0, 0.1),
     'L1_attn_bv': (0.0, 0.1),
     'L1_attn_bo': (0.0, 0.8)}
    factors = {'L0_ffn_gate_w': 8.0,
     'L0_ffn_w_gate': 8.0,
     'L0_ffn_w_up': 8.0,
     'L0_ffn_w_down': 8.0,
     'L1_ffn_gate_w': 2.961}
    for name, (base, spread) in spreads.items():
        noise = np.random.default_rng([zlib.crc32(name.encode()), seed]).standard_normal(out[name].shape)
        drawn = base * np.exp(spread * noise) if base else spread * noise
        out[name] = jnp.asarray(drawn.astype(out[name].dtype))
    for name, factor in factors.items():
        out[name] = (out[name] * factor).astype(out[name].dtype)
    return out
```

```python
from contextlib import ExitStack

import numpy as np

import concourse.bass as bass
from concourse import mybir

ALU = mybir.AluOpType
ACT = mybir.ActivationFunctionType
F32 = mybir.dt.float32
BF16 = mybir.dt.bfloat16
U32 = mybir.dt.uint32
AX = mybir.AxisListType

P = 128
N, D = 1024, 256
NT = N // P
KT = D // P
T = 512
H, HD = 16, 16
GH = 8
NI = T // P
UNITS = (H // GH) * (N // T)
SLOTS = 6
KR = SLOTS * HD
PART_A = (0, 0, 1, 1, 0, 2)
PART_B = (0, 1, 0, 1, 2, 0)
SB = 16
LEVELS = (16, 32, 64)
SCALE = HD ** -0.5
EPS = 1e-5
E0, F0, K0 = 64, 96, 8
CAP = 2 * N * K0 // E0
E1, F1 = 8, 512
BIG = 32768.0

OFF = {0: 0, 1: 512, 3: 896, 2: 1024}
WIDE = 10 * P
ROWAT = {3: 0, 2: 512, 0: 896, 1: 1024}


def build_kernel(nc, a, out, stop):
    with ExitStack() as ctx:
        def sb(name, shape, dt=F32):
            return ctx.enter_context(nc.sbuf_tensor(name, shape, dt))

        def sem(name):
            return ctx.enter_context(nc.semaphore(name))

        scores = ctx.enter_context(nc.psum_tensor("scores", [P, 2, 3 * 512], F32))
        misc = ctx.enter_context(nc.psum_tensor("misc", [P, 2, 512], F32))

        X = sb("X", [P, NT, D])
        xnT = sb("xnT", [P, KT, N])
        stats = sb("stats", [P, NT, 6])
        mv = sb("mv", [P, NT, 2])
        std = sb("std", [P, NT])
        rstd = sb("rstd", [P, NT])
        eps = sb("eps", [P, 1])
        cf = sb("cf", [P, a["cf"].shape[1]])
        cb = sb("cb", [P, a["cb"].shape[1]], BF16)
        identf = cf[:, 0:128]
        cosT = cf[:, 128:640]
        sinT = cf[:, 640:1152]
        eye16 = cf[:, 1152:1408]
        second = cf[:, 1408:1411]
        iota8 = cf[:, 1411:1419]
        onesf = cf[:, 1419:1420]
        pairs = cf[:, 1420:1548]
        identb = cb[:, 0:128]
        mask = {("q", 0): cb[:, 128:256], ("k", 0): cb[:, 384:512]}
        for i in range(1, NI):
            mask["q", i] = cb[:, 128:256]
            mask["k", i] = cb[:, 256:384]
        triu = cb[:, 512:640]
        onesb = cb[:, 640:768]

        s_x, s_w, s_eps = sem("x_loaded"), sem("weights_loaded"), sem("eps_set")
        s_var, s_std, s_xn = sem("variance"), sem("std"), sem("xn_tile")
        s_tr, s_xnT = sem("transposed"), sem("xnT_quarter")
        s_dv, s_po = sem("vector_chain"), sem("pool_chain")
        s_dv2, s_pk = sem("vector_chain_moe"), sem("weight_picked")
        s_out, s_zf = sem("stored"), sem("slots_zeroed")
        zero = sb("zero", [P, 1024])
        base0 = cf[:, 1548:1612]
        NZ = E0 * CAP * D // (P * 1024)
        xbuf = nc.dram_tensor("expert_rows", [E0 * CAP, D], F32, kind="Internal").ap()
        ybuf = nc.dram_tensor("expert_outputs", [E0 * CAP, D], F32, kind="Internal").ap()
        xb_v = xbuf.rearrange("(e n) d -> e n d", e=E0)
        yb_v = ybuf.rearrange("(e n) d -> e n d", e=E0)
        xb_z = xbuf.rearrange("(z p n) d -> z p (n d)", z=NZ, p=P)

        def chain(eng, s):
            count = [0]

            def link(ins):
                count[0] += 1
                ins.then_inc(s, 1)
                eng.wait_ge(s, count[0])
            return link

        def dve_norm(dve, link, l, xn):
            for t in range(NT):
                ins = nc.vector.bn_stats(stats[:, t, :], X[:, t, :])
            link(ins)
            for t in range(NT):
                ins = nc.vector.bn_aggr(mv[:, t, :], stats[:, t, :])
            ins.then_inc(s_var, 1)
            dve.wait_ge(s_std, l + 1)
            link(nc.vector.reciprocal(rstd[:], std[:]))
            for t in range(NT):
                nc.vector.tensor_scalar(xn[:, t, :], X[:, t, :], mv[:, t, 0:1], rstd[:, t:t + 1],
                                        ALU.subtract, ALU.mult).then_inc(s_xn, 1)

        def act_std(act, l):
            act.wait_ge(s_var, l + 1)
            nc.scalar.activation(std[:], mv[:, :, 1], ACT.Sqrt, bias=eps[:, 0:1]).then_inc(s_std, 1)

        def pe_transposes(pe, n, src, ready):
            for p in range(4):
                ready(p)
                if 4 * n + p - 1 > 0:
                    pe.wait_ge(s_xnT, 4 * n + p - 1)
                for k in range(KT):
                    for t in range(2):
                        c = (2 * k + t) * P
                        ins = nc.tensor.transpose(misc[:, p % 2, c:c + P],
                                                  src[:, 2 * p + t, k * P:(k + 1) * P], identf)
                ins.then_inc(s_tr, 1)

        def act_transposes(act, n):
            for p in range(4):
                act.wait_ge(s_tr, 4 * n + p + 1)
                nc.scalar.copy(xnT[:, :, 2 * P * p:2 * P * (p + 1)],
                               misc[:, p % 2, :].rearrange("p (k n) -> p k n", k=KT)).then_inc(s_xnT, 1)

        def xn_ready(pe, l):
            return lambda p: pe.wait_ge(s_xn, NT * l + 2 * p + 2)

        with ExitStack() as att:
            def sba(name, shape, dt=F32):
                return att.enter_context(nc.sbuf_tensor(name, shape, dt))

            early = sba("early", [P, 4608])
            wqk = early[:, 0:2048].rearrange("p (a k d) -> p a k d", a=4, k=KT)
            ropes = early[:, 2048:3072].rearrange("p (a n) -> p a n", a=2)
            parts = early[:, 3072:4608].bitcast(BF16).rearrange("p (a b n) -> p a b n", a=2, b=3)
            T1 = early[:, 0:3072].rearrange("p (a h n) -> p a h n", a=3, h=GH)
            wvb = sba("wvb", [P, KT, D + H])
            wo0 = sba("wo0", [P, KT, D])
            bb = sba("bb", [P, H])
            VB = sba("VB", [P, NT, D + H])
            AO = sba("AO", [P, NT, D])
            stk = {c: sba(f"stack_{c}", [P, 2, GH, T], BF16) for c in ("k", "B", "q")}
            nm = sba("nm", [P, 2, GH * NI])
            nmr = sba("nmr", [P, GH * NI])
            nms = sba("nms", [P, 2, 3, GH * NI], BF16)
            mrow = sba("mrow", [3 * GH * NI, 2, P], BF16)
            E = sba("E", [P, GH, WIDE])
            EQ = sba("EQ", [P, 2, WIDE])
            den = sba("den", [P, GH * NI])
            ng = sba("ng", [P, GH * NI])
            ngm = sba("ngm", [P, 3, GH * NI])
            G = sba("G", [P, 2, SB])
            LB = sba("LB", [P, 2, SB, SB])
            Y = sba("Y", [P, 2, SB, SB])
            YT = sba("YT", [P, 2, SB, SB])
            tmp = YT
            XT = sba("XT", [P, GH * NI, P])
            XR = sba("XR", [P, GH * NI, P])
            R = sba("R", [P, GH, HD])
            U = sba("U", [P, NI, GH, HD + 1])
            rec = sba("rec", [P, GH // 2, NI])

            scr = nc.dram_tensor("split_heads", [2, 3, D, N], BF16, kind="Internal").ap()
            edd = nc.dram_tensor("diagonals", [2, GH * NI, P, P], F32, kind="Internal").ap()
            xsd = nc.dram_tensor("inverses", [2, 2, P, 2, SB, SB], F32, kind="Internal").ap()

            s_pj, s_rf, s_parts = sem("projected"), sem("projection_read"), sem("parts_split")
            s_pw = [sem("parts_stored0"), sem("parts_stored1")]
            s_stk = [sem("stack_loaded0"), sem("stack_loaded1")]
            s_ones, s_cb = sem("ones_set"), sem("masks_ready")
            s_v, s_vc, s_vb = sem("v_projected"), sem("v_copied"), sem("beta_ready")
            s_sc, s_fd, s_fa = sem("scores_ready"), sem("maxima_taken"), sem("exps_done")
            s_nms, s_mt, s_mr, s_ml = sem("maxima_split"), sem("maxima_turned"), sem("maxima_rows"), sem("maxima_in_stack")
            s_dk, s_dq = sem("kk_masked"), sem("qk_masked")
            s_den, s_ng, s_gt, s_g = sem("denominators"), sem("g_ready"), sem("g_turned"), sem("g_in_blocks")
            s_ed, s_lb, s_y, s_ys, s_z, s_xt = (sem("diag_stored"), sem("blocks_loaded"), sem("blocks_inverted"),
                                                sem("inverses_stored"), sem("XT_zeroed"), sem("inverses_loaded"))
            s_tt, s_t1, s_pq, s_lv = sem("level_T"), sem("level_T1"), sem("level_PQ"), sem("level_joined")
            s_s, s_r, s_us, s_uv = sem("solve_sums"), sem("solve_r"), sem("solve_u"), sem("u_stored")
            s_o, s_ao, s_wo, s_xw = sem("attended"), sem("ao_ready"), sem("wo_done"), sem("x_attended")

            def blk(tile, h, jt, it):
                c = OFF[jt] + (it - jt) * P
                return tile[:, h, c:c + P]

            def halves(ap, n, which):
                return ap.rearrange("p h (b t n) -> p h b t n", t=2, n=n)[:, :, :, which, :]

            def scores_free(pe, n):
                u, m = n // 32, n % 32
                if n < 0:
                    return
                if m < 16:
                    pe.wait_ge(s_fd, 16 * u + m + 1)
                else:
                    pe.wait_ge(s_fa, 16 * u + m - 15)

            with nc.Block() as block:
                @block.tensor
                def _(pe):
                    pe.wait_ge(s_w, 16 * 9)
                    pe_transposes(pe, 0, AO, xn_ready(pe, 0))
                    pe.wait_ge(s_xnT, 4)
                    for w in range(8):
                        mt, half, c = w // 4, w // 2 % 2, w % 2
                        if w >= 2:
                            pe.wait_ge(s_rf, w - 1)
                        for rot in range(2):
                            for k in range(KT):
                                ins = nc.tensor.matmul(scores[:, w % 2, rot * 512:rot * 512 + T],
                                                       wqk[:, 2 * c + rot, k, mt * P:(mt + 1) * P],
                                                       xnT[:, k, half * T:(half + 1) * T],
                                                       start=(k == 0), stop=(k == KT - 1))
                        ins.then_inc(s_pj, 1)
                    for t in range(NT):
                        if t >= 2:
                            pe.wait_ge(s_vc, t - 1)
                        for k in range(KT):
                            ins = nc.tensor.matmul(misc[:, t % 2, 0:D + H], xnT[:, k, t * P:(t + 1) * P],
                                                   wvb[:, k, :], start=(k == 0), stop=(k == KT - 1))
                        ins.then_inc(s_v, 1)
                    pe.wait_ge(s_rf, 8)
                    pe.wait_ge(s_vc, NT)
                    pe.wait_ge(s_ones, 1)
                    pe.wait_ge(s_cb, 1)

                    def turn_maxima(u, c):
                        pe.wait_ge(s_nms, 2 * u + c + 1)
                        if u:
                            pe.wait_ge(s_ao, 2 * u)
                        nc.tensor.transpose(misc[0:96, c, 0:64].bitcast(BF16),
                                            nms[:, c, :, :].rearrange("p a b -> p (a b)"), identb
                                            ).then_inc(s_mt, 1)

                    for u in range(UNITS):
                        buf = u % 2
                        kB = stk["B"][:, buf]
                        pe.wait_ge(s_stk[buf], 16 * 18 * (u // 2 + 1))
                        for m in range(16):
                            c, h = "kq"[m // 8], m % 8
                            n = 32 * u + m
                            scores_free(pe, n - 2)
                            for it in range(NI):
                                w = (it + 1) * P
                                o = ROWAT[it]
                                nc.tensor.matmul(scores[:, n % 2, o:o + w],
                                                 stk[c][0:KR, buf, h, it * P:w], kB[0:KR, h, 0:w],
                                                 start=True, stop=False)
                                ins = nc.tensor.matmul(scores[:, n % 2, o + w - P:o + w], identb,
                                                       mask[c, it], start=False, stop=True)
                            ins.then_inc(s_sc, 1)
                            if m == 11:
                                turn_maxima(u, 0)

                        def transposed_scores(c, h):
                            n = 32 * u + 16 + 8 * c + h
                            scores_free(pe, n - 2)
                            for jt in range(NI):
                                o = OFF[jt]
                                ins = nc.tensor.matmul(scores[:, n % 2, o:o + T - jt * P],
                                                       kB[0:KR + 3, h, jt * P:(jt + 1) * P],
                                                       stk["kq"[c]][0:KR + 3, buf, h, jt * P:T],
                                                       start=True, stop=True)
                            ins.then_inc(s_sc, 1)

                        pe.wait_ge(s_ml, 96 * u + 48)
                        for h in range(GH):
                            transposed_scores(0, h)
                        turn_maxima(u, 1)
                        pe.wait_ge(s_mr, 2 * u + 1)
                        pe.wait_ge(s_dk, GH * (u + 1))
                        for h in range(GH):
                            for it in range(NI):
                                for jt in range(it + 1):
                                    ins = nc.tensor.matmul(misc[:, 0, NI * h + it:NI * h + it + 1],
                                                           blk(E, h, jt, it), onesf,
                                                           start=(jt == 0), stop=(jt == it))
                        ins.then_inc(s_den, 1)
                        pe.wait_ge(s_ng, u + 1)
                        pe.wait_ge(s_mr, 2 * u + 2)
                        nc.tensor.transpose(misc[0:GH * NI, 1, 0:P], ng[:], identf).then_inc(s_gt, 1)
                        pe.wait_ge(s_xt, 16 * 16 * (u + 1))
                        pe.wait_ge(s_fa, 16 * u + 8)

                        def join(q):
                            li, it = q // NI, q % NI
                            n = LEVELS[li]
                            g = 12 * u + q
                            pe.wait_ge(s_t1, g + 1)
                            if q >= 2:
                                pe.wait_ge(s_lv, g - 1)
                            for h in range(GH):
                                ap = XT[:, h * NI + it:h * NI + it + 1, :]
                                if li < 2:
                                    nc.tensor.matmul(scores[:, q % 2, 512 + 64 * h:576 + 64 * h], ap[:, 0, :],
                                                     halves(T1[:, li, h:h + 1, :], n, 0)[:, 0], start=True, stop=True)
                                ins = nc.tensor.matmul(scores[:, q % 2, 1024 + 64 * h:1088 + 64 * h],
                                                       T1[:, li, h, :], halves(ap, n, 1)[:, 0],
                                                       start=True, stop=True)
                            ins.then_inc(s_pq, 1)

                        for q in range(12):
                            li, it = q // NI, q % NI
                            g = 12 * u + q
                            if q >= 2:
                                pe.wait_ge(s_t1, g - 1)
                            if q >= 4:
                                pe.wait_ge(s_lv, g - 3)
                            for h in range(GH):
                                ap = XR[:, h * NI + it:h * NI + it + 1, :]
                                ins = nc.tensor.matmul(scores[:, q % 2, 64 * h:64 * h + 64], blk(E, h, it, it),
                                                       halves(ap, LEVELS[li], 0)[:, 0], start=True, stop=True)
                            ins.then_inc(s_tt, 1)
                            if q >= 1:
                                join(q - 1)
                        join(11)
                        pe.wait_ge(s_lv, 12 * (u + 1))
                        pe.wait_ge(s_g, u + 1)
                        for it in range(NI):
                            if it:
                                pe.wait_ge(s_uv, 4 * u + it)
                                for h in range(GH):
                                    for jt in range(it):
                                        ins = nc.tensor.matmul(misc[:, 0, HD * h:HD * (h + 1)],
                                                               blk(E, h, jt, it), U[:, jt, h, 0:HD],
                                                               start=(jt == 0), stop=(jt == it - 1))
                                ins.then_inc(s_s, 1)
                            pe.wait_ge(s_r, 4 * u + it + 1)
                            for h in range(GH):
                                ins = nc.tensor.matmul(misc[:, 1, HD * h:HD * (h + 1)],
                                                       XT[:, h * NI + it, :], R[:, h, :], start=True, stop=True)
                            ins.then_inc(s_us, 1)
                        pe.wait_ge(s_ml, 96 * u + 96)
                        pe.wait_ge(s_uv, 4 * (u + 1))

                        def attend(h):
                            pe.wait_ge(s_dq, GH * u + h + 1)
                            for it in range(NI):
                                c = (h % 4) * NI * (HD + 1) + it * (HD + 1)
                                for jt in range(it + 1):
                                    ins = nc.tensor.matmul(misc[:, h // 4, c:c + HD + 1],
                                                           blk(EQ, h % 2, jt, it), U[:, jt, h, :],
                                                           start=(jt == 0), stop=(jt == it))
                            ins.then_inc(s_o, 1)

                        for h in range(GH):
                            transposed_scores(1, h)
                            if h:
                                attend(h - 1)
                        attend(GH - 1)
                    pe_transposes(pe, 1, AO, lambda p: pe.wait_ge(s_ao, 2 * UNITS))
                    pe.wait_ge(s_xnT, 8)
                    for t in range(NT):
                        if t >= 2:
                            pe.wait_ge(s_xw, t - 1)
                        for k in range(KT):
                            ins = nc.tensor.matmul(misc[:, t % 2, 0:D], xnT[:, k, t * P:(t + 1) * P],
                                                   wo0[:, k, :], start=(k == 0), stop=(k == KT - 1))
                        ins.then_inc(s_wo, 1)

                @block.vector
                def _(dve):
                    link = chain(dve, s_dv)
                    nc.vector.memset(eps[:], EPS).then_inc(s_eps, 1)
                    link(nc.vector.memset(U[:], 1.0))
                    dve.wait_ge(s_x, 16)
                    dve_norm(dve, link, 0, AO)
                    dve.wait_ge(s_w, 16 * 9)
                    link(nc.vector.tensor_copy(cb[:], E[:, 0, 0:a["cb"].shape[1]]))
                    nc.vector.sem_inc(s_cb, 1)
                    for w in range(8):
                        dve.wait_ge(s_pj, w + 1)
                        if w >= 2:
                            dve.wait_ge(s_pw[w % 2], 16 * (w // 2))
                        a0, a1 = ropes[:, 0, :], ropes[:, 1, :]
                        nc.vector.tensor_tensor(a0, scores[:, w % 2, 0:T], cosT, ALU.mult)
                        ins = nc.vector.tensor_tensor(a1, scores[:, w % 2, 512:512 + T], sinT, ALU.mult)
                        link(ins)
                        nc.vector.sem_inc(s_rf, 1)
                        link(nc.vector.tensor_tensor(a0, a0, a1, ALU.add))
                        link(nc.vector.tensor_copy(parts[:, w % 2, 0, :], a0))
                        link(nc.vector.tensor_tensor(a0, a0, parts[:, w % 2, 0, :], ALU.subtract))
                        link(nc.vector.tensor_copy(parts[:, w % 2, 1, :], a0))
                        link(nc.vector.tensor_tensor(parts[:, w % 2, 2, :], a0, parts[:, w % 2, 1, :],
                                                     ALU.subtract))
                        nc.vector.sem_inc(s_parts, 1)
                    link(nc.vector.memset(early[:, 0:3072], 0.0))
                    dve.wait_ge(s_vc, NT)
                    bcol = VB[:, :, D:D + H]
                    link(nc.vector.tensor_tensor(bcol, bcol, bb[:].unsqueeze(1).to_broadcast([P, NT, H]), ALU.add))
                    for u in range(UNITS):
                        hg, b = u // 2, u % 2
                        for c in range(2):
                            for h in range(GH):
                                n = 32 * u + 8 * c + h
                                dve.wait_ge(s_sc, n + 1)
                                for it in range(NI):
                                    o = ROWAT[it]
                                    ins = nc.vector.tensor_reduce(nm[:, c, NI * h + it:NI * h + it + 1],
                                                                  scores[:, n % 2, o:o + (it + 1) * P],
                                                                  AX.X, ALU.max, negate=True)
                                ins.then_inc(s_fd, 1)
                            dve.wait_ge(s_fd, 16 * u + 8 * (c + 1))
                            if u:
                                dve.wait_ge(s_mt, 2 * (u - 1) + c + 1)
                            link(nc.vector.tensor_copy(nms[:, c, 0, :], nm[:, c, :]))
                            link(nc.vector.tensor_tensor(nmr[:], nm[:, c, :], nms[:, c, 0, :], ALU.subtract))
                            link(nc.vector.tensor_copy(nms[:, c, 1, :], nmr[:]))
                            nc.vector.tensor_tensor(nms[:, c, 2, :], nmr[:], nms[:, c, 1, :],
                                                    ALU.subtract).then_inc(s_nms, 1)
                        dve.wait_ge(s_den, u + 1)
                        link(nc.vector.tensor_scalar(den[:], misc[:, 0, 0:GH * NI], 1e-30, None, ALU.max))
                        link(nc.vector.reciprocal(den[:], den[:]))
                        beta = VB[:, b * NI:(b + 1) * NI, D + hg * GH:D + (hg + 1) * GH].rearrange("p i h -> p h i")
                        link(nc.vector.scalar_tensor_tensor(
                            out=ng[:].rearrange("p (h i) -> p h i", i=NI),
                            in0=den[:].rearrange("p (h i) -> p h i", i=NI), scalar=-1.0, in1=beta,
                            op0=ALU.mult, op1=ALU.mult))
                        nc.vector.sem_inc(s_ng, 1)
                        for li in range(3):
                            ins = nc.vector.tensor_scalar(ngm[:, li, :], ng[:], second[:, li:li + 1], None, ALU.mult)
                        link(ins)
                        dve.wait_ge(s_gt, u + 1)
                        for s4 in range(4):
                            ins = nc.vector.tensor_copy(G[32 * s4:32 * s4 + 32, :, :].rearrange("p a b -> p (a b)"),
                                                        misc[0:32, 1, 32 * s4:32 * s4 + 32])
                        link(ins)
                        nc.vector.sem_inc(s_g, 1)
                        dve.wait_ge(s_lb, 16 * 8 * (u + 1))
                        for s2 in range(2):
                            nc.vector.tensor_copy(Y[:, s2].rearrange("p a b -> p (a b)"), eye16)
                            ins = nc.vector.tensor_tensor(
                                LB[:, s2], LB[:, s2], G[:, s2].unsqueeze(1).to_broadcast([P, SB, SB]), ALU.mult)
                        link(ins)
                        for i in range(1, SB):
                            row = LB[:, :, 0:i, i].unsqueeze(2).to_broadcast([P, 2, i, i])
                            link(nc.vector.tensor_tensor(tmp[:, :, 0:i, 0:i], Y[:, :, 0:i, 0:i], row, ALU.mult))
                            link(nc.vector.tensor_reduce(Y[:, :, 0:i, i], tmp[:, :, 0:i, 0:i], AX.X, ALU.add))
                        link(nc.vector.tensor_copy(YT[:], Y[:].rearrange("p s c i -> p s i c")))
                        nc.vector.sem_inc(s_y, 1)
                        dve.wait_ge(s_xt, 16 * 16 * (u + 1))

                        def joined(q):
                            li, it = q // NI, q % NI
                            n = LEVELS[li]
                            dve.wait_ge(s_pq, 12 * u + q + 1)
                            for X_, o, which in ((XR, 512, 0), (XT, 1024, 1)):
                                if X_ is XR and li == 2:
                                    continue
                                dst = halves(X_[:].rearrange("p (h i) c -> p h i c", i=NI)[:, :, it, :], n, which)
                                src = scores[:, q % 2, o:o + 512].rearrange("p (h b n) -> p h b n", h=GH, n=n)
                                ins = nc.vector.tensor_tensor(dst, src, dst, ALU.add)
                            ins.then_inc(s_lv, 1)

                        for q in range(12):
                            li, it = q // NI, q % NI
                            n = LEVELS[li]
                            if q:
                                joined(q - 1)
                            dve.wait_ge(s_tt, 12 * u + q + 1)
                            nb = 64 // n
                            g_ = ngm[:, li, :].rearrange("p (h i) -> p h i", i=NI)[:, :, it]
                            if nb > 1:
                                g_ = g_.unsqueeze(2).unsqueeze(3).to_broadcast([P, GH, nb, n])
                                dst = halves(T1[:, li], n, 0)
                                src = scores[:, q % 2, 0:512].rearrange("p (h b n) -> p h b n", h=GH, n=n)
                            else:
                                g_ = g_.unsqueeze(2).to_broadcast([P, GH, n])
                                dst = T1[:, li, :, 0:n]
                                src = scores[:, q % 2, 0:512].rearrange("p (h n) -> p h n", h=GH)
                            ins = nc.vector.tensor_tensor(dst, src, g_, ALU.mult)
                            if li < 2:
                                link(ins)
                                m_ = pairs[:, 64 * li:64 * li + 64].rearrange("p (b n) -> p b n", n=n)
                                ins = nc.vector.tensor_tensor(
                                    dst, dst, m_.unsqueeze(1).to_broadcast([P, GH, nb, n]), ALU.mult)
                            ins.then_inc(s_t1, 1)
                        joined(11)
                        for it in range(NI):
                            v = VB[:, b * NI + it, hg * P:(hg + 1) * P].rearrange("p (h d) -> p h d", d=HD)
                            g_ = ng[:].rearrange("p (h i) -> p h i", i=NI)[:, :, it].unsqueeze(2).to_broadcast([P, GH, HD])
                            if it:
                                dve.wait_ge(s_s, 3 * u + it)
                                link(nc.vector.tensor_tensor(
                                    R[:], misc[:, 0, 0:P].rearrange("p (h d) -> p h d", d=HD), g_, ALU.mult))
                                nc.vector.tensor_tensor(R[:], R[:], v, ALU.add).then_inc(s_r, 1)
                            else:
                                nc.vector.tensor_copy(R[:], v).then_inc(s_r, 1)
                            dve.wait_ge(s_us, 4 * u + it + 1)
                            nc.vector.tensor_copy(U[:, it, :, 0:HD],
                                                  misc[:, 1, 0:P].rearrange("p (h d) -> p h d", d=HD)
                                                  ).then_inc(s_uv, 1)
                        for hh in range(2):
                            dve.wait_ge(s_o, GH * u + 4 * (hh + 1))
                            o4 = misc[:, hh, 0:4 * NI * (HD + 1)].rearrange("p (h i d) -> p h i d", h=4, i=NI)
                            if u or hh:
                                dve.wait_ge(s_ao, 2 * u + hh)
                            link(nc.vector.reciprocal(rec[:], o4[:, :, :, HD]))
                            for h in range(4):
                                c = (hg * GH + hh * 4 + h) * HD
                                ins = nc.vector.tensor_tensor(
                                    AO[:, b * NI:(b + 1) * NI, c:c + HD], o4[:, h, :, 0:HD],
                                    rec[:, h].unsqueeze(2).to_broadcast([P, NI, HD]), ALU.mult)
                            ins.then_inc(s_ao, 1)
                    for t in range(NT):
                        dve.wait_ge(s_wo, t + 1)
                        nc.vector.tensor_tensor(X[:, t, :], misc[:, t % 2, 0:D], X[:, t, :], ALU.add).then_inc(s_xw, 1)
                    dve.wait_ge(s_xw, NT)

                @block.scalar
                def _(act):
                    act.wait_ge(s_eps, 1)
                    act_std(act, 0)
                    act_transposes(act, 0)
                    for t in range(NT):
                        act.wait_ge(s_v, t + 1)
                        nc.scalar.copy(VB[:, t, :], misc[:, t % 2, 0:D + H]).then_inc(s_vc, 1)

                    def rows(u, c):
                        act.wait_ge(s_mt, 2 * u + c + 1)
                        if u:
                            act.wait_ge(s_ml, 96 * (u - 1) + 48 * (c + 1))
                        nc.scalar.copy(mrow[:, c, :], misc[0:96, c, 0:64].bitcast(BF16)).then_inc(s_mr, 1)

                    for u in range(UNITS):
                        rows(u, 0)
                        if u:
                            act.wait_ge(s_o, GH * u)
                        for c in range(2):
                            for h in range(GH):
                                n = 32 * u + 16 + 8 * c + h
                                act.wait_ge(s_sc, n + 1)
                                if c and 8 * u + h - 1 > 0:
                                    act.wait_ge(s_o, GH * u + h - 1)
                                dst = EQ[:, h % 2, :] if c else E[:, h, :]
                                nc.scalar.activation(dst, scores[:, n % 2, 0:WIDE], ACT.Exp,
                                                     scale=SCALE).then_inc(s_fa, 1)
                            if c == 0:
                                rows(u, 1)
                        if u == 0:
                            act.wait_ge(s_ones, 2)
                        for z in range(NZ // UNITS):
                            act.dma_start(xb_z[u * (NZ // UNITS) + z], zero[:]).then_inc(s_zf, 16)
                    act_transposes(act, 1)

                @block.gpsimd
                def _(pool):
                    link = chain(pool, s_po)
                    for c in range(2):
                        link(nc.gpsimd.memset(stk["B"][96:99, c], 1.0))
                    nc.gpsimd.sem_inc(s_ones, 1)
                    link(nc.gpsimd.memset(zero[:], 0.0))
                    nc.gpsimd.sem_inc(s_ones, 1)
                    for u in range(UNITS):
                        if u:
                            pool.wait_ge(s_us, 4 * u)
                            pool.wait_ge(s_lv, 12 * u)
                        link(nc.gpsimd.memset(XT[:], 0.0))
                        link(nc.gpsimd.memset(XR[:], 0.0))
                        nc.gpsimd.sem_inc(s_z, 1)
                        for c in range(2):
                            for h in range(GH):
                                pool.wait_ge(s_fa, 16 * u + 8 * c + h + 1)
                                e = EQ[:, h % 2, :] if c else E[:, h, :]
                                for d in (e[:, 0:1024].rearrange("p (a n) -> p a n", a=2)[:, :, 0:P],
                                          e[:, 896:1152].rearrange("p (a n) -> p a n", a=2)):
                                    ins = nc.gpsimd.affine_select(
                                        out=d, in_=d, pattern=[[0, 2], [1, P]], base=0, channel_multiplier=-1,
                                        compare_op=ALU.is_ge if c else ALU.is_gt, fill=0.0)
                                ins.then_inc(s_dq if c else s_dk, 1)

                @block.sync
                def _(sp):
                    sp.dma_start(X[:], a["x"].rearrange("(t p) d -> p t d", p=P)).then_inc(s_x, 16)
                    sp.dma_start(cf[:], a["cf"]).then_inc(s_w, 16)
                    sp.dma_start(E[:, 0, 0:a["cb"].shape[1]], a["cb"]).then_inc(s_w, 16)
                    for i, name in enumerate(("wk0", "wk0r", "wq0", "wq0r")):
                        sp.dma_start(wqk[:, i], a[name].rearrange("(k p) n -> p k n", p=P)).then_inc(s_w, 16)
                    sp.dma_start(wvb[:], a["wvb0"].rearrange("(k p) n -> p k n", p=P)).then_inc(s_w, 16)
                    sp.dma_start(wo0[:], a["wo0"].rearrange("(k p) n -> p k n", p=P)).then_inc(s_w, 16)
                    sp.dma_start(bb[:], a["bb"].partition_broadcast(P)).then_inc(s_w, 16)

                    def store_parts(w):
                        mt, half, c = w // 4, w // 2 % 2, w % 2
                        sp.wait_ge(s_parts, w + 1)
                        sp.dma_start(scr[c, :, mt * P:(mt + 1) * P, half * T:(half + 1) * T].rearrange("t p n -> p t n"),
                                     parts[:, w % 2]).then_inc(s_pw[w % 2], 16)

                    def load_stacks(u):
                        hg, b = u // 2, u % 2
                        sp.wait_ge(s_pw[0], 16 * (u + 1))
                        sp.wait_ge(s_pw[1], 16 * (u + 1))
                        if u >= 2:
                            sp.wait_ge(s_o, GH * (u - 1))
                        for c, x, order in (("k", 0, PART_A), ("B", 0, PART_B), ("q", 1, PART_A)):
                            for s, part in enumerate(order):
                                sp.dma_start(stk[c][HD * s:HD * (s + 1), u % 2],
                                             scr[x, part, hg * P:(hg + 1) * P, b * T:(b + 1) * T]
                                             .rearrange("(h d) n -> d h n", d=HD)).then_inc(s_stk[u % 2], 16)

                    for w in range(8):
                        store_parts(w)
                        if w % 2 and w < 4:
                            load_stacks(w // 2)
                    for u in range(UNITS):
                        for c in range(2):
                            def maxima_rows(c=c):
                                sp.wait_ge(s_mr, 2 * u + c + 1)
                                for part in range(3):
                                    sp.dma_start(stk["kq"[c]][KR + part:KR + part + 1, u % 2].rearrange("p h n -> p (h n)"),
                                                 mrow[32 * part:32 * part + 32, c, :]).then_inc(s_ml, 16)
                            maxima_rows()
                            if c:
                                continue
                        sp.wait_ge(s_dk, GH * (u + 1))
                        for it in range(NI):
                            sp.dma_start(edd[u % 2].rearrange("(h i) j q -> i j h q", i=NI)[it],
                                         E[:, :, OFF[it]:OFF[it] + P]).then_inc(s_ed, 16)
                        sp.wait_ge(s_ed, 16 * 4 * (u + 1))
                        if u:
                            sp.wait_ge(s_y, u)
                        for s in range(8):
                            sp.dma_start(LB[32 * (s // 2):32 * (s // 2) + 32, s % 2],
                                         edd[u % 2, :, SB * s:SB * (s + 1), SB * s:SB * (s + 1)]).then_inc(s_lb, 16)
                        sp.wait_ge(s_y, u + 1)
                        sp.dma_start(xsd[u % 2, 0], Y[:]).then_inc(s_ys, 16)
                        sp.dma_start(xsd[u % 2, 1], YT[:]).then_inc(s_ys, 16)
                        sp.wait_ge(s_ys, 32 * (u + 1))
                        sp.wait_ge(s_z, u + 1)
                        for x, dst in enumerate((XT, XR)):
                            for s in range(8):
                                sp.dma_start(dst[SB * s:SB * (s + 1), :, SB * s:SB * (s + 1)],
                                             xsd[u % 2, x, 32 * (s // 2):32 * (s // 2) + 32, s % 2]
                                             .rearrange("e c i -> c e i")).then_inc(s_xt, 16)
                        if u + 2 < UNITS:
                            load_stacks(u + 2)
                    if stop == 1:
                        sp.wait_ge(s_xw, NT)
                        sp.dma_start(out.rearrange("(t p) d -> p t d", p=P), X[:]).then_inc(s_out, 16)
                        sp.wait_ge(s_out, 16)
        if stop == 1:
            return

        with ExitStack() as moe:
            def sbm(name, shape, dt=F32):
                return moe.enter_context(nc.sbuf_tensor(name, shape, dt))

            xn = sbm("xn_moe", [P, NT, D])
            gate0 = sbm("gate0", [P, KT, E0])
            pr = sbm("probs", [P, NT, E0])
            sel = sbm("sel", [P, NT, E0])
            selb = sbm("selb", [P, NT, E0], BF16)
            val = sbm("val", [P, NT, E0])
            slot = sbm("slot", [P, NT, E0])
            Vg = sbm("Vg", [P, NT, E0])
            Vs = sbm("Vs", [P, NT, E0])
            pick = sbm("pick", [P, 2, E0])
            mx = sbm("mx", [P, NT])
            m8 = sbm("m8", [P, NT, K0])
            V8g = sbm("V8g", [P, NT, K0])
            V8s = sbm("V8s", [P, NT, K0])
            ig = sbm("gather_slots", [P, NT, K0], U32)
            isc = sbm("scatter_slots", [P, NT, K0], U32)
            w8 = sbm("w8", [P, NT, K0])
            NB = 4
            xg = sbm("xg", [P, NB, 2, D])
            wgu = sbm("wgu", [P, NB, KT, 2 * F0])
            wd = sbm("wd", [F0, NB, D])
            xgT = sbm("xgT", [P, 2, KT, CAP])
            sg = sbm("sg", [F0, 2, CAP])
            hT = sbm("hT", [F0, 2, CAP])
            yb = sbm("yb", [P, NB, 2, D])
            NG = 16
            gb = sbm("gb", [P, NG, D])

            s_gw, s_lg, s_sub, s_ex = sem("gate_loaded"), sem("logits"), sem("logits_shifted"), sem("logits_exp")
            s_sel, s_rk, s_idx, s_sc0, s_w8 = (sem("selected"), sem("ranks"), sem("slots_ready"), sem("rows_scattered"),
                                              sem("weights_ready"))
            s_ld = [sem(f"expert_loaded{j}") for j in range(NB)]
            s_t, s_xt0, s_gu, s_sl = sem("rows_turned"), sem("rows_copied"), sem("gate_up"), sem("silu_done")
            s_h, s_y0, s_yv = sem("hidden_ready"), sem("down_done"), sem("down_copied")
            s_st = [sem(f"y_stored{j}") for j in range(NB)]
            s_gb = [sem(f"gathered{j}") for j in range(NG)]
            s_acc = sem("row_added")

            def steps(fori, total, body):
                body(0, True, False)
                body(1, False, False)
                with fori(2, total - 1) as i:
                    body(i, False, False)
                body(total - 1, False, True)

            with nc.Block() as block:
                @block.tensor
                def _(pe):
                    pe_transposes(pe, 2, xn, xn_ready(pe, 1))
                    pe.wait_ge(s_xnT, 12)
                    pe.wait_ge(s_gw, 16)
                    for t in range(NT):
                        for k in range(KT):
                            ins = nc.tensor.matmul(scores[:, 0, t * E0:(t + 1) * E0], xnT[:, k, t * P:(t + 1) * P],
                                                   gate0[:, k, :], start=(k == 0), stop=(k == KT - 1))
                    ins.then_inc(s_lg, 1)
                    pe.wait_ge(s_sel, 1)
                    for t in range(NT):
                        for q in range(t + 1):
                            ins = nc.tensor.matmul(scores[:, 1, t * E0:(t + 1) * E0], triu if q == t else onesb,
                                                   selb[:, q, :], start=(q == 0), stop=(q == t))
                    ins.then_inc(s_rk, 1)
                    pe.wait_ge(s_w8, 1)

                    def turn(j, i):
                        pe.wait_ge(s_ld[j], (i + 1) * 48)
                        for k in range(KT):
                            for t in range(2):
                                c = (2 * k + t) * P
                                ins = nc.tensor.transpose(misc[:, j % 2, c:c + P], xg[:, j, t, k * P:(k + 1) * P], identf)
                        ins.then_inc(s_t, 1)

                    def down(j, e, wait):
                        pe.wait_ge(s_h, e + 1)
                        if wait:
                            pe.wait_ge(s_yv, e - 1)
                        for t in range(2):
                            ins = nc.tensor.matmul(scores[:, j % 2, 512 + t * D:512 + (t + 1) * D],
                                                   hT[:, j % 2, t * P:(t + 1) * P], wd[:, j, :], start=True, stop=True)
                        ins.then_inc(s_y0, 1)

                    def body(i, first, last):
                        for j in range(NB):
                            e = NB * i + j
                            if not (last and j == NB - 1):
                                turn((j + 1) % NB, i + (j + 1) // NB)
                            pe.wait_ge(s_xt0, e + 1)
                            for g in range(2):
                                for k in range(KT):
                                    ins = nc.tensor.matmul(scores[0:F0, j % 2, g * CAP:(g + 1) * CAP],
                                                           wgu[:, j, k, g * F0:(g + 1) * F0], xgT[:, j % 2, k, :],
                                                           start=(k == 0), stop=(k == KT - 1))
                            ins.then_inc(s_gu, 1)
                            if not (first and j == 0):
                                down((j - 1) % NB, e - 1, not (first and j < 3))

                    turn(0, 0)
                    steps(pe.Fori, E0 // NB, body)
                    down(NB - 1, E0 - 1, True)

                @block.vector
                def _(dve):
                    link = chain(dve, s_dv2)
                    dve_norm(dve, link, 1, xn)
                    dve.wait_ge(s_lg, 1)
                    lg = scores[:, 0, 0:512].rearrange("p (t e) -> p t e", e=E0)
                    bc = [P, NT, E0]
                    link(nc.vector.tensor_reduce(mx[:], lg, AX.X, ALU.max))
                    nc.vector.tensor_tensor(pr[:], lg, mx[:].unsqueeze(2).to_broadcast(bc), ALU.subtract).then_inc(s_sub, 1)
                    dve.wait_ge(s_ex, 1)
                    link(nc.vector.tensor_reduce(mx[:], pr[:], AX.X, ALU.add))
                    link(nc.vector.reciprocal(mx[:], mx[:]))
                    link(nc.vector.tensor_tensor(pr[:], pr[:], mx[:].unsqueeze(2).to_broadcast(bc), ALU.mult))
                    for t in range(NT):
                        ins = nc.vector.max(m8[:, t, :], pr[:, t, :])
                    link(ins)
                    for t in range(NT):
                        ins = nc.vector.match_replace(sel[:, t, :], m8[:, t, :], pr[:, t, :], -1.0)
                    link(ins)
                    nc.vector.tensor_scalar(selb[:], sel[:], 0.0, None, ALU.is_lt).then_inc(s_sel, 1)
                    dve.wait_ge(s_sel, 1)
                    dve.wait_ge(s_rk, 1)
                    rk = scores[:, 1, 0:512].rearrange("p (t e) -> p t e", e=E0)
                    link(nc.vector.tensor_scalar(slot[:], rk, float(CAP), -1.0, ALU.min, ALU.add))
                    link(nc.vector.tensor_scalar(val[:], rk, float(CAP), None, ALU.is_le))
                    link(nc.vector.tensor_tensor(slot[:], slot[:], base0.unsqueeze(1).to_broadcast(bc), ALU.add))
                    link(nc.vector.tensor_scalar(slot[:], slot[:], -1.0, BIG, ALU.mult, ALU.add))
                    link(nc.vector.tensor_tensor(Vg[:], slot[:], selb[:], ALU.mult))
                    link(nc.vector.tensor_tensor(Vs[:], Vg[:], val[:], ALU.mult))
                    for t in range(NT):
                        nc.vector.max(V8s[:, t, :], Vs[:, t, :])
                        ins = nc.vector.max(V8g[:, t, :], Vg[:, t, :])
                    link(ins)
                    nc.vector.tensor_scalar(isc[:], V8s[:], -1.0, BIG, ALU.mult, ALU.add).then_inc(s_idx, 1)
                    nc.vector.tensor_scalar(ig[:], V8g[:], -1.0, BIG, ALU.mult, ALU.add).then_inc(s_idx, 1)
                    link(nc.vector.tensor_tensor(pr[:], pr[:], val[:], ALU.mult))
                    for g in range(NT * K0):
                        t, k = g // K0, g % K0
                        if g >= 2:
                            dve.wait_ge(s_pk, g - 1)
                        nc.vector.scalar_tensor_tensor(
                            out=pick[:, g % 2, :], in0=Vg[:, t, :], scalar=V8g[:, t, k:k + 1], in1=pr[:, t, :],
                            op0=ALU.is_equal, op1=ALU.mult, accum_out=w8[:, t, k:k + 1]).then_inc(s_pk, 1)
                    dve.wait_ge(s_pk, NT * K0)
                    nc.vector.sem_inc(s_w8, 1)

                    def copy_down(j, e, n):
                        dve.wait_ge(s_y0, e + 1)
                        if n is not None:
                            dve.wait_ge(s_st[j], n * 16)
                        nc.vector.tensor_copy(yb[:, j].rearrange("p t d -> p (t d)"),
                                              scores[:, j % 2, 512:1024]).then_inc(s_yv, 1)

                    def body(i, first, last):
                        for j in range(NB):
                            e = NB * i + j
                            dve.wait_ge(s_sl, e + 1)
                            nc.vector.tensor_tensor(hT[:, j % 2, :], sg[:, j % 2, :], scores[0:F0, j % 2, CAP:2 * CAP],
                                                    ALU.mult).then_inc(s_h, 1)
                            if j:
                                copy_down(j - 1, e - 1, None if first else i)
                            elif not first:
                                copy_down(NB - 1, e - 1, None if isinstance(i, int) and i == 1 else i - 1)

                    steps(dve.Fori, E0 // NB, body)
                    copy_down(NB - 1, E0 - 1, E0 // NB - 1)
                    for g in range(NT * K0):
                        k, t = g // NT, g % NT
                        dve.wait_ge(s_gb[g % NG], 16 * (g // NG + 1))
                        if g >= NT:
                            dve.wait_ge(s_acc, g - NT + 1)
                        nc.vector.scalar_tensor_tensor(out=X[:, t, :], in0=gb[:, g % NG, :], scalar=w8[:, t, k:k + 1],
                                                       in1=X[:, t, :], op0=ALU.mult, op1=ALU.add).then_inc(s_acc, 1)
                    dve.wait_ge(s_acc, NT * K0)

                @block.scalar
                def _(act):
                    act_std(act, 1)
                    act_transposes(act, 2)
                    act.wait_ge(s_sub, 1)
                    nc.scalar.activation(pr[:], pr[:], ACT.Exp).then_inc(s_ex, 1)

                    def copy_rows(j, e):
                        act.wait_ge(s_t, e + 1)
                        nc.scalar.copy(xgT[:, j % 2].rearrange("p k n -> p (k n)"), misc[:, j % 2, :]).then_inc(s_xt0, 1)

                    def body(i, first, last):
                        for j in range(NB):
                            e = NB * i + j
                            if not (last and j == NB - 1):
                                copy_rows(j + 1, e + 1)
                            act.wait_ge(s_gu, e + 1)
                            nc.scalar.activation(sg[:, j % 2, :], scores[0:F0, j % 2, 0:CAP], ACT.Silu).then_inc(s_sl, 1)

                    copy_rows(0, 0)
                    steps(act.Fori, E0 // NB, body)

                @block.gpsimd
                def _(pool):
                    pool.wait_ge(s_idx, 2)
                    pool.wait_ge(s_zf, 16 * NZ)
                    for t in range(NT):
                        for k in range(K0):
                            pool.indirect_dma_start(
                                out=xbuf, out_offset=bass.IndirectOffsetOnAxis(ap=isc[:, t, k:k + 1], axis=0),
                                in_=xn[:, t, :], in_offset=None, bounds_check=E0 * CAP - 1,
                                oob_is_err=False).then_inc(s_sc0, 16)
                    for j in range(NB):
                        pool.wait_ge(s_st[j], 16 * (E0 // NB))
                    for g in range(NT * K0):
                        k, t = g // NT, g % NT
                        if g >= NG:
                            pool.wait_ge(s_acc, g - NG + 1)
                        pool.indirect_dma_start(
                            out=gb[:, g % NG, :], out_offset=None, in_=ybuf,
                            in_offset=bass.IndirectOffsetOnAxis(ap=ig[:, t, k:k + 1], axis=0),
                            bounds_check=E0 * CAP - 1, oob_is_err=True).then_inc(s_gb[g % NG], 16)

                @block.sync
                def _(sp):
                    sp.dma_start(gate0[:], a["gate0"].rearrange("(k p) n -> p k n", p=P)).then_inc(s_gw, 16)

                    def load_weights(j, e):
                        sp.dma_start(wgu[:, j], a["wgu0"][e].rearrange("p (k n) -> p k n", k=KT)).then_inc(s_ld[j], 16)
                        sp.dma_start(wd[:, j], a["wd0"][e]).then_inc(s_ld[j], 16)

                    def load_rows(j, e):
                        sp.dma_start(xg[:, j], xb_v[e].rearrange("(t p) d -> p t d", p=P)).then_inc(s_ld[j], 16)

                    for e in range(3):
                        load_weights(e, e)
                    sp.wait_ge(s_sc0, 16 * NT * K0)
                    for e in range(3):
                        load_rows(e, e)

                    def body(i, first, last):
                        for j in range(NB):
                            e = NB * i + j
                            if not (first and j == 0):
                                sp.wait_ge(s_y0, e)
                            if not (last and j > 0):
                                load_weights((j + 3) % NB, e + 3)
                                load_rows((j + 3) % NB, e + 3)
                            if not (first and j == 0):
                                jj = (j - 1) % NB
                                sp.wait_ge(s_yv, e)
                                sp.dma_start(yb_v[e - 1].rearrange("(t p) d -> p t d", p=P), yb[:, jj]).then_inc(s_st[jj], 16)

                    steps(sp.Fori, E0 // NB, body)
                    sp.wait_ge(s_yv, E0)
                    sp.dma_start(yb_v[E0 - 1].rearrange("(t p) d -> p t d", p=P), yb[:, NB - 1]).then_inc(s_st[NB - 1], 16)
                    if stop == 2:
                        sp.wait_ge(s_acc, NT * K0)
                        sp.dma_start(out.rearrange("(t p) d -> p t d", p=P), X[:]).then_inc(s_out, 16)
                        sp.wait_ge(s_out, 16)
        if stop == 2:
            return

        with ExitStack() as lin:
            def sbl(name, shape, dt=F32):
                return lin.enter_context(nc.sbuf_tensor(name, shape, dt))

            xn = sbl("xn_lin", [P, NT, D])
            w1 = sbl("w_lin", [P, 4, KT, D])
            bias = sbl("bias_lin", [P, 3, KT])
            bo = sbl("bo", [P, D])
            low = sbl("low", [P, 2, 2, T])
            relu = sbl("relu", [P, 2, 2, T])
            kv = sbl("kv", [P, 2, T])
            cum = sbl("cum", [P, 2, T])
            ctxT = sbl("ctxT", [P, KT, N])
            s_re = sem("lin_relu")
            s_lw, s_pr, s_lo, s_ph, s_cx, s_oo, s_xl, s_kvr = (
                sem("lin_weights"), sem("lin_projected"), sem("lin_low"), sem("lin_phi"), sem("lin_context"),
                sem("lin_out"), sem("lin_added"), sem("lin_chain"))

            with nc.Block() as block:
                @block.sync
                def _(sp):
                    for i, name in enumerate(("wk1", "wv1", "wq1", "wo1")):
                        sp.dma_start(w1[:, i], a[name].rearrange("(k p) n -> p k n", p=P)).then_inc(s_lw, 16)
                    for i, name in enumerate(("bk1", "bv1", "bq1")):
                        sp.dma_start(bias[:, i, :], a[name].rearrange("(k p) -> p k", p=P),
                                     allow_slow_non_contiguous=True).then_inc(s_lw, 16)
                    sp.dma_start(bo[:], a["bo1"].partition_broadcast(P)).then_inc(s_lw, 16)
                    if stop == 3:
                        sp.wait_ge(s_xl, NT)
                        sp.dma_start(out.rearrange("(t p) d -> p t d", p=P), X[:]).then_inc(s_out, 16)
                        sp.wait_ge(s_out, 16)

                @block.tensor
                def _(pe):
                    pe_transposes(pe, 3, xn, xn_ready(pe, 2))
                    pe.wait_ge(s_xnT, 16)
                    pe.wait_ge(s_lw, 16 * 8)
                    for w in range(4):
                        mt, half = w // 2, w % 2
                        if w >= 2:
                            pe.wait_ge(s_cx, w - 1)
                        for c in range(3):
                            for k in range(KT):
                                ins = nc.tensor.matmul(scores[:, w % 2, c * T:(c + 1) * T], w1[:, c, k, mt * P:(mt + 1) * P],
                                                       xnT[:, k, half * T:(half + 1) * T],
                                                       start=(k == 0), stop=(k == KT - 1))
                        ins.then_inc(s_pr, 1)
                    pe.wait_ge(s_cx, 4)
                    for t in range(NT):
                        if t >= 2:
                            pe.wait_ge(s_xl, t - 1)
                        for k in range(KT):
                            ins = nc.tensor.matmul(misc[:, t % 2, 0:D], ctxT[:, k, t * P:(t + 1) * P], w1[:, 3, k, :],
                                                   start=(k == 0), stop=(k == KT - 1))
                        ins.then_inc(s_oo, 1)

                @block.scalar
                def _(act):
                    act_std(act, 2)
                    act_transposes(act, 3)
                    for w in range(4):
                        mt, r = w // 2, w % 2
                        act.wait_ge(s_pr, w + 1)
                        for x, c in ((0, 0), (1, 2)):
                            ins = nc.scalar.activation(relu[:, r, x, :], scores[:, r, c * T:(c + 1) * T], ACT.Relu,
                                                       bias=bias[:, c, mt:mt + 1])
                        ins.then_inc(s_re, 1)
                        act.wait_ge(s_lo, w + 1)
                        nc.scalar.activation(low[:, r], low[:, r], ACT.Exp).then_inc(s_ph, 1)

                @block.vector
                def _(dve):
                    link = chain(dve, s_kvr)
                    dve_norm(dve, link, 2, xn)
                    dve.wait_ge(s_lw, 16 * 8)
                    for w in range(4):
                        mt, half, r = w // 2, w % 2, w % 2
                        dve.wait_ge(s_re, w + 1)
                        for x, c in ((0, 0), (1, 2)):
                            ins = nc.vector.tensor_scalar(low[:, r, x, :], scores[:, r, c * T:(c + 1) * T],
                                                          bias[:, c, mt:mt + 1], 0.0, ALU.add, ALU.min)
                        ins.then_inc(s_lo, 1)
                        dve.wait_ge(s_ph, w + 1)
                        link(nc.vector.tensor_tensor(relu[:, r], relu[:, r], low[:, r], ALU.add))
                        link(nc.vector.scalar_tensor_tensor(out=kv[:, r, :], in0=scores[:, r, T:2 * T],
                                                            scalar=bias[:, 1, mt:mt + 1], in1=relu[:, r, 0, :],
                                                            op0=ALU.add, op1=ALU.mult))
                        link(nc.vector.tensor_tensor_scan(cum[:, r, :], onesf.to_broadcast([P, T]), kv[:, r, :],
                                                          0.0, ALU.mult, ALU.add))
                        nc.vector.scalar_tensor_tensor(out=ctxT[:, mt, half * T:(half + 1) * T], in0=cum[:, r, :],
                                                       scalar=SCALE, in1=relu[:, r, 1, :], op0=ALU.mult,
                                                       op1=ALU.mult).then_inc(s_cx, 1)
                    link(nc.vector.tensor_tensor(X[:], X[:], bo[:].unsqueeze(1).to_broadcast([P, NT, D]), ALU.add))
                    for t in range(NT):
                        dve.wait_ge(s_oo, t + 1)
                        nc.vector.tensor_tensor(X[:, t, :], misc[:, t % 2, 0:D], X[:, t, :], ALU.add).then_inc(s_xl, 1)
                    dve.wait_ge(s_xl, NT)
        if stop == 3:
            return

        with ExitStack() as ffn:
            def sbf(name, shape, dt=F32):
                return ffn.enter_context(nc.sbuf_tensor(name, shape, dt))

            FT = F1 // P
            xn = sbf("xn_ffn", [P, NT, D])
            gate1 = sbf("gate1", [P, KT, E1])
            pr = sbf("probs1", [P, NT, E1])
            mx = sbf("mx1", [P, NT])
            m8 = sbf("m81", [P, NT, E1])
            i8 = sbf("i81", [P, NT, E1], U32)
            f8 = sbf("f81", [P, NT, E1])
            wt = sbf("wt1", [P, NT, 2])
            den2 = sbf("den2", [P, NT])
            one = sbf("one1", [P, 2, NT, E1])
            comb = sbf("comb1", [P, NT, E1])
            w13 = sbf("w13", [P, 2, KT, 2 * F1])
            w2 = sbf("w2", [P, 2, FT, D])
            sg = sbf("sg1", [P, 2, T])
            hT = sbf("hT1", [P, 2, FT, N])
            s_gw, s_lg, s_sub, s_ex = sem("gate1_loaded"), sem("logits1"), sem("shifted1"), sem("exp1")
            s_lnk = sem("chain1")
            s_ld = [sem("ffn_loaded0"), sem("ffn_loaded1")]
            s_gu, s_sl, s_h, s_y, s_acc, s_cmb = (sem("gate_up1"), sem("silu1"), sem("hidden1"), sem("down1"),
                                                  sem("added1"), sem("combine1"))
            IT = 2 * FT

            with nc.Block() as block:
                @block.sync
                def _(sp):
                    sp.dma_start(gate1[:], a["gate1"].rearrange("(k p) n -> p k n", p=P)).then_inc(s_gw, 16)

                    def load(j, e):
                        sp.dma_start(w13[:, j], a["w13"][e].rearrange("p (k n) -> p k n", k=KT)).then_inc(s_ld[j], 16)
                        sp.dma_start(w2[:, j], a["w2"][e].rearrange("p (k n) -> p k n", k=FT)).then_inc(s_ld[j], 16)
                    load(0, 0)
                    load(1, 1)
                    with sp.Fori(0, E1 // 2 - 1) as i:
                        for j in range(2):
                            sp.wait_ge(s_y, (2 * i + j + 1) * NT)
                            load(j, 2 * i + j + 2)
                    sp.wait_ge(s_acc, NT * E1)
                    sp.dma_start(out.rearrange("(t p) d -> p t d", p=P), X[:]).then_inc(s_out, 16)
                    sp.wait_ge(s_out, 16)

                @block.tensor
                def _(pe):
                    pe_transposes(pe, 4, xn, xn_ready(pe, 3))
                    pe.wait_ge(s_xnT, 20)
                    pe.wait_ge(s_gw, 16)
                    for t in range(NT):
                        for k in range(KT):
                            ins = nc.tensor.matmul(misc[:, 0, t * E1:(t + 1) * E1], xnT[:, k, t * P:(t + 1) * P],
                                                   gate1[:, k, :], start=(k == 0), stop=(k == KT - 1))
                    ins.then_inc(s_lg, 1)
                    pe.wait_ge(s_cmb, 1)

                    def gate_up(j, i, first):
                        pe.wait_ge(s_ld[j], (i + 1) * 32)
                        for q in range(IT):
                            ft, half = q // 2, q % 2
                            if not (first and q < 2):
                                pe.wait_ge(s_h, (2 * i + j) * IT + q - 1)
                            for g in range(2):
                                for k in range(KT):
                                    c = g * F1 + ft * P
                                    ins = nc.tensor.matmul(scores[:, q % 2, g * T:(g + 1) * T], w13[:, j, k, c:c + P],
                                                           xnT[:, k, half * T:(half + 1) * T],
                                                           start=(k == 0), stop=(k == KT - 1))
                            ins.then_inc(s_gu, 1)

                    def down(j, e, first):
                        pe.wait_ge(s_h, (e + 1) * IT)
                        for t in range(NT):
                            if not (first and t < 2):
                                pe.wait_ge(s_acc, e * NT + t - 1)
                            for f in range(FT):
                                ins = nc.tensor.matmul(misc[:, t % 2, 0:D], hT[:, j, f, t * P:(t + 1) * P],
                                                       w2[:, j, f, :], start=(f == 0), stop=(f == FT - 1))
                            ins.then_inc(s_y, 1)

                    gate_up(0, 0, True)
                    gate_up(1, 0, False)
                    down(0, 0, True)
                    with pe.Fori(1, E1 // 2) as i:
                        gate_up(0, i, False)
                        down(1, 2 * i - 1, False)
                        gate_up(1, i, False)
                        down(0, 2 * i, False)
                    down(1, E1 - 1, False)

                @block.scalar
                def _(act):
                    act_std(act, 3)
                    act_transposes(act, 4)
                    act.wait_ge(s_sub, 1)
                    nc.scalar.activation(pr[:], pr[:], ACT.Exp).then_inc(s_ex, 1)
                    with act.Fori(0, E1) as e:
                        for q in range(IT):
                            act.wait_ge(s_gu, e * IT + q + 1)
                            nc.scalar.activation(sg[:, q % 2, :], scores[:, q % 2, 0:T], ACT.Silu).then_inc(s_sl, 1)

                @block.vector
                def _(dve):
                    link = chain(dve, s_lnk)
                    dve_norm(dve, link, 3, xn)
                    dve.wait_ge(s_lg, 1)
                    lg = misc[:, 0, 0:NT * E1].rearrange("p (t e) -> p t e", e=E1)
                    bc = [P, NT, E1]
                    link(nc.vector.tensor_reduce(mx[:], lg, AX.X, ALU.max))
                    nc.vector.tensor_tensor(pr[:], lg, mx[:].unsqueeze(2).to_broadcast(bc), ALU.subtract).then_inc(s_sub, 1)
                    dve.wait_ge(s_ex, 1)
                    link(nc.vector.tensor_reduce(mx[:], pr[:], AX.X, ALU.add))
                    link(nc.vector.reciprocal(mx[:], mx[:]))
                    link(nc.vector.tensor_tensor(pr[:], pr[:], mx[:].unsqueeze(2).to_broadcast(bc), ALU.mult))
                    for t in range(NT):
                        ins = nc.vector.max(m8[:, t, :], pr[:, t, :])
                    link(ins)
                    for t in range(NT):
                        ins = nc.vector.max_index(i8[:, t, :], m8[:, t, :], pr[:, t, :])
                    link(ins)
                    nc.vector.tensor_copy(f8[:], i8[:])
                    link(nc.vector.tensor_tensor(den2[:], m8[:, :, 0], m8[:, :, 1], ALU.add))
                    link(nc.vector.reciprocal(den2[:], den2[:]))
                    link(nc.vector.tensor_tensor(wt[:], m8[:, :, 0:2], den2[:].unsqueeze(2).to_broadcast([P, NT, 2]), ALU.mult))
                    for t in range(NT):
                        for k in range(2):
                            ins = nc.vector.tensor_scalar(one[:, k, t, :], iota8, f8[:, t, k:k + 1], wt[:, t, k:k + 1],
                                                          ALU.is_equal, ALU.mult)
                    link(ins)
                    nc.vector.tensor_tensor(comb[:], one[:, 0], one[:, 1], ALU.add).then_inc(s_cmb, 1)
                    dve.wait_ge(s_cmb, 1)

                    def hidden(j, e):
                        for q in range(IT):
                            ft, half = q // 2, q % 2
                            dve.wait_ge(s_sl, e * IT + q + 1)
                            nc.vector.tensor_tensor(hT[:, j, ft, half * T:(half + 1) * T], sg[:, q % 2, :],
                                                    scores[:, q % 2, T:2 * T], ALU.mult).then_inc(s_h, 1)

                    def add(e, first):
                        for t in range(NT):
                            dve.wait_ge(s_y, e * NT + t + 1)
                            if not first:
                                dve.wait_ge(s_acc, (e - 1) * NT + t + 1)
                            nc.vector.scalar_tensor_tensor(out=X[:, t, :], in0=misc[:, t % 2, 0:D],
                                                           scalar=comb[:, t, bass.ds(e, 1)], in1=X[:, t, :],
                                                           op0=ALU.mult, op1=ALU.add).then_inc(s_acc, 1)

                    hidden(0, 0)
                    hidden(1, 1)
                    add(0, True)
                    with dve.Fori(1, E1 // 2) as i:
                        hidden(0, 2 * i)
                        add(2 * i - 1, False)
                        hidden(1, 2 * i + 1)
                        add(2 * i, False)
                    add(E1 - 1, False)


_INS = ['L0_attn_hidden_states']
STOP = 0


def shape_constants():
    r = np.arange(P)
    half = HD // 2
    inv = (np.float32(1.0) / np.power(np.float32(10000.0), np.arange(half, dtype=np.float32) / np.float32(half))).astype(np.float32)
    ang = (np.arange(T, dtype=np.float32)[:, None] * inv[None, :]).astype(np.float32)
    cos, sin = np.cos(ang).astype(np.float32), np.sin(ang).astype(np.float32)
    d = r % HD
    C = cos[:, d % half].T
    S = np.where(d[:, None] < half, -1.0, 1.0) * sin[:, d % half].T
    sec = np.stack([(r // n) % 2 for n in LEVELS], 1)
    pairs = [(r[:, None] // (2 * n) == np.arange(64)[None, :] // n) & (r[:, None] // n % 2 == 1)
             for n in LEVELS[:2]]
    cf = np.concatenate([np.eye(P), C, S, np.tile(np.eye(SB).ravel(), (P, 1)), sec,
                         np.tile(np.arange(E1), (P, 1)), np.ones((P, 1))] + pairs + [np.tile(np.arange(E0) * CAP, (P, 1))], 1).astype(np.float32)
    neg = -1e30
    causal = np.where(r[None, :] > r[:, None], neg, 0)
    strict = np.where(r[None, :] >= r[:, None], neg, 0)
    first = strict.copy()
    first[0, 0] = 0
    cb = np.concatenate([np.eye(P), causal, strict, first, r[:, None] <= r[None, :], np.ones((P, P))], 1)
    return cf, cb.astype(np.float32)


def kernel(**inputs):
    import concourse.bacc as _bacc
    from concourse.bass_utils import run_bass_kernel_spmd as _run

    g = {k: np.asarray(v) for k, v in inputs.items()}
    swap = np.arange(D).reshape(H, 2, HD // 2)[:, ::-1].reshape(-1)
    wq, wk = g["L0_attn_Wq"], g["L0_attn_Wk"]
    cf, cb = shape_constants()
    data = {
        "x": g["L0_attn_hidden_states"].reshape(N, D), "cf": cf, "cb": cb,
        "wk0": wk, "wk0r": wk[:, swap], "wq0": wq, "wq0r": wq[:, swap],
        "wvb0": np.concatenate([g["L0_attn_Wv"], g["L0_attn_Wb"]], 1), "wo0": g["L0_attn_Wo"],
        "bb": g["L0_attn_bb"], "gate0": g["L0_ffn_gate_w"].T,
        "wgu0": np.concatenate([g["L0_ffn_w_gate"], g["L0_ffn_w_up"]], 1).reshape(E0, 2 * F0, KT, P)
        .transpose(0, 3, 2, 1).reshape(E0, P, KT * 2 * F0),
        "wd0": g["L0_ffn_w_down"].transpose(0, 2, 1),
        "wk1": g["L1_attn_Wk"].T, "wv1": g["L1_attn_Wv"].T, "wq1": g["L1_attn_Wq"].T, "wo1": g["L1_attn_Wo"].T,
        "bk1": g["L1_attn_bk"], "bv1": g["L1_attn_bv"], "bq1": g["L1_attn_bq"], "bo1": g["L1_attn_bo"],
        "gate1": g["L1_ffn_gate_w"].T,
        "w13": np.concatenate([g["L1_ffn_w1"], g["L1_ffn_w3"]], 1).reshape(E1, 2 * F1, KT, P)
        .transpose(0, 3, 2, 1).reshape(E1, P, KT * 2 * F1),
        "w2": g["L1_ffn_w2"].reshape(E1, D, F1 // P, P).transpose(0, 3, 2, 1).reshape(E1, P, F1 // P * D),
    }
    nc = _bacc.Bacc("TRN2", target_bir_lowering=False, num_devices=1)
    arrays, aps = {}, {}
    for name, x in data.items():
        x = np.ascontiguousarray(x)
        arrays["in_" + name] = x
        aps[name] = nc.dram_tensor("in_" + name, x.shape, mybir.dt.from_np(x.dtype), kind="ExternalInput").ap()
    out = nc.dram_tensor("out_0", (N, D), F32, kind="ExternalOutput").ap()
    build_kernel(nc, aps, out, STOP)
    r = _run(nc, [arrays], core_ids=[0])
    return r.results[0]["out_0"].reshape(2, T, D)
```

```python
from contextlib import ExitStack

import numpy as np

import concourse.bass as bass
from concourse import mybir

ALU = mybir.AluOpType
ACT = mybir.ActivationFunctionType
F32 = mybir.dt.float32
BF16 = mybir.dt.bfloat16
U32 = mybir.dt.uint32
AX = mybir.AxisListType

P = 128
N, D = 1024, 256
NT = N // P
KT = D // P
T = 512
H, HD = 16, 16
GH = 8
NI = T // P
UNITS = (H // GH) * (N // T)
SLOTS = 6
KR = SLOTS * HD
PART_A = (0, 0, 1, 1, 0, 2)
PART_B = (0, 1, 0, 1, 2, 0)
SB = 16
LEVELS = (16, 32, 64)
SCALE = HD ** -0.5
EPS = 1e-5
E0, F0, K0 = 64, 96, 8
CAP = 2 * N * K0 // E0
E1, F1 = 8, 512
BIG = 32768.0

OFF = {0: 0, 1: 512, 3: 896, 2: 1024}
WIDE = 10 * P
ROWAT = {3: 0, 2: 512, 0: 896, 1: 1024}


def build_kernel(nc, a, out, stop):
    with ExitStack() as ctx:
        def sb(name, shape, dt=F32):
            return ctx.enter_context(nc.sbuf_tensor(name, shape, dt))

        def sem(name):
            return ctx.enter_context(nc.semaphore(name))

        scores = ctx.enter_context(nc.psum_tensor("scores", [P, 2, 3 * 512], F32))
        misc = ctx.enter_context(nc.psum_tensor("misc", [P, 2, 512], F32))

        X = sb("X", [P, NT, D])
        xnT = sb("xnT", [P, KT, N])
        stats = sb("stats", [P, NT, 6])
        mv = sb("mv", [P, NT, 2])
        std = sb("std", [P, NT])
        rstd = sb("rstd", [P, NT])
        eps = sb("eps", [P, 1])
        cf = sb("cf", [P, a["cf"].shape[1]])
        cb = sb("cb", [P, a["cb"].shape[1]], BF16)
        identf = cf[:, 0:128]
        cosT = cf[:, 128:640]
        sinT = cf[:, 640:1152]
        eye16 = cf[:, 1152:1408]
        second = cf[:, 1408:1411]
        iota8 = cf[:, 1411:1419]
        onesf = cf[:, 1419:1420]
        pairs = cf[:, 1420:1452]
        identb = cb[:, 0:128]
        mask = {("q", 0): cb[:, 128:256], ("k", 0): cb[:, 384:512]}
        for i in range(1, NI):
            mask["q", i] = cb[:, 128:256]
            mask["k", i] = cb[:, 256:384]
        triu = cb[:, 512:640]
        onesb = cb[:, 640:768]

        s_x, s_w, s_eps = sem("x_loaded"), sem("weights_loaded"), sem("eps_set")
        s_var, s_std, s_xn = sem("variance"), sem("std"), sem("xn_tile")
        s_tr, s_xnT = sem("transposed"), sem("xnT_quarter")
        s_dv, s_po = sem("vector_chain"), sem("pool_chain")
        s_dv2, s_pk = sem("vector_chain_moe"), sem("weight_picked")
        s_out, s_zf = sem("stored"), sem("slots_zeroed")
        zero = sb("zero", [P, 1024])
        base0 = cf[:, 1548:1612]
        ones2 = cf[:, 1612:1676]
        NZ = E0 * CAP * D // (P * 1024)
        xbuf = nc.dram_tensor("expert_rows", [E0 * CAP, D], F32, kind="Internal").ap()
        ybuf = nc.dram_tensor("expert_outputs", [E0 * CAP, D], F32, kind="Internal").ap()
        xb_v = xbuf.rearrange("(e n) d -> e n d", e=E0)
        yb_v = ybuf.rearrange("(e n) d -> e n d", e=E0)
        xb_z = xbuf.rearrange("(z p n) d -> z p (n d)", z=NZ, p=P)

        def chain(eng, s):
            count = [0]

            def link(ins):
                count[0] += 1
                ins.then_inc(s, 1)
                eng.wait_ge(s, count[0])
            return link

        def dve_norm(dve, link, l, xn):
            for t in range(NT):
                ins = nc.vector.bn_stats(stats[:, t, :], X[:, t, :])
            link(ins)
            for t in range(NT):
                ins = nc.vector.bn_aggr(mv[:, t, :], stats[:, t, :])
            ins.then_inc(s_var, 1)
            dve.wait_ge(s_std, l + 1)
            link(nc.vector.reciprocal(rstd[:], std[:]))
            for t in range(NT):
                nc.vector.tensor_scalar(xn[:, t, :], X[:, t, :], mv[:, t, 0:1], rstd[:, t:t + 1],
                                        ALU.subtract, ALU.mult).then_inc(s_xn, 1)

        def act_std(act, l):
            act.wait_ge(s_var, l + 1)
            nc.scalar.activation(std[:], mv[:, :, 1], ACT.Sqrt, bias=eps[:, 0:1]).then_inc(s_std, 1)

        def pe_transposes(pe, n, src, ready):
            for p in range(4):
                ready(p)
                if 4 * n + p - 1 > 0:
                    pe.wait_ge(s_xnT, 4 * n + p - 1)
                for k in range(KT):
                    for t in range(2):
                        c = (2 * k + t) * P
                        ins = nc.tensor.transpose(misc[:, p % 2, c:c + P],
                                                  src[:, 2 * p + t, k * P:(k + 1) * P], identf)
                ins.then_inc(s_tr, 1)

        def act_transposes(act, n):
            for p in range(4):
                act.wait_ge(s_tr, 4 * n + p + 1)
                nc.scalar.copy(xnT[:, :, 2 * P * p:2 * P * (p + 1)],
                               misc[:, p % 2, :].rearrange("p (k n) -> p k n", k=KT)).then_inc(s_xnT, 1)

        def xn_ready(pe, l):
            return lambda p: pe.wait_ge(s_xn, NT * l + 2 * p + 2)

        with ExitStack() as att:
            def sba(name, shape, dt=F32):
                return att.enter_context(nc.sbuf_tensor(name, shape, dt))

            early = sba("early", [P, 4608])
            wqk = early[:, 0:2048].rearrange("p (a k d) -> p a k d", a=4, k=KT)
            ropes = early[:, 2048:3072].rearrange("p (a n) -> p a n", a=2)
            parts = early[:, 3072:4608].bitcast(BF16).rearrange("p (a b n) -> p a b n", a=2, b=3)
            T1 = early[:, 0:1536].rearrange("p (a h n) -> p a h n", a=3, h=GH)
            wvb = sba("wvb", [P, KT, D + H])
            wo0 = sba("wo0", [P, KT, D])
            bb = sba("bb", [P, H])
            VB = sba("VB", [P, NT, D + H])
            AO = sba("AO", [P, NT, D])
            stk = {c: sba(f"stack_{c}", [P, 2, GH, T], BF16) for c in ("k", "B", "q")}
            nm = sba("nm", [P, 2, GH * NI])
            nmr = sba("nmr", [P, GH * NI])
            nms = sba("nms", [P, 2, 3, GH * NI], BF16)
            mrow = sba("mrow", [3 * GH * NI, 2, P], BF16)
            E = sba("E", [P, GH, WIDE])
            bankT = sba("bankT", [P, 512])
            den = sba("den", [P, GH * NI])
            ng = sba("ng", [P, GH * NI])
            ngm = sba("ngm", [P, 3, GH * NI])
            G = sba("G", [P, 2, SB])
            LB = sba("LB", [P, 2, SB, SB])
            Y = sba("Y", [P, 2, SB, SB])
            YT = sba("YT", [P, 2, SB, SB])
            tmp = YT
            XT = sba("XT", [P, GH * NI, P])
            XR = sba("XR", [P, GH * NI, 64])
            R = sba("R", [P, GH, 32])
            EQ23 = sba("EQ23", [P, 2, WIDE])
            U = sba("U", [P, NI, GH, 32])
            rec = sba("rec", [P, NI, 4])

            scr = nc.dram_tensor("split_heads", [2, 3, D, N], BF16, kind="Internal").ap()
            edd = nc.dram_tensor("diagonals", [2, GH * NI, P, P], F32, kind="Internal").ap()
            xsd = nc.dram_tensor("inverses", [2, 2, P, 2, SB, SB], F32, kind="Internal").ap()

            s_pj, s_rf, s_parts = sem("projected"), sem("projection_read"), sem("parts_split")
            s_pw = [sem("parts_stored0"), sem("parts_stored1")]
            s_stk = [sem("stack_loaded0"), sem("stack_loaded1")]
            s_ones, s_cb = sem("ones_set"), sem("masks_ready")
            s_v, s_vc, s_vb = sem("v_projected"), sem("v_copied"), sem("beta_ready")
            s_sa, s_sc, s_fd, s_fa = sem("rows_ready"), sem("scores_ready"), sem("maxima_taken"), sem("exps_done")
            s_nms, s_mt, s_mr, s_ml = sem("maxima_split"), sem("maxima_turned"), sem("maxima_rows"), sem("maxima_in_stack")
            s_dk, s_dq = sem("kk_masked"), sem("qk_masked")
            s_dc, s_dt, s_oc, s_ot = sem("denominators_copied"), sem("denominators_turned"), sem("o_copied"), sem("o_turned")
            s_den, s_ng, s_gt, s_g = sem("denominators"), sem("g_ready"), sem("g_turned"), sem("g_in_blocks")
            s_ed, s_lb, s_y, s_ys, s_z, s_z2, s_xt, s_xr = (sem("diag_stored"), sem("blocks_loaded"), sem("blocks_inverted"),
                                                sem("inverses_stored"), sem("XT_zeroed"), sem("XR_zeroed"),
                                                sem("XT_loaded"), sem("XR_loaded"))
            s_tt, s_t1, s_pq, s_lv = sem("level_T"), sem("level_T1"), sem("level_PQ"), sem("level_joined")
            s_sn, s_st1, s_un, s_ut = sem("sums_copied"), sem("sums_turned"), sem("u_copied"), sem("u_turned")
            s_s, s_r, s_us, s_uv = sem("solve_sums"), sem("solve_r"), sem("solve_u"), sem("u_stored")
            s_o, s_ao, s_wo, s_xw = sem("attended"), sem("ao_ready"), sem("wo_done"), sem("x_attended")

            def EQ(h):
                if h % 4 < 2:
                    return early[:, 1536 + (h % 4) * WIDE:1536 + (h % 4 + 1) * WIDE]
                return EQ23[:, h % 4 - 2]

            def use(c, u):
                if c == 0:
                    return 16 * u - 8 if u else 0
                return 16 * u + 16 if u + 1 < UNITS else 16 * u + 8

            def blk(tile, h, jt, it):
                c = OFF[jt] + (it - jt) * P
                return tile[:, h, c:c + P]

            def halves(ap, n, which):
                return ap.rearrange("p h (b t n) -> p h b t n", t=2, n=n)[:, :, :, which, :]

            def maxima_due(q):
                return range(max(0, q - 2) * 16 // 10, max(0, q - 1) * 16 // 10)

            with nc.Block() as block:
                @block.tensor
                def _(pe):
                    pe.wait_ge(s_w, 16 * 9)
                    pe_transposes(pe, 0, AO, xn_ready(pe, 0))
                    pe.wait_ge(s_xnT, 4)
                    for w in range(8):
                        mt, half, c = w // 4, w // 2 % 2, w % 2
                        if w >= 2:
                            pe.wait_ge(s_rf, w - 1)
                        for rot in range(2):
                            for k in range(KT):
                                ins = nc.tensor.matmul(scores[:, w % 2, rot * 512:rot * 512 + T],
                                                       wqk[:, 2 * c + rot, k, mt * P:(mt + 1) * P],
                                                       xnT[:, k, half * T:(half + 1) * T],
                                                       start=(k == 0), stop=(k == KT - 1))
                        ins.then_inc(s_pj, 1)
                    for t in range(NT):
                        if t >= 2:
                            pe.wait_ge(s_vc, t - 1)
                        for k in range(KT):
                            ins = nc.tensor.matmul(misc[:, t % 2, 0:D + H], xnT[:, k, t * P:(t + 1) * P],
                                                   wvb[:, k, :], start=(k == 0), stop=(k == KT - 1))
                        ins.then_inc(s_v, 1)
                    pe.wait_ge(s_rf, 8)
                    pe.wait_ge(s_vc, NT)
                    pe.wait_ge(s_ones, 1)
                    pe.wait_ge(s_cb, 1)

                    def turn_maxima(u, c):
                        pe.wait_ge(s_nms, 2 * u + c + 1)
                        if u:
                            pe.wait_ge(s_g, u)
                        nc.tensor.transpose(misc[0:96, c, 0:64].bitcast(BF16),
                                            nms[:, c, :, :].rearrange("p a b -> p (a b)"), identb
                                            ).then_inc(s_mt, 1)

                    def row_scores(u, m, slot):
                        c, h = "kq"[m // 8], m % 8
                        for it in range(NI):
                            w = (it + 1) * P
                            o = ROWAT[it]
                            nc.tensor.matmul(scores[:, slot, o:o + w],
                                             stk[c][0:KR, u % 2, h, it * P:w], stk["B"][0:KR, u % 2, h, 0:w],
                                             start=True, stop=False)
                            ins = nc.tensor.matmul(scores[:, slot, o + w - P:o + w], identb,
                                                   mask[c, it], start=False, stop=True)
                        ins.then_inc(s_sa, 1)

                    def transposed_scores(u, c, h):
                        k = use(c, u) + h
                        if k >= 2:
                            pe.wait_ge(s_fa, k - 1)
                        for jt in range(NI):
                            o = OFF[jt]
                            ins = nc.tensor.matmul(scores[:, k % 2, o:o + T - jt * P],
                                                   stk["B"][0:KR + 3, u % 2, h, jt * P:(jt + 1) * P],
                                                   stk["kq"[c]][0:KR + 3, u % 2, h, jt * P:T],
                                                   start=True, stop=True)
                        ins.then_inc(s_sc, 1)

                    def key_softmax(u):
                        pe.wait_ge(s_ml, 96 * u + 96)
                        pe.wait_ge(s_fd, 16 * (u + 1))
                        if u:
                            pe.wait_ge(s_lv, 12 * u)
                        for h in range(GH):
                            transposed_scores(u, 0, h)
                        pe.wait_ge(s_mr, 2 * u + 2)
                        if u:
                            pe.wait_ge(s_uv, 4 * u)
                        pe.wait_ge(s_dk, GH * (u + 1))
                        for hh in range(2):
                            for jt in range(NI):
                                for g in range(4):
                                    o = OFF[jt]
                                    ins = nc.tensor.matmul(misc[32 * g:32 * g + 32, 0, jt * P:T], ones2[:, 32 * hh:32 * hh + 32],
                                                           E[:, 4 * hh + g, o:o + T - jt * P],
                                                           start=(hh == 0 and jt == 0), stop=(hh == 1 and jt == NI - 1),
                                                           skip_group_check=True)
                        ins.then_inc(s_den, 1)
                        pe.wait_ge(s_dc, u + 1)
                        for it in range(NI):
                            ins = nc.tensor.transpose(misc[:, 1, it * P:(it + 1) * P], bankT[:, it * P:(it + 1) * P], identf)
                        ins.then_inc(s_dt, 1)
                        pe.wait_ge(s_ng, u + 1)
                        nc.tensor.transpose(misc[0:GH * NI, 1, 0:P], ng[:], identf).then_inc(s_gt, 1)

                    def sums(u, q):
                        li, it = q // NI, q % NI
                        g = 12 * u + q
                        if q:
                            pe.wait_ge(s_t1, g)
                        if q >= 4:
                            pe.wait_ge(s_lv, g - 3)
                        for h in range(GH):
                            e, x = blk(E, h, it, it), h * NI + it
                            if li == 2:
                                ins = nc.tensor.matmul(scores[64:128, 1, 64 * h:64 * h + 64], e[0:64, 64:128],
                                                       XR[0:64, x, :], start=True, stop=True)
                                continue
                            for r in (slice(0, 64), slice(64, 128)):
                                ins = nc.tensor.matmul(scores[r, 1, 32 * h:32 * h + 32], e[r, r],
                                                       halves(XR[r, x:x + 1, :], LEVELS[li], 0)[:, 0],
                                                       start=True, stop=True, skip_group_check=True)
                        ins.then_inc(s_tt, 1)

                    def join(u, q):
                        li, it = q // NI, q % NI
                        n = LEVELS[li]
                        g = 12 * u + q
                        pe.wait_ge(s_t1, g + 1)
                        if q:
                            pe.wait_ge(s_lv, g)
                        for h in range(GH):
                            x = h * NI + it
                            if li == 2:
                                ins = nc.tensor.matmul(scores[0:64, 1, 1024 + 64 * h:1088 + 64 * h], T1[64:128, 2, h, :],
                                                       XT[64:128, x, 64:128], start=True, stop=True)
                                continue
                            for r in (slice(0, 64), slice(64, 128)):
                                nc.tensor.matmul(scores[r, 1, 512 + 32 * h:544 + 32 * h], XT[r, x, r],
                                                 halves(T1[r, li, h:h + 1, :], n, 0)[:, 0],
                                                 start=True, stop=True, skip_group_check=True)
                                ins = nc.tensor.matmul(scores[r, 1, 1024 + 32 * h:1056 + 32 * h], T1[r, li, h, :],
                                                       halves(XT[r, x:x + 1, r], n, 1)[:, 0],
                                                       start=True, stop=True, skip_group_check=True)
                        ins.then_inc(s_pq, 1)

                    def solve(u):
                        for it in range(NI):
                            if it:
                                pe.wait_ge(s_uv, 4 * u + it)
                                for hh in range(2):
                                    for jt in range(it):
                                        for g in range(4):
                                            h = 4 * hh + g
                                            ins = nc.tensor.matmul(misc[32 * g:32 * g + 32, 0, hh * P:(hh + 1) * P],
                                                                   U[:, jt, h, :], blk(E, h, jt, it),
                                                                   start=(jt == 0), stop=(jt == it - 1),
                                                                   skip_group_check=True)
                                ins.then_inc(s_s, 1)
                                pe.wait_ge(s_sn, 3 * u + it)
                                for hh in range(2):
                                    ins = nc.tensor.transpose(misc[:, 0, hh * P:(hh + 1) * P],
                                                              bankT[:, hh * P:(hh + 1) * P], identf)
                                ins.then_inc(s_st1, 1)
                            pe.wait_ge(s_r, 4 * u + it + 1)
                            for hh in range(2):
                                for g in range(4):
                                    h = 4 * hh + g
                                    ins = nc.tensor.matmul(misc[32 * g:32 * g + 32, 1, hh * P:(hh + 1) * P],
                                                           R[:, h, :], XT[:, h * NI + it, :], start=True, stop=True,
                                                           skip_group_check=True)
                            ins.then_inc(s_us, 1)
                            pe.wait_ge(s_un, 4 * u + it + 1)
                            for hh in range(2):
                                ins = nc.tensor.transpose(misc[:, 1, hh * P:(hh + 1) * P],
                                                          bankT[:, 256 + hh * P:256 + (hh + 1) * P], identf)
                            ins.then_inc(s_ut, 1)

                    def attend(u, hh):
                        pe.wait_ge(s_dq, GH * u + 4 * (hh + 1))
                        for jt in range(NI):
                            for g in range(4):
                                h, o = 4 * hh + g, OFF[jt]
                                ins = nc.tensor.matmul(misc[32 * g:32 * g + 32, hh, jt * P:T], U[:, jt, h, :],
                                                       EQ(h)[:, o:o + T - jt * P], start=(jt == 0),
                                                       stop=(jt == NI - 1), skip_group_check=True)
                        ins.then_inc(s_o, 1)

                    def turn_outputs(u, hh):
                        pe.wait_ge(s_oc, 2 * u + hh + 1)
                        for it in range(NI):
                            ins = nc.tensor.transpose(misc[:, hh, it * P:(it + 1) * P], bankT[:, it * P:(it + 1) * P], identf)
                        ins.then_inc(s_ot, 1)

                    pe.wait_ge(s_stk[0], 16 * 18)
                    for m in range(16):
                        if m >= 2:
                            pe.wait_ge(s_fd, m - 1)
                        row_scores(0, m, m % 2)
                    turn_maxima(0, 0)
                    turn_maxima(0, 1)
                    key_softmax(0)
                    for u in range(UNITS):
                        last = u + 1 == UNITS
                        pe.wait_ge(s_xt, 16 * 8 * (u + 1))
                        pe.wait_ge(s_xr, 16 * 8 * (u + 1))
                        pe.wait_ge(s_fa, 16 * u + 8)
                        for q in range(12):
                            sums(u, q)
                            if q:
                                join(u, q - 1)
                            if not last:
                                if q == 2:
                                    pe.wait_ge(s_stk[(u + 1) % 2], 16 * 18 * ((u + 1) // 2 + 1))
                                for m in maxima_due(q):
                                    pe.wait_ge(s_fd, 16 * (u + 1) + m)
                                    row_scores(u + 1, m, 0)
                        join(u, 11)
                        if not last:
                            turn_maxima(u + 1, 0)
                            turn_maxima(u + 1, 1)
                            pe.wait_ge(s_mr, 2 * u + 4)
                        pe.wait_ge(s_lv, 12 * (u + 1))
                        pe.wait_ge(s_g, u + 1)
                        solve(u)
                        if not last:
                            key_softmax(u + 1)
                            pe.wait_ge(s_g, u + 2)
                        else:
                            pe.wait_ge(s_uv, 4 * (u + 1))
                        for h in range(GH):
                            transposed_scores(u, 1, h)
                            if h == 4:
                                attend(u, 0)
                            if h == 6:
                                turn_outputs(u, 0)
                        attend(u, 1)
                        turn_outputs(u, 1)
                        pe.wait_ge(s_ao, 2 * (u + 1))
                    pe_transposes(pe, 1, AO, lambda p: pe.wait_ge(s_ao, 2 * UNITS))
                    pe.wait_ge(s_xnT, 8)
                    for t in range(NT):
                        if t >= 2:
                            pe.wait_ge(s_xw, t - 1)
                        for k in range(KT):
                            ins = nc.tensor.matmul(misc[:, t % 2, 0:D], xnT[:, k, t * P:(t + 1) * P],
                                                   wo0[:, k, :], start=(k == 0), stop=(k == KT - 1))
                        ins.then_inc(s_wo, 1)

                @block.vector
                def _(dve):
                    link = chain(dve, s_dv)
                    nc.vector.memset(eps[:], EPS).then_inc(s_eps, 1)
                    link(nc.vector.memset(U[:], 0.0))
                    link(nc.vector.memset(U[:, :, :, HD:HD + 1], 1.0))
                    link(nc.vector.memset(R[:], 0.0))
                    dve.wait_ge(s_x, 16)
                    dve_norm(dve, link, 0, AO)
                    dve.wait_ge(s_w, 16 * 9)
                    link(nc.vector.tensor_copy(cb[:], E[:, 0, 0:a["cb"].shape[1]]))
                    nc.vector.sem_inc(s_cb, 1)
                    for w in range(8):
                        dve.wait_ge(s_pj, w + 1)
                        if w >= 2:
                            dve.wait_ge(s_pw[w % 2], 16 * (w // 2))
                        a0, a1 = ropes[:, 0, :], ropes[:, 1, :]
                        nc.vector.tensor_tensor(a0, scores[:, w % 2, 0:T], cosT, ALU.mult)
                        ins = nc.vector.tensor_tensor(a1, scores[:, w % 2, 512:512 + T], sinT, ALU.mult)
                        link(ins)
                        nc.vector.sem_inc(s_rf, 1)
                        link(nc.vector.tensor_tensor(a0, a0, a1, ALU.add))
                        link(nc.vector.tensor_copy(parts[:, w % 2, 0, :], a0))
                        link(nc.vector.tensor_tensor(a0, a0, parts[:, w % 2, 0, :], ALU.subtract))
                        link(nc.vector.tensor_copy(parts[:, w % 2, 1, :], a0))
                        link(nc.vector.tensor_tensor(parts[:, w % 2, 2, :], a0, parts[:, w % 2, 1, :],
                                                     ALU.subtract))
                        nc.vector.sem_inc(s_parts, 1)
                    link(nc.vector.memset(T1[:], 0.0))
                    dve.wait_ge(s_vc, NT)
                    bcol = VB[:, :, D:D + H]
                    link(nc.vector.tensor_tensor(bcol, bcol, bb[:].unsqueeze(1).to_broadcast([P, NT, H]), ALU.add))

                    def maxima(u, m, slot):
                        c, h = m // 8, m % 8
                        dve.wait_ge(s_sa, 16 * u + m + 1)
                        for it in range(NI):
                            o = ROWAT[it]
                            ins = nc.vector.tensor_reduce(nm[:, c, NI * h + it:NI * h + it + 1],
                                                          scores[:, slot, o:o + (it + 1) * P],
                                                          AX.X, ALU.max, negate=True)
                        ins.then_inc(s_fd, 1)
                        if h < GH - 1:
                            return
                        dve.wait_ge(s_fd, 16 * u + 8 * (c + 1))
                        if u:
                            dve.wait_ge(s_mt, 2 * (u - 1) + c + 1)
                        link(nc.vector.tensor_copy(nms[:, c, 0, :], nm[:, c, :]))
                        link(nc.vector.tensor_tensor(nmr[:], nm[:, c, :], nms[:, c, 0, :], ALU.subtract))
                        link(nc.vector.tensor_copy(nms[:, c, 1, :], nmr[:]))
                        link(nc.vector.tensor_tensor(nms[:, c, 2, :], nmr[:], nms[:, c, 1, :], ALU.subtract))
                        nc.vector.sem_inc(s_nms, 1)

                    def scale_and_invert(u):
                        hg, b = u // 2, u % 2
                        dve.wait_ge(s_dt, u + 1)
                        link(nc.vector.tensor_scalar(
                            den[:].rearrange("p (a g i) -> p a g i", a=2, g=4),
                            misc[:, 1, :].rearrange("p (i g a) -> p a g i", i=NI, g=4)[:, 0:2], 1e-30, None, ALU.max))
                        link(nc.vector.reciprocal(den[:], den[:]))
                        beta = VB[:, b * NI:(b + 1) * NI, D + hg * GH:D + (hg + 1) * GH].rearrange("p i h -> p h i")
                        link(nc.vector.scalar_tensor_tensor(
                            out=ng[:].rearrange("p (h i) -> p h i", i=NI),
                            in0=den[:].rearrange("p (h i) -> p h i", i=NI), scalar=-1.0, in1=beta,
                            op0=ALU.mult, op1=ALU.mult))
                        nc.vector.sem_inc(s_ng, 1)
                        for li in range(3):
                            ins = nc.vector.tensor_scalar(ngm[:, li, :], ng[:], second[:, li:li + 1], None, ALU.mult)
                        link(ins)
                        dve.wait_ge(s_gt, u + 1)
                        for s4 in range(4):
                            ins = nc.vector.tensor_copy(G[32 * s4:32 * s4 + 32, :, :].rearrange("p a b -> p (a b)"),
                                                        misc[0:32, 1, 32 * s4:32 * s4 + 32])
                        link(ins)
                        nc.vector.sem_inc(s_g, 1)
                        dve.wait_ge(s_lb, 16 * 8 * (u + 1))
                        for s2 in range(2):
                            nc.vector.tensor_copy(Y[:, s2].rearrange("p a b -> p (a b)"), eye16)
                            ins = nc.vector.tensor_tensor(
                                LB[:, s2], LB[:, s2], G[:, s2].unsqueeze(1).to_broadcast([P, SB, SB]), ALU.mult)
                        link(ins)
                        for i in range(1, SB):
                            row = LB[:, :, 0:i, i].unsqueeze(2).to_broadcast([P, 2, i, i])
                            link(nc.vector.tensor_tensor(tmp[:, :, 0:i, 0:i], Y[:, :, 0:i, 0:i], row, ALU.mult))
                            link(nc.vector.tensor_reduce(Y[:, :, 0:i, i], tmp[:, :, 0:i, 0:i], AX.X, ALU.add))
                        link(nc.vector.tensor_copy(YT[:], Y[:].rearrange("p s c i -> p s i c")))
                        nc.vector.sem_inc(s_y, 1)

                    def joined(u, q):
                        li, it = q // NI, q % NI
                        n = LEVELS[li]
                        dve.wait_ge(s_pq, 12 * u + q + 1)
                        xt = XT[:].rearrange("p (h i) c -> p h i c", i=NI)[:, :, it, :]
                        xr = XR[:].rearrange("p (h i) c -> p h i c", i=NI)[:, :, it, :]
                        if li == 2:
                            ins = nc.vector.tensor_copy(xt[0:64, :, 64:128],
                                                        scores[0:64, 1, 1024:1536].rearrange("p (h n) -> p h n", h=GH))
                        for r in (0, 64):
                            lo, hi = slice(r, r + 32), slice(r + 32, r + 64)
                            if li == 1:
                                nc.vector.tensor_copy(xr[hi, :, 0:32],
                                                      scores[hi, 1, 512:768].rearrange("p (h n) -> p h n", h=GH))
                                ins = nc.vector.tensor_copy(xt[lo, :, r + 32:r + 64],
                                                            scores[lo, 1, 1024:1280].rearrange("p (h n) -> p h n", h=GH))
                            if li == 0:
                                rs = slice(r, r + 64)
                                for dst, o in ((halves(xr[rs], n, 0), 512), (halves(xt[rs, :, rs], n, 1), 1024)):
                                    ins = nc.vector.tensor_tensor(
                                        dst, scores[rs, 1, o:o + 256].rearrange("p (h b n) -> p h b n", h=GH, n=n),
                                        dst, ALU.add)
                        ins.then_inc(s_lv, 1)

                    def scaled_sums(u, q):
                        li, it = q // NI, q % NI
                        n = LEVELS[li]
                        dve.wait_ge(s_tt, 12 * u + q + 1)
                        g_ = ngm[:, li, :].rearrange("p (h i) -> p h i", i=NI)[:, :, it]
                        if li == 0:
                            dst = halves(T1[:, li], n, 0)
                            src = scores[:, 1, 0:256].rearrange("p (h b n) -> p h b n", h=GH, n=n)
                            link(nc.vector.tensor_tensor(
                                dst, src, g_.unsqueeze(2).unsqueeze(3).to_broadcast([P, GH, 2, n]), ALU.mult))
                            m_ = pairs.rearrange("p (b n) -> p b n", n=n)
                            ins = nc.vector.tensor_tensor(
                                dst, dst, m_.unsqueeze(1).to_broadcast([P, GH, 2, n]), ALU.mult)
                        elif li == 1:
                            ins = nc.vector.tensor_tensor(
                                T1[:, li, :, 0:n], scores[:, 1, 0:256].rearrange("p (h n) -> p h n", h=GH),
                                g_.unsqueeze(2).to_broadcast([P, GH, n]), ALU.mult)
                        else:
                            ins = nc.vector.tensor_tensor(
                                T1[64:128, li], scores[64:128, 1, 0:512].rearrange("p (h n) -> p h n", h=GH),
                                g_[64:128].unsqueeze(2).to_broadcast([64, GH, n]), ALU.mult)
                        ins.then_inc(s_t1, 1)

                    def solved(u):
                        hg, b = u // 2, u % 2
                        for it in range(NI):
                            v = VB[:, b * NI + it, hg * P:(hg + 1) * P].rearrange("p (h d) -> p h d", d=HD)
                            g_ = ng[:].rearrange("p (h i) -> p h i", i=NI)[:, :, it].unsqueeze(2).to_broadcast([P, GH, HD])
                            r = R[:, :, 0:HD]
                            if it:
                                dve.wait_ge(s_st1, 3 * u + it)
                                link(nc.vector.tensor_tensor(
                                    r, misc[:, 0, 0:2 * P].rearrange("p (h d) -> p h d", d=32)[:, :, 0:HD], g_, ALU.mult))
                                nc.vector.tensor_tensor(r, r, v, ALU.add).then_inc(s_r, 1)
                            else:
                                nc.vector.tensor_copy(r, v).then_inc(s_r, 1)
                            dve.wait_ge(s_ut, 4 * u + it + 1)
                            nc.vector.tensor_copy(U[:, it, :, 0:HD],
                                                  misc[:, 1, 0:2 * P].rearrange("p (h d) -> p h d", d=32)[:, :, 0:HD]
                                                  ).then_inc(s_uv, 1)

                    def outputs(u):
                        hg, b = u // 2, u % 2
                        for hh in range(2):
                            dve.wait_ge(s_ot, 2 * u + hh + 1)
                            o4 = misc[:, hh, :].rearrange("p (i g d) -> p i g d", i=NI, g=4)
                            if u or hh:
                                dve.wait_ge(s_ao, 2 * u + hh)
                            link(nc.vector.reciprocal(rec[:], o4[:, :, :, HD]))
                            c = (hg * GH + hh * 4) * HD
                            nc.vector.tensor_tensor(
                                AO[:, b * NI:(b + 1) * NI, c:c + 4 * HD].rearrange("p i (g d) -> p i g d", g=4),
                                o4[:, :, :, 0:HD], rec[:].unsqueeze(3).to_broadcast([P, NI, 4, HD]),
                                ALU.mult).then_inc(s_ao, 1)

                    for m in range(16):
                        maxima(0, m, m % 2)
                    scale_and_invert(0)
                    for u in range(UNITS):
                        last = u + 1 == UNITS
                        dve.wait_ge(s_xt, 16 * 8 * (u + 1))
                        dve.wait_ge(s_xr, 16 * 8 * (u + 1))
                        for q in range(12):
                            if q:
                                joined(u, q - 1)
                            scaled_sums(u, q)
                            if not last:
                                for m in maxima_due(q):
                                    maxima(u + 1, m, 0)
                        joined(u, 11)
                        solved(u)
                        if not last:
                            scale_and_invert(u + 1)
                        outputs(u)
                    for t in range(NT):
                        dve.wait_ge(s_wo, t + 1)
                        nc.vector.tensor_tensor(X[:, t, :], misc[:, t % 2, 0:D], X[:, t, :], ALU.add).then_inc(s_xw, 1)
                    dve.wait_ge(s_xw, NT)

                @block.scalar
                def _(act):
                    act.wait_ge(s_eps, 1)
                    act_std(act, 0)
                    act_transposes(act, 0)
                    for t in range(NT):
                        act.wait_ge(s_v, t + 1)
                        nc.scalar.copy(VB[:, t, :], misc[:, t % 2, 0:D + H]).then_inc(s_vc, 1)

                    def rows(u, c):
                        act.wait_ge(s_mt, 2 * u + c + 1)
                        if u:
                            act.wait_ge(s_ml, 96 * (u - 1) + 48 * (c + 1))
                        nc.scalar.copy(mrow[:, c, :], misc[0:96, c, 0:64].bitcast(BF16)).then_inc(s_mr, 1)

                    def exps(u, c, h):
                        k = use(c, u) + h
                        act.wait_ge(s_sc, k + 1)
                        if c and h == 4:
                            act.wait_ge(s_o, 2 * u + 1)
                        nc.scalar.activation(EQ(h) if c else E[:, h, :], scores[:, k % 2, 0:WIDE], ACT.Exp,
                                             scale=SCALE).then_inc(s_fa, 1)

                    def key_softmax(u):
                        if u:
                            act.wait_ge(s_us, NI * u)
                        for h in range(GH):
                            exps(u, 0, h)
                        act.wait_ge(s_den, u + 1)
                        nc.scalar.copy(bankT[:], misc[:, 0, :]).then_inc(s_dc, 1)

                    def copy_outputs(u, hh):
                        act.wait_ge(s_o, 2 * u + hh + 1)
                        if hh:
                            act.wait_ge(s_ot, 2 * u + 1)
                        else:
                            act.wait_ge(s_dt, min(u + 2, UNITS))
                        nc.scalar.copy(bankT[:], misc[:, hh, :]).then_inc(s_oc, 1)

                    rows(0, 0)
                    rows(0, 1)
                    key_softmax(0)
                    for u in range(UNITS):
                        for z in range(NZ // UNITS):
                            if u == 0 and z == 0:
                                act.wait_ge(s_ones, 2)
                            act.dma_start(xb_z[u * (NZ // UNITS) + z], zero[:]).then_inc(s_zf, 16)
                        if u + 1 < UNITS:
                            rows(u + 1, 0)
                            rows(u + 1, 1)
                        for it in range(NI):
                            if it:
                                act.wait_ge(s_s, 3 * u + it)
                                nc.scalar.copy(bankT[:, 0:256], misc[:, 0, 0:256]).then_inc(s_sn, 1)
                            act.wait_ge(s_us, 4 * u + it + 1)
                            nc.scalar.copy(bankT[:, 256:512], misc[:, 1, 0:256]).then_inc(s_un, 1)
                        if u + 1 < UNITS:
                            key_softmax(u + 1)
                        act.wait_ge(s_pw[0], 64)
                        act.wait_ge(s_pw[1], 64)
                        for h in range(GH):
                            exps(u, 1, h)
                            if h == 5:
                                copy_outputs(u, 0)
                        copy_outputs(u, 1)
                    act_transposes(act, 1)

                @block.gpsimd
                def _(pool):
                    link = chain(pool, s_po)
                    for c in range(2):
                        link(nc.gpsimd.memset(stk["B"][96:99, c], 1.0))
                    nc.gpsimd.sem_inc(s_ones, 1)
                    link(nc.gpsimd.memset(zero[:], 0.0))
                    nc.gpsimd.sem_inc(s_ones, 1)
                    link(nc.gpsimd.memset(XT[:], 0.0))
                    nc.gpsimd.sem_inc(s_z, 1)
                    link(nc.gpsimd.memset(XR[:], 0.0))
                    nc.gpsimd.sem_inc(s_z2, 1)

                    def select(u, c):
                        for h in range(GH):
                            pool.wait_ge(s_fa, use(c, u) + h + 1)
                            e = EQ(h) if c else E[:, h, :]
                            for d in (e[:, 0:1024].rearrange("p (a n) -> p a n", a=2)[:, :, 0:P],
                                      e[:, 896:1152].rearrange("p (a n) -> p a n", a=2)):
                                ins = nc.gpsimd.affine_select(
                                    out=d, in_=d, pattern=[[0, 2], [1, P]], base=0, channel_multiplier=-1,
                                    compare_op=ALU.is_ge if c else ALU.is_gt, fill=0.0)
                            ins.then_inc(s_dq if c else s_dk, 1)

                    select(0, 0)
                    for u in range(UNITS):
                        if u + 1 < UNITS:
                            select(u + 1, 0)
                            pool.wait_ge(s_dk, GH * (u + 2))
                            pool.wait_ge(s_us, 4 * (u + 1))
                            link(nc.gpsimd.memset(XT[:], 0.0))
                            nc.gpsimd.sem_inc(s_z, 1)
                            link(nc.gpsimd.memset(XR[:], 0.0))
                            nc.gpsimd.sem_inc(s_z2, 1)
                        select(u, 1)

                @block.sync
                def _(sp):
                    sp.dma_start(X[:], a["x"].rearrange("(t p) d -> p t d", p=P)).then_inc(s_x, 16)
                    sp.dma_start(cf[:], a["cf"]).then_inc(s_w, 16)
                    sp.dma_start(E[:, 0, 0:a["cb"].shape[1]], a["cb"]).then_inc(s_w, 16)
                    for i, name in enumerate(("wk0", "wk0r", "wq0", "wq0r")):
                        sp.dma_start(wqk[:, i], a[name].rearrange("(k p) n -> p k n", p=P)).then_inc(s_w, 16)
                    sp.dma_start(wvb[:], a["wvb0"].rearrange("(k p) n -> p k n", p=P)).then_inc(s_w, 16)
                    sp.dma_start(wo0[:], a["wo0"].rearrange("(k p) n -> p k n", p=P)).then_inc(s_w, 16)
                    sp.dma_start(bb[:], a["bb"].partition_broadcast(P)).then_inc(s_w, 16)

                    def store_parts(w):
                        mt, half, c = w // 4, w // 2 % 2, w % 2
                        sp.wait_ge(s_parts, w + 1)
                        sp.dma_start(scr[c, :, mt * P:(mt + 1) * P, half * T:(half + 1) * T].rearrange("t p n -> p t n"),
                                     parts[:, w % 2]).then_inc(s_pw[w % 2], 16)

                    def load_stacks(u):
                        hg, b = u // 2, u % 2
                        sp.wait_ge(s_pw[0], 16 * (u + 1))
                        sp.wait_ge(s_pw[1], 16 * (u + 1))
                        if u >= 2:
                            sp.wait_ge(s_o, 2 * (u - 1))
                        for c, x, order in (("k", 0, PART_A), ("B", 0, PART_B), ("q", 1, PART_A)):
                            for s, part in enumerate(order):
                                sp.dma_start(stk[c][HD * s:HD * (s + 1), u % 2],
                                             scr[x, part, hg * P:(hg + 1) * P, b * T:(b + 1) * T]
                                             .rearrange("(h d) n -> d h n", d=HD)).then_inc(s_stk[u % 2], 16)

                    for w in range(8):
                        store_parts(w)
                        if w % 2 and w < 4:
                            load_stacks(w // 2)
                    for u in range(UNITS):
                        for c in range(2):
                            sp.wait_ge(s_mr, 2 * u + c + 1)
                            for part in range(3):
                                sp.dma_start(stk["kq"[c]][KR + part:KR + part + 1, u % 2].rearrange("p h n -> p (h n)"),
                                             mrow[32 * part:32 * part + 32, c, :]).then_inc(s_ml, 16)
                        sp.wait_ge(s_dk, GH * (u + 1))
                        for it in range(NI):
                            sp.dma_start(edd[u % 2].rearrange("(h i) j q -> i j h q", i=NI)[it],
                                         E[:, :, OFF[it]:OFF[it] + P]).then_inc(s_ed, 16)
                        sp.wait_ge(s_ed, 16 * 4 * (u + 1))
                        if u:
                            sp.wait_ge(s_y, u)
                        for s in range(8):
                            sp.dma_start(LB[32 * (s // 2):32 * (s // 2) + 32, s % 2],
                                         edd[u % 2, :, SB * s:SB * (s + 1), SB * s:SB * (s + 1)]).then_inc(s_lb, 16)
                        sp.wait_ge(s_y, u + 1)
                        sp.dma_start(xsd[u % 2, 0], Y[:]).then_inc(s_ys, 16)
                        sp.dma_start(xsd[u % 2, 1], YT[:]).then_inc(s_ys, 16)
                        sp.wait_ge(s_ys, 32 * (u + 1))
                        for x, (dst, zeroed, loaded) in enumerate(((XT, s_z, s_xt), (XR, s_z2, s_xr))):
                            sp.wait_ge(zeroed, u + 1)
                            for s in range(8):
                                c = SB * (s % 4 if x else s)
                                sp.dma_start(dst[SB * s:SB * (s + 1), :, c:c + SB],
                                             xsd[u % 2, x, 32 * (s // 2):32 * (s // 2) + 32, s % 2]
                                             .rearrange("e c i -> c e i")).then_inc(loaded, 16)
                        if 1 <= u < UNITS - 1:
                            load_stacks(u + 1)
                    if stop == 1:
                        sp.wait_ge(s_xw, NT)
                        sp.dma_start(out.rearrange("(t p) d -> p t d", p=P), X[:]).then_inc(s_out, 16)
                        sp.wait_ge(s_out, 16)
        if stop == 1:
            return

        with ExitStack() as moe:
            def sbm(name, shape, dt=F32):
                return moe.enter_context(nc.sbuf_tensor(name, shape, dt))

            xn = sbm("xn_moe", [P, NT, D])
            gate0 = sbm("gate0", [P, KT, E0])
            pr = sbm("probs", [P, NT, E0])
            sel = sbm("sel", [P, NT, E0])
            selb = sbm("selb", [P, NT, E0], BF16)
            val = sbm("val", [P, NT, E0])
            slot = sbm("slot", [P, NT, E0])
            Vg = sbm("Vg", [P, NT, E0])
            Vs = sbm("Vs", [P, NT, E0])
            pick = sbm("pick", [P, 2, E0])
            mx = sbm("mx", [P, NT])
            m8 = sbm("m8", [P, NT, K0])
            V8g = sbm("V8g", [P, NT, K0])
            V8s = sbm("V8s", [P, NT, K0])
            ig = sbm("gather_slots", [P, NT, K0], U32)
            isc = sbm("scatter_slots", [P, NT, K0], U32)
            w8 = sbm("w8", [P, NT, K0])
            NB = 4
            xg = sbm("xg", [P, NB, 2, D])
            wgu = sbm("wgu", [P, NB, KT, 2 * F0])
            wd = sbm("wd", [F0, NB, D])
            xgT = sbm("xgT", [P, 2, KT, CAP])
            sg = sbm("sg", [F0, 2, CAP])
            hT = sbm("hT", [F0, 2, CAP])
            yb = sbm("yb", [P, NB, 2, D])
            NG = 16
            gb = sbm("gb", [P, NG, D])

            s_gw, s_lg, s_sub, s_ex = sem("gate_loaded"), sem("logits"), sem("logits_shifted"), sem("logits_exp")
            s_sel, s_rk, s_idx, s_sc0, s_w8 = (sem("selected"), sem("ranks"), sem("slots_ready"), sem("rows_scattered"),
                                              sem("weights_ready"))
            s_ld = [sem(f"expert_loaded{j}") for j in range(NB)]
            s_t, s_xt0, s_gu, s_sl = sem("rows_turned"), sem("rows_copied"), sem("gate_up"), sem("silu_done")
            s_h, s_y0, s_yv = sem("hidden_ready"), sem("down_done"), sem("down_copied")
            s_st = [sem(f"y_stored{j}") for j in range(NB)]
            s_gb = [sem(f"gathered{j}") for j in range(NG)]
            s_acc = sem("row_added")

            def steps(fori, total, body):
                body(0, True, False)
                body(1, False, False)
                with fori(2, total - 1) as i:
                    body(i, False, False)
                body(total - 1, False, True)

            with nc.Block() as block:
                @block.tensor
                def _(pe):
                    pe_transposes(pe, 2, xn, xn_ready(pe, 1))
                    pe.wait_ge(s_xnT, 12)
                    pe.wait_ge(s_gw, 16)
                    for t in range(NT):
                        for k in range(KT):
                            ins = nc.tensor.matmul(scores[:, 0, t * E0:(t + 1) * E0], xnT[:, k, t * P:(t + 1) * P],
                                                   gate0[:, k, :], start=(k == 0), stop=(k == KT - 1))
                    ins.then_inc(s_lg, 1)
                    pe.wait_ge(s_sel, 1)
                    for t in range(NT):
                        for q in range(t + 1):
                            ins = nc.tensor.matmul(scores[:, 1, t * E0:(t + 1) * E0], triu if q == t else onesb,
                                                   selb[:, q, :], start=(q == 0), stop=(q == t))
                    ins.then_inc(s_rk, 1)
                    pe.wait_ge(s_w8, 1)

                    def turn(j, i):
                        pe.wait_ge(s_ld[j], (i + 1) * 48)
                        for k in range(KT):
                            for t in range(2):
                                c = (2 * k + t) * P
                                ins = nc.tensor.transpose(misc[:, j % 2, c:c + P], xg[:, j, t, k * P:(k + 1) * P], identf)
                        ins.then_inc(s_t, 1)

                    def down(j, e, wait):
                        pe.wait_ge(s_h, e + 1)
                        if wait:
                            pe.wait_ge(s_yv, e - 1)
                        for t in range(2):
                            ins = nc.tensor.matmul(scores[:, j % 2, 512 + t * D:512 + (t + 1) * D],
                                                   hT[:, j % 2, t * P:(t + 1) * P], wd[:, j, :], start=True, stop=True)
                        ins.then_inc(s_y0, 1)

                    def body(i, first, last):
                        for j in range(NB):
                            e = NB * i + j
                            if not (last and j == NB - 1):
                                turn((j + 1) % NB, i + (j + 1) // NB)
                            pe.wait_ge(s_xt0, e + 1)
                            for g in range(2):
                                for k in range(KT):
                                    ins = nc.tensor.matmul(scores[0:F0, j % 2, g * CAP:(g + 1) * CAP],
                                                           wgu[:, j, k, g * F0:(g + 1) * F0], xgT[:, j % 2, k, :],
                                                           start=(k == 0), stop=(k == KT - 1))
                            ins.then_inc(s_gu, 1)
                            if not (first and j == 0):
                                down((j - 1) % NB, e - 1, not (first and j < 3))

                    turn(0, 0)
                    steps(pe.Fori, E0 // NB, body)
                    down(NB - 1, E0 - 1, True)

                @block.vector
                def _(dve):
                    link = chain(dve, s_dv2)
                    dve_norm(dve, link, 1, xn)
                    dve.wait_ge(s_lg, 1)
                    lg = scores[:, 0, 0:512].rearrange("p (t e) -> p t e", e=E0)
                    bc = [P, NT, E0]
                    link(nc.vector.tensor_reduce(mx[:], lg, AX.X, ALU.max))
                    nc.vector.tensor_tensor(pr[:], lg, mx[:].unsqueeze(2).to_broadcast(bc), ALU.subtract).then_inc(s_sub, 1)
                    dve.wait_ge(s_ex, 1)
                    link(nc.vector.tensor_reduce(mx[:], pr[:], AX.X, ALU.add))
                    link(nc.vector.reciprocal(mx[:], mx[:]))
                    link(nc.vector.tensor_tensor(pr[:], pr[:], mx[:].unsqueeze(2).to_broadcast(bc), ALU.mult))
                    for t in range(NT):
                        ins = nc.vector.max(m8[:, t, :], pr[:, t, :])
                    link(ins)
                    for t in range(NT):
                        ins = nc.vector.match_replace(sel[:, t, :], m8[:, t, :], pr[:, t, :], -1.0)
                    link(ins)
                    nc.vector.tensor_scalar(selb[:], sel[:], 0.0, None, ALU.is_lt).then_inc(s_sel, 1)
                    dve.wait_ge(s_sel, 1)
                    dve.wait_ge(s_rk, 1)
                    rk = scores[:, 1, 0:512].rearrange("p (t e) -> p t e", e=E0)
                    link(nc.vector.tensor_scalar(slot[:], rk, float(CAP), -1.0, ALU.min, ALU.add))
                    link(nc.vector.tensor_scalar(val[:], rk, float(CAP), None, ALU.is_le))
                    link(nc.vector.tensor_tensor(slot[:], slot[:], base0.unsqueeze(1).to_broadcast(bc), ALU.add))
                    link(nc.vector.tensor_scalar(slot[:], slot[:], -1.0, BIG, ALU.mult, ALU.add))
                    link(nc.vector.tensor_tensor(Vg[:], slot[:], selb[:], ALU.mult))
                    link(nc.vector.tensor_tensor(Vs[:], Vg[:], val[:], ALU.mult))
                    for t in range(NT):
                        nc.vector.max(V8s[:, t, :], Vs[:, t, :])
                        ins = nc.vector.max(V8g[:, t, :], Vg[:, t, :])
                    link(ins)
                    nc.vector.tensor_scalar(isc[:], V8s[:], -1.0, BIG, ALU.mult, ALU.add).then_inc(s_idx, 1)
                    nc.vector.tensor_scalar(ig[:], V8g[:], -1.0, BIG, ALU.mult, ALU.add).then_inc(s_idx, 1)
                    link(nc.vector.tensor_tensor(pr[:], pr[:], val[:], ALU.mult))
                    for g in range(NT * K0):
                        t, k = g // K0, g % K0
                        if g >= 2:
                            dve.wait_ge(s_pk, g - 1)
                        nc.vector.scalar_tensor_tensor(
                            out=pick[:, g % 2, :], in0=Vg[:, t, :], scalar=V8g[:, t, k:k + 1], in1=pr[:, t, :],
                            op0=ALU.is_equal, op1=ALU.mult, accum_out=w8[:, t, k:k + 1]).then_inc(s_pk, 1)
                    dve.wait_ge(s_pk, NT * K0)
                    nc.vector.sem_inc(s_w8, 1)

                    def copy_down(j, e, n):
                        dve.wait_ge(s_y0, e + 1)
                        if n is not None:
                            dve.wait_ge(s_st[j], n * 16)
                        nc.vector.tensor_copy(yb[:, j].rearrange("p t d -> p (t d)"),
                                              scores[:, j % 2, 512:1024]).then_inc(s_yv, 1)

                    def body(i, first, last):
                        for j in range(NB):
                            e = NB * i + j
                            dve.wait_ge(s_sl, e + 1)
                            nc.vector.tensor_tensor(hT[:, j % 2, :], sg[:, j % 2, :], scores[0:F0, j % 2, CAP:2 * CAP],
                                                    ALU.mult).then_inc(s_h, 1)
                            if j:
                                copy_down(j - 1, e - 1, None if first else i)
                            elif not first:
                                copy_down(NB - 1, e - 1, None if isinstance(i, int) and i == 1 else i - 1)

                    steps(dve.Fori, E0 // NB, body)
                    copy_down(NB - 1, E0 - 1, E0 // NB - 1)
                    for g in range(NT * K0):
                        k, t = g // NT, g % NT
                        dve.wait_ge(s_gb[g % NG], 16 * (g // NG + 1))
                        if g >= NT:
                            dve.wait_ge(s_acc, g - NT + 1)
                        nc.vector.scalar_tensor_tensor(out=X[:, t, :], in0=gb[:, g % NG, :], scalar=w8[:, t, k:k + 1],
                                                       in1=X[:, t, :], op0=ALU.mult, op1=ALU.add).then_inc(s_acc, 1)
                    dve.wait_ge(s_acc, NT * K0)

                @block.scalar
                def _(act):
                    act_std(act, 1)
                    act_transposes(act, 2)
                    act.wait_ge(s_sub, 1)
                    nc.scalar.activation(pr[:], pr[:], ACT.Exp).then_inc(s_ex, 1)

                    def copy_rows(j, e):
                        act.wait_ge(s_t, e + 1)
                        nc.scalar.copy(xgT[:, j % 2].rearrange("p k n -> p (k n)"), misc[:, j % 2, :]).then_inc(s_xt0, 1)

                    def body(i, first, last):
                        for j in range(NB):
                            e = NB * i + j
                            if not (last and j == NB - 1):
                                copy_rows(j + 1, e + 1)
                            act.wait_ge(s_gu, e + 1)
                            nc.scalar.activation(sg[:, j % 2, :], scores[0:F0, j % 2, 0:CAP], ACT.Silu).then_inc(s_sl, 1)

                    copy_rows(0, 0)
                    steps(act.Fori, E0 // NB, body)

                @block.gpsimd
                def _(pool):
                    pool.wait_ge(s_idx, 2)
                    pool.wait_ge(s_zf, 16 * NZ)
                    for t in range(NT):
                        for k in range(K0):
                            pool.indirect_dma_start(
                                out=xbuf, out_offset=bass.IndirectOffsetOnAxis(ap=isc[:, t, k:k + 1], axis=0),
                                in_=xn[:, t, :], in_offset=None, bounds_check=E0 * CAP - 1,
                                oob_is_err=False).then_inc(s_sc0, 16)
                    for j in range(NB):
                        pool.wait_ge(s_st[j], 16 * (E0 // NB))
                    for g in range(NT * K0):
                        k, t = g // NT, g % NT
                        if g >= NG:
                            pool.wait_ge(s_acc, g - NG + 1)
                        pool.indirect_dma_start(
                            out=gb[:, g % NG, :], out_offset=None, in_=ybuf,
                            in_offset=bass.IndirectOffsetOnAxis(ap=ig[:, t, k:k + 1], axis=0),
                            bounds_check=E0 * CAP - 1, oob_is_err=True).then_inc(s_gb[g % NG], 16)

                @block.sync
                def _(sp):
                    sp.dma_start(gate0[:], a["gate0"].rearrange("(k p) n -> p k n", p=P)).then_inc(s_gw, 16)

                    def load_weights(j, e):
                        sp.dma_start(wgu[:, j], a["wgu0"][e].rearrange("p (k n) -> p k n", k=KT)).then_inc(s_ld[j], 16)
                        sp.dma_start(wd[:, j], a["wd0"][e]).then_inc(s_ld[j], 16)

                    def load_rows(j, e):
                        sp.dma_start(xg[:, j], xb_v[e].rearrange("(t p) d -> p t d", p=P)).then_inc(s_ld[j], 16)

                    for e in range(3):
                        load_weights(e, e)
                    sp.wait_ge(s_sc0, 16 * NT * K0)
                    for e in range(3):
                        load_rows(e, e)

                    def body(i, first, last):
                        for j in range(NB):
                            e = NB * i + j
                            if not (first and j == 0):
                                sp.wait_ge(s_y0, e)
                            if not (last and j > 0):
                                load_weights((j + 3) % NB, e + 3)
                                load_rows((j + 3) % NB, e + 3)
                            if not (first and j == 0):
                                jj = (j - 1) % NB
                                sp.wait_ge(s_yv, e)
                                sp.dma_start(yb_v[e - 1].rearrange("(t p) d -> p t d", p=P), yb[:, jj]).then_inc(s_st[jj], 16)

                    steps(sp.Fori, E0 // NB, body)
                    sp.wait_ge(s_yv, E0)
                    sp.dma_start(yb_v[E0 - 1].rearrange("(t p) d -> p t d", p=P), yb[:, NB - 1]).then_inc(s_st[NB - 1], 16)
                    if stop == 2:
                        sp.wait_ge(s_acc, NT * K0)
                        sp.dma_start(out.rearrange("(t p) d -> p t d", p=P), X[:]).then_inc(s_out, 16)
                        sp.wait_ge(s_out, 16)
        if stop == 2:
            return

        with ExitStack() as lin:
            def sbl(name, shape, dt=F32):
                return lin.enter_context(nc.sbuf_tensor(name, shape, dt))

            xn = sbl("xn_lin", [P, NT, D])
            w1 = sbl("w_lin", [P, 4, KT, D])
            bias = sbl("bias_lin", [P, 3, KT])
            bo = sbl("bo", [P, D])
            low = sbl("low", [P, 2, 2, T])
            relu = sbl("relu", [P, 2, 2, T])
            kv = sbl("kv", [P, 2, T])
            cum = sbl("cum", [P, 2, T])
            ctxT = sbl("ctxT", [P, KT, N])
            s_re = sem("lin_relu")
            s_lw, s_pr, s_lo, s_ph, s_cx, s_oo, s_xl, s_kvr = (
                sem("lin_weights"), sem("lin_projected"), sem("lin_low"), sem("lin_phi"), sem("lin_context"),
                sem("lin_out"), sem("lin_added"), sem("lin_chain"))

            with nc.Block() as block:
                @block.sync
                def _(sp):
                    for i, name in enumerate(("wk1", "wv1", "wq1", "wo1")):
                        sp.dma_start(w1[:, i], a[name].rearrange("(k p) n -> p k n", p=P)).then_inc(s_lw, 16)
                    for i, name in enumerate(("bk1", "bv1", "bq1")):
                        sp.dma_start(bias[:, i, :], a[name].rearrange("(k p) -> p k", p=P),
                                     allow_slow_non_contiguous=True).then_inc(s_lw, 16)
                    sp.dma_start(bo[:], a["bo1"].partition_broadcast(P)).then_inc(s_lw, 16)
                    if stop == 3:
                        sp.wait_ge(s_xl, NT)
                        sp.dma_start(out.rearrange("(t p) d -> p t d", p=P), X[:]).then_inc(s_out, 16)
                        sp.wait_ge(s_out, 16)

                @block.tensor
                def _(pe):
                    pe_transposes(pe, 3, xn, xn_ready(pe, 2))
                    pe.wait_ge(s_xnT, 16)
                    pe.wait_ge(s_lw, 16 * 8)
                    for w in range(4):
                        mt, half = w // 2, w % 2
                        if w >= 2:
                            pe.wait_ge(s_cx, w - 1)
                        for c in range(3):
                            for k in range(KT):
                                ins = nc.tensor.matmul(scores[:, w % 2, c * T:(c + 1) * T], w1[:, c, k, mt * P:(mt + 1) * P],
                                                       xnT[:, k, half * T:(half + 1) * T],
                                                       start=(k == 0), stop=(k == KT - 1))
                        ins.then_inc(s_pr, 1)
                    pe.wait_ge(s_cx, 4)
                    for t in range(NT):
                        if t >= 2:
                            pe.wait_ge(s_xl, t - 1)
                        for k in range(KT):
                            ins = nc.tensor.matmul(misc[:, t % 2, 0:D], ctxT[:, k, t * P:(t + 1) * P], w1[:, 3, k, :],
                                                   start=(k == 0), stop=(k == KT - 1))
                        ins.then_inc(s_oo, 1)

                @block.scalar
                def _(act):
                    act_std(act, 2)
                    act_transposes(act, 3)
                    for w in range(4):
                        mt, r = w // 2, w % 2
                        act.wait_ge(s_pr, w + 1)
                        for x, c in ((0, 0), (1, 2)):
                            ins = nc.scalar.activation(relu[:, r, x, :], scores[:, r, c * T:(c + 1) * T], ACT.Relu,
                                                       bias=bias[:, c, mt:mt + 1])
                        ins.then_inc(s_re, 1)
                        act.wait_ge(s_lo, w + 1)
                        nc.scalar.activation(low[:, r], low[:, r], ACT.Exp).then_inc(s_ph, 1)

                @block.vector
                def _(dve):
                    link = chain(dve, s_kvr)
                    dve_norm(dve, link, 2, xn)
                    dve.wait_ge(s_lw, 16 * 8)
                    for w in range(4):
                        mt, half, r = w // 2, w % 2, w % 2
                        dve.wait_ge(s_re, w + 1)
                        for x, c in ((0, 0), (1, 2)):
                            ins = nc.vector.tensor_scalar(low[:, r, x, :], scores[:, r, c * T:(c + 1) * T],
                                                          bias[:, c, mt:mt + 1], 0.0, ALU.add, ALU.min)
                        ins.then_inc(s_lo, 1)
                        dve.wait_ge(s_ph, w + 1)
                        link(nc.vector.tensor_tensor(relu[:, r], relu[:, r], low[:, r], ALU.add))
                        link(nc.vector.scalar_tensor_tensor(out=kv[:, r, :], in0=scores[:, r, T:2 * T],
                                                            scalar=bias[:, 1, mt:mt + 1], in1=relu[:, r, 0, :],
                                                            op0=ALU.add, op1=ALU.mult))
                        link(nc.vector.tensor_tensor_scan(cum[:, r, :], onesf.to_broadcast([P, T]), kv[:, r, :],
                                                          0.0, ALU.mult, ALU.add))
                        nc.vector.scalar_tensor_tensor(out=ctxT[:, mt, half * T:(half + 1) * T], in0=cum[:, r, :],
                                                       scalar=SCALE, in1=relu[:, r, 1, :], op0=ALU.mult,
                                                       op1=ALU.mult).then_inc(s_cx, 1)
                    link(nc.vector.tensor_tensor(X[:], X[:], bo[:].unsqueeze(1).to_broadcast([P, NT, D]), ALU.add))
                    for t in range(NT):
                        dve.wait_ge(s_oo, t + 1)
                        nc.vector.tensor_tensor(X[:, t, :], misc[:, t % 2, 0:D], X[:, t, :], ALU.add).then_inc(s_xl, 1)
                    dve.wait_ge(s_xl, NT)
        if stop == 3:
            return

        with ExitStack() as ffn:
            def sbf(name, shape, dt=F32):
                return ffn.enter_context(nc.sbuf_tensor(name, shape, dt))

            FT = F1 // P
            xn = sbf("xn_ffn", [P, NT, D])
            gate1 = sbf("gate1", [P, KT, E1])
            pr = sbf("probs1", [P, NT, E1])
            mx = sbf("mx1", [P, NT])
            m8 = sbf("m81", [P, NT, E1])
            i8 = sbf("i81", [P, NT, E1], U32)
            f8 = sbf("f81", [P, NT, E1])
            wt = sbf("wt1", [P, NT, 2])
            den2 = sbf("den2", [P, NT])
            one = sbf("one1", [P, 2, NT, E1])
            comb = sbf("comb1", [P, NT, E1])
            w13 = sbf("w13", [P, 2, KT, 2 * F1])
            w2 = sbf("w2", [P, 2, FT, D])
            sg = sbf("sg1", [P, 2, T])
            hT = sbf("hT1", [P, 2, FT, N])
            s_gw, s_lg, s_sub, s_ex = sem("gate1_loaded"), sem("logits1"), sem("shifted1"), sem("exp1")
            s_lnk = sem("chain1")
            s_ld = [sem("ffn_loaded0"), sem("ffn_loaded1")]
            s_gu, s_sl, s_h, s_y, s_acc, s_cmb = (sem("gate_up1"), sem("silu1"), sem("hidden1"), sem("down1"),
                                                  sem("added1"), sem("combine1"))
            IT = 2 * FT

            with nc.Block() as block:
                @block.sync
                def _(sp):
                    sp.dma_start(gate1[:], a["gate1"].rearrange("(k p) n -> p k n", p=P)).then_inc(s_gw, 16)

                    def load(j, e):
                        sp.dma_start(w13[:, j], a["w13"][e].rearrange("p (k n) -> p k n", k=KT)).then_inc(s_ld[j], 16)
                        sp.dma_start(w2[:, j], a["w2"][e].rearrange("p (k n) -> p k n", k=FT)).then_inc(s_ld[j], 16)
                    load(0, 0)
                    load(1, 1)
                    with sp.Fori(0, E1 // 2 - 1) as i:
                        for j in range(2):
                            sp.wait_ge(s_y, (2 * i + j + 1) * NT)
                            load(j, 2 * i + j + 2)
                    sp.wait_ge(s_acc, NT * E1)
                    sp.dma_start(out.rearrange("(t p) d -> p t d", p=P), X[:]).then_inc(s_out, 16)
                    sp.wait_ge(s_out, 16)

                @block.tensor
                def _(pe):
                    pe_transposes(pe, 4, xn, xn_ready(pe, 3))
                    pe.wait_ge(s_xnT, 20)
                    pe.wait_ge(s_gw, 16)
                    for t in range(NT):
                        for k in range(KT):
                            ins = nc.tensor.matmul(misc[:, 0, t * E1:(t + 1) * E1], xnT[:, k, t * P:(t + 1) * P],
                                                   gate1[:, k, :], start=(k == 0), stop=(k == KT - 1))
                    ins.then_inc(s_lg, 1)
                    pe.wait_ge(s_cmb, 1)

                    def gate_up(j, i, first):
                        pe.wait_ge(s_ld[j], (i + 1) * 32)
                        for q in range(IT):
                            ft, half = q // 2, q % 2
                            if not (first and q < 2):
                                pe.wait_ge(s_h, (2 * i + j) * IT + q - 1)
                            for g in range(2):
                                for k in range(KT):
                                    c = g * F1 + ft * P
                                    ins = nc.tensor.matmul(scores[:, q % 2, g * T:(g + 1) * T], w13[:, j, k, c:c + P],
                                                           xnT[:, k, half * T:(half + 1) * T],
                                                           start=(k == 0), stop=(k == KT - 1))
                            ins.then_inc(s_gu, 1)

                    def down(j, e, first):
                        pe.wait_ge(s_h, (e + 1) * IT)
                        for t in range(NT):
                            if not (first and t < 2):
                                pe.wait_ge(s_acc, e * NT + t - 1)
                            for f in range(FT):
                                ins = nc.tensor.matmul(misc[:, t % 2, 0:D], hT[:, j, f, t * P:(t + 1) * P],
                                                       w2[:, j, f, :], start=(f == 0), stop=(f == FT - 1))
                            ins.then_inc(s_y, 1)

                    gate_up(0, 0, True)
                    gate_up(1, 0, False)
                    down(0, 0, True)
                    with pe.Fori(1, E1 // 2) as i:
                        gate_up(0, i, False)
                        down(1, 2 * i - 1, False)
                        gate_up(1, i, False)
                        down(0, 2 * i, False)
                    down(1, E1 - 1, False)

                @block.scalar
                def _(act):
                    act_std(act, 3)
                    act_transposes(act, 4)
                    act.wait_ge(s_sub, 1)
                    nc.scalar.activation(pr[:], pr[:], ACT.Exp).then_inc(s_ex, 1)
                    with act.Fori(0, E1) as e:
                        for q in range(IT):
                            act.wait_ge(s_gu, e * IT + q + 1)
                            nc.scalar.activation(sg[:, q % 2, :], scores[:, q % 2, 0:T], ACT.Silu).then_inc(s_sl, 1)

                @block.vector
                def _(dve):
                    link = chain(dve, s_lnk)
                    dve_norm(dve, link, 3, xn)
                    dve.wait_ge(s_lg, 1)
                    lg = misc[:, 0, 0:NT * E1].rearrange("p (t e) -> p t e", e=E1)
                    bc = [P, NT, E1]
                    link(nc.vector.tensor_reduce(mx[:], lg, AX.X, ALU.max))
                    nc.vector.tensor_tensor(pr[:], lg, mx[:].unsqueeze(2).to_broadcast(bc), ALU.subtract).then_inc(s_sub, 1)
                    dve.wait_ge(s_ex, 1)
                    link(nc.vector.tensor_reduce(mx[:], pr[:], AX.X, ALU.add))
                    link(nc.vector.reciprocal(mx[:], mx[:]))
                    link(nc.vector.tensor_tensor(pr[:], pr[:], mx[:].unsqueeze(2).to_broadcast(bc), ALU.mult))
                    for t in range(NT):
                        ins = nc.vector.max(m8[:, t, :], pr[:, t, :])
                    link(ins)
                    for t in range(NT):
                        ins = nc.vector.max_index(i8[:, t, :], m8[:, t, :], pr[:, t, :])
                    link(ins)
                    nc.vector.tensor_copy(f8[:], i8[:])
                    link(nc.vector.tensor_tensor(den2[:], m8[:, :, 0], m8[:, :, 1], ALU.add))
                    link(nc.vector.reciprocal(den2[:], den2[:]))
                    link(nc.vector.tensor_tensor(wt[:], m8[:, :, 0:2], den2[:].unsqueeze(2).to_broadcast([P, NT, 2]), ALU.mult))
                    for t in range(NT):
                        for k in range(2):
                            ins = nc.vector.tensor_scalar(one[:, k, t, :], iota8, f8[:, t, k:k + 1], wt[:, t, k:k + 1],
                                                          ALU.is_equal, ALU.mult)
                    link(ins)
                    nc.vector.tensor_tensor(comb[:], one[:, 0], one[:, 1], ALU.add).then_inc(s_cmb, 1)
                    dve.wait_ge(s_cmb, 1)

                    def hidden(j, e):
                        for q in range(IT):
                            ft, half = q // 2, q % 2
                            dve.wait_ge(s_sl, e * IT + q + 1)
                            nc.vector.tensor_tensor(hT[:, j, ft, half * T:(half + 1) * T], sg[:, q % 2, :],
                                                    scores[:, q % 2, T:2 * T], ALU.mult).then_inc(s_h, 1)

                    def add(e, first):
                        for t in range(NT):
                            dve.wait_ge(s_y, e * NT + t + 1)
                            if not first:
                                dve.wait_ge(s_acc, (e - 1) * NT + t + 1)
                            nc.vector.scalar_tensor_tensor(out=X[:, t, :], in0=misc[:, t % 2, 0:D],
                                                           scalar=comb[:, t, bass.ds(e, 1)], in1=X[:, t, :],
                                                           op0=ALU.mult, op1=ALU.add).then_inc(s_acc, 1)

                    hidden(0, 0)
                    hidden(1, 1)
                    add(0, True)
                    with dve.Fori(1, E1 // 2) as i:
                        hidden(0, 2 * i)
                        add(2 * i - 1, False)
                        hidden(1, 2 * i + 1)
                        add(2 * i, False)
                    add(E1 - 1, False)


_INS = ['L0_attn_hidden_states']
STOP = 0


def shape_constants():
    r = np.arange(P)
    half = HD // 2
    inv = (np.float32(1.0) / np.power(np.float32(10000.0), np.arange(half, dtype=np.float32) / np.float32(half))).astype(np.float32)
    ang = (np.arange(T, dtype=np.float32)[:, None] * inv[None, :]).astype(np.float32)
    cos, sin = np.cos(ang).astype(np.float32), np.sin(ang).astype(np.float32)
    d = r % HD
    C = cos[:, d % half].T
    S = np.where(d[:, None] < half, -1.0, 1.0) * sin[:, d % half].T
    sec = np.stack([(r // n) % 2 for n in LEVELS], 1)
    pairs = [(r[:, None] // (2 * SB) % 2 == np.arange(32)[None, :] // SB) & (r[:, None] // SB % 2 == 1), np.zeros((P, 96))]
    ones2 = np.zeros((P, 64))
    ones2[:, [0, 33]] = 1
    cf = np.concatenate([np.eye(P), C, S, np.tile(np.eye(SB).ravel(), (P, 1)), sec,
                         np.tile(np.arange(E1), (P, 1)), np.ones((P, 1))] + pairs + [np.tile(np.arange(E0) * CAP, (P, 1)), ones2], 1).astype(np.float32)
    neg = -1e30
    causal = np.where(r[None, :] > r[:, None], neg, 0)
    strict = np.where(r[None, :] >= r[:, None], neg, 0)
    first = strict.copy()
    first[0, 0] = 0
    cb = np.concatenate([np.eye(P), causal, strict, first, r[:, None] <= r[None, :], np.ones((P, P))], 1)
    return cf, cb.astype(np.float32)


def kernel(**inputs):
    import concourse.bacc as _bacc
    from concourse.bass_utils import run_bass_kernel_spmd as _run

    g = {k: np.asarray(v) for k, v in inputs.items()}
    swap = np.arange(D).reshape(H, 2, HD // 2)[:, ::-1].reshape(-1)
    wq, wk = g["L0_attn_Wq"], g["L0_attn_Wk"]
    cf, cb = shape_constants()
    data = {
        "x": g["L0_attn_hidden_states"].reshape(N, D), "cf": cf, "cb": cb,
        "wk0": wk, "wk0r": wk[:, swap], "wq0": wq, "wq0r": wq[:, swap],
        "wvb0": np.concatenate([g["L0_attn_Wv"], g["L0_attn_Wb"]], 1), "wo0": g["L0_attn_Wo"],
        "bb": g["L0_attn_bb"], "gate0": g["L0_ffn_gate_w"].T,
        "wgu0": np.concatenate([g["L0_ffn_w_gate"], g["L0_ffn_w_up"]], 1).reshape(E0, 2 * F0, KT, P)
        .transpose(0, 3, 2, 1).reshape(E0, P, KT * 2 * F0),
        "wd0": g["L0_ffn_w_down"].transpose(0, 2, 1),
        "wk1": g["L1_attn_Wk"].T, "wv1": g["L1_attn_Wv"].T, "wq1": g["L1_attn_Wq"].T, "wo1": g["L1_attn_Wo"].T,
        "bk1": g["L1_attn_bk"], "bv1": g["L1_attn_bv"], "bq1": g["L1_attn_bq"], "bo1": g["L1_attn_bo"],
        "gate1": g["L1_ffn_gate_w"].T,
        "w13": np.concatenate([g["L1_ffn_w1"], g["L1_ffn_w3"]], 1).reshape(E1, 2 * F1, KT, P)
        .transpose(0, 3, 2, 1).reshape(E1, P, KT * 2 * F1),
        "w2": g["L1_ffn_w2"].reshape(E1, D, F1 // P, P).transpose(0, 3, 2, 1).reshape(E1, P, F1 // P * D),
    }
    nc = _bacc.Bacc("TRN2", target_bir_lowering=False, num_devices=1)
    arrays, aps = {}, {}
    for name, x in data.items():
        x = np.ascontiguousarray(x)
        arrays["in_" + name] = x
        aps[name] = nc.dram_tensor("in_" + name, x.shape, mybir.dt.from_np(x.dtype), kind="ExternalInput").ap()
    out = nc.dram_tensor("out_0", (N, D), F32, kind="ExternalOutput").ap()
    build_kernel(nc, aps, out, STOP)
    r = _run(nc, [arrays], core_ids=[0])
    return r.results[0]["out_0"].reshape(2, T, D)
```

```python
from contextlib import ExitStack

import numpy as np

import concourse.bass as bass
from concourse import mybir

ALU = mybir.AluOpType
ACT = mybir.ActivationFunctionType
F32 = mybir.dt.float32
BF16 = mybir.dt.bfloat16
U32 = mybir.dt.uint32
I32 = mybir.dt.int32
AX = mybir.AxisListType

P = 128
N, D = 1024, 256
NT = N // P
KT = D // P
T = 512
H, HD = 16, 16
GH = 8
NI = HT = T // P
UNITS = (H // GH) * (N // T)
SLOTS = 6
KR = SLOTS * HD
PART_A = (0, 0, 1, 1, 0, 2)
PART_B = (0, 1, 0, 1, 2, 0)
SB = 32
PAIRS = ((slice(0, 32), slice(32, 64)), (slice(64, 96), slice(96, 128)))
LEVELS = (32, 64)
SCALE = HD ** -0.5
EPS = 1e-5
E0, F0, K0 = 64, 96, 8
CAP = 2 * N * K0 // E0
E1, F1, K1 = 8, 512, 2
FT = F1 // P
TL = N * K1 // P + E1 - 1
BIG = 32768.0

OFF = {0: 0, 1: 512, 3: 896, 2: 1024}
WIDE = 10 * P
ROWAT = {3: 0, 2: 512, 0: 896, 1: 1024}


def build_kernel(nc, a, out):
    with ExitStack() as ctx:
        def sb(name, shape, dt=F32):
            return ctx.enter_context(nc.sbuf_tensor(name, shape, dt))

        def sem(name):
            return ctx.enter_context(nc.semaphore(name))

        scores = ctx.enter_context(nc.psum_tensor("scores", [P, 2, 3 * 512], F32))
        misc = ctx.enter_context(nc.psum_tensor("misc", [P, 2, 512], F32))

        X = sb("X", [P, NT, D])
        xnT = sb("xnT", [P, KT, N])
        stats = sb("stats", [P, NT, 6])
        mv = sb("mv", [P, NT, 2])
        std = sb("std", [P, NT])
        rstd = sb("rstd", [P, NT])
        eps = sb("eps", [P, 1])
        cf = sb("cf", [P, a["cf"].shape[1]])
        cb = sb("cb", [P, a["cb"].shape[1]], BF16)
        identf = cf[:, 0:128]
        cosT = cf[:, 128:640]
        sinT = cf[:, 640:1152]
        iota8 = cf[:, 1152:1160]
        onesf = cf[:, 1160:1161]
        identb = cb[:, 0:128]
        mask = {("q", 0): cb[:, 128:256], ("k", 0): cb[:, 384:512]}
        for i in range(1, NI):
            mask["q", i] = cb[:, 128:256]
            mask["k", i] = cb[:, 256:384]
        triu = cb[:, 512:640]
        onesb = cb[:, 640:768]

        s_x, s_w, s_eps = sem("x_loaded"), sem("weights_loaded"), sem("eps_set")
        s_var, s_std, s_xn = sem("variance"), sem("std"), sem("xn_tile")
        s_tr, s_xnT = sem("transposed"), sem("xnT_quarter")
        s_dv, s_po = sem("vector_chain"), sem("pool_chain")
        s_dv2, s_pk = sem("vector_chain_moe"), sem("weight_picked")
        s_out, s_zf = sem("stored"), sem("slots_zeroed")
        zero = sb("zero", [P, 1024])
        base0 = cf[:, 1161:1225]
        ones2 = cf[:, 1225:1289]
        NZ = E0 * CAP * D // (P * 1024)
        xbuf = nc.dram_tensor("expert_rows", [E0 * CAP, D], F32, kind="Internal").ap()
        ybuf = nc.dram_tensor("expert_outputs", [E0 * CAP, D], F32, kind="Internal").ap()
        xb_v = xbuf.rearrange("(e n) d -> e n d", e=E0)
        yb_v = ybuf.rearrange("(e n) d -> e n d", e=E0)
        xs = nc.dram_tensor("sorted_rows", [TL * P, D], F32, kind="Internal").ap()
        ys = nc.dram_tensor("sorted_outputs", [TL * P, D], F32, kind="Internal").ap()
        xs_v = xs.rearrange("(t p) d -> t p d", p=P)
        ys_v = ys.rearrange("(t p) d -> t p d", p=P)
        s_zf1, s_w1 = sem("sorted_rows_zeroed"), sem("ffn1_weights")
        NZ1 = -(-TL // 4)
        xb_z = xbuf.rearrange("(z p n) d -> z p (n d)", z=NZ, p=P)

        def chain(eng, s):
            count = [0]

            def link(ins):
                count[0] += 1
                ins.then_inc(s, 1)
                eng.wait_ge(s, count[0])
            return link

        def dve_norm(dve, link, n, xn, tiles=range(NT)):
            lo, hi = tiles.start, tiles.stop
            for t in tiles:
                ins = nc.vector.bn_stats(stats[:, t, :], X[:, t, :])
            link(ins)
            for t in tiles:
                ins = nc.vector.bn_aggr(mv[:, t, :], stats[:, t, :])
            ins.then_inc(s_var, 1)
            dve.wait_ge(s_std, n + 1)
            link(nc.vector.reciprocal(rstd[:, lo:hi], std[:, lo:hi]))
            for t in tiles:
                nc.vector.tensor_scalar(xn[:, t, :], X[:, t, :], mv[:, t, 0:1], rstd[:, t:t + 1],
                                        ALU.subtract, ALU.mult).then_inc(s_xn, 1)

        def act_std(act, n, tiles=range(NT)):
            lo, hi = tiles.start, tiles.stop
            act.wait_ge(s_var, n + 1)
            nc.scalar.activation(std[:, lo:hi], mv[:, lo:hi, 1], ACT.Sqrt, bias=eps[:, 0:1]).then_inc(s_std, 1)

        def pe_transposes(pe, n, src, ready, pairs=range(NT // 2)):
            for p in pairs:
                ready(p)
                if 4 * n + p - 1 > 0:
                    pe.wait_ge(s_xnT, 4 * n + p - 1)
                for k in range(KT):
                    for t in range(2):
                        c = (2 * k + t) * P
                        ins = nc.tensor.transpose(misc[:, p % 2, c:c + P],
                                                  src[:, 2 * p + t, k * P:(k + 1) * P], identf)
                ins.then_inc(s_tr, 1)

        def act_transposes(act, n, pairs=range(NT // 2)):
            for p in pairs:
                act.wait_ge(s_tr, 4 * n + p + 1)
                nc.scalar.copy(xnT[:, :, 2 * P * p:2 * P * (p + 1)],
                               misc[:, p % 2, :].rearrange("p (k n) -> p k n", k=KT)).then_inc(s_xnT, 1)

        def xn_ready(pe, l):
            return lambda p: pe.wait_ge(s_xn, NT * l + 2 * p + 2)

        with ExitStack() as att:
            def sba(name, shape, dt=F32):
                return att.enter_context(nc.sbuf_tensor(name, shape, dt))

            early = sba("early", [P, 4608])
            wqk = early[:, 0:2048].rearrange("p (a k d) -> p a k d", a=4, k=KT)
            ropes = early[:, 2048:3072].rearrange("p (a n) -> p a n", a=2)
            parts = early[:, 3072:4608].bitcast(BF16).rearrange("p (a b n) -> p a b n", a=2, b=3)
            T1 = early[:, 0:1024].rearrange("p (a h n) -> p a h n", a=2, h=GH)
            wvb = sba("wvb", [P, KT, D + H])
            wo0 = sba("wo0", [P, KT, D])
            bb = sba("bb", [P, H])
            VB = sba("VB", [P, NT, D + H])
            AO = sba("AO", [P, NT, D])
            stk = {c: sba(f"stack_{c}", [P, 2, GH, T], BF16) for c in ("k", "B", "q")}
            nm = sba("nm", [P, 2, GH * NI])
            nmr = sba("nmr", [P, GH * NI])
            nms = sba("nms", [P, 2, 3, GH * NI], BF16)
            mrow = sba("mrow", [3 * GH * NI, 2, P], BF16)
            E = sba("E", [P, GH, WIDE])
            bankT = sba("bankT", [P, 512])
            den = sba("den", [P, GH * NI])
            ng = sba("ng", [P, GH * NI])
            G = sba("G", [P, SB])
            LB = sba("LB", [P, SB, SB])
            Y = sba("Y", [P, SB, SB])
            YT = LB
            tmp = sba("tmp", [P, 2, SB * SB // 8 + SB // 4])
            s_inv = sem("inversion_step")
            XT = sba("XT", [P, GH * NI, P])
            XR = sba("XR", [P, GH * NI, 64])
            R = sba("R", [P, GH, 32])
            EQ23 = sba("EQ23", [P, 2, WIDE])
            U = sba("U", [P, NI, GH, 32])
            rec = sba("rec", [P, NI, 4])

            scr = nc.dram_tensor("split_heads", [2, 3, D, N], BF16, kind="Internal").ap()
            edd = nc.dram_tensor("diagonals", [2, GH * NI, P, P], F32, kind="Internal").ap()
            xsd = nc.dram_tensor("inverses", [2, 2, P, SB, SB], F32, kind="Internal").ap()

            s_pj, s_rf, s_parts = sem("projected"), sem("projection_read"), sem("parts_split")
            s_pw = [sem("parts_stored0"), sem("parts_stored1")]
            s_stk = [sem("stack_loaded0"), sem("stack_loaded1")]
            s_stq = [sem("q_stack_loaded0"), sem("q_stack_loaded1")]
            s_ones, s_cb = sem("ones_set"), sem("masks_ready")
            s_v, s_vc, s_vb = sem("v_projected"), sem("v_copied"), sem("beta_ready")
            s_sa, s_sc, s_fd, s_fa = sem("rows_ready"), sem("scores_ready"), sem("maxima_taken"), sem("exps_done")
            s_nms, s_mt, s_mr, s_ml = sem("maxima_split"), sem("maxima_turned"), sem("maxima_rows"), sem("maxima_in_stack")
            s_dk, s_dq = sem("kk_masked"), sem("qk_masked")
            s_dc, s_dt, s_oc, s_ot = sem("denominators_copied"), sem("denominators_turned"), sem("o_copied"), sem("o_turned")
            s_den, s_ng, s_gt, s_g = sem("denominators"), sem("g_ready"), sem("g_turned"), sem("g_in_blocks")
            s_ed, s_lb, s_y, s_ys, s_z, s_z2, s_xt, s_xr = (sem("diag_stored"), sem("blocks_loaded"), sem("blocks_inverted"),
                                                sem("inverses_stored"), sem("XT_zeroed"), sem("XR_zeroed"),
                                                sem("XT_loaded"), sem("XR_loaded"))
            s_tt, s_t1, s_pq, s_lv = sem("level_T"), sem("level_T1"), sem("level_PQ"), sem("level_joined")
            s_sn, s_st1, s_un, s_ut = sem("sums_copied"), sem("sums_turned"), sem("u_copied"), sem("u_turned")
            s_s, s_r, s_us, s_uv = sem("solve_sums"), sem("solve_r"), sem("solve_u"), sem("u_stored")
            s_o, s_ao, s_wo, s_xw = sem("attended"), sem("ao_ready"), sem("wo_done"), sem("x_attended")

            def EQ(h):
                if h % 4 < 2:
                    return early[:, 1536 + (h % 4) * WIDE:1536 + (h % 4 + 1) * WIDE]
                return EQ23[:, h % 4 - 2]

            def use(c, u):
                if c == 0:
                    return 16 * u - 8 if u else 0
                return 16 * u + 16 if u + 1 < UNITS else 16 * u + 8

            def blk(tile, h, jt, it):
                c = OFF[jt] + (it - jt) * P
                return tile[:, h, c:c + P]

            def ahead(u):
                return GH if u >= 2 else 0

            def maxima_due(u, q):
                first, n = ahead(u), 2 * GH - ahead(u)
                return range(first + max(0, q - 1) * n // 7, first + q * n // 7)

            def store_parts(q, w):
                mt, half, c = w // 4, w // 2 % 2, w % 2
                q.wait_ge(s_parts, w + 1)
                q.dma_start(scr[c, :, mt * P:(mt + 1) * P, half * T:(half + 1) * T].rearrange("t p n -> p t n"),
                             parts[:, w % 2]).then_inc(s_pw[w % 2], 16)

            def load_stack(q, u, c):
                hg, b = u // 2, u % 2
                x, order = {"k": (0, PART_A), "B": (0, PART_B), "q": (1, PART_A)}[c]
                for s, part in enumerate(order):
                    q.dma_start(stk[c][HD * s:HD * (s + 1), u % 2],
                                scr[x, part, hg * P:(hg + 1) * P, b * T:(b + 1) * T]
                                .rearrange("(h d) n -> d h n", d=HD)).then_inc((s_stq if c == "q" else s_stk)[u % 2], 16)

            def load_stacks(q, u):
                q.wait_ge(s_pw[0], 16 * (u + 1))
                q.wait_ge(s_pw[1], 16 * (u + 1))
                for c in "kBq":
                    load_stack(q, u, c)

            with nc.Block() as block:
                @block.tensor
                def _(pe):
                    pe.wait_ge(s_w, 16 * 9)
                    pe_transposes(pe, 0, AO, xn_ready(pe, 0))
                    pe.wait_ge(s_xnT, 4)
                    def project(w):
                        mt, half, c = w // 4, w // 2 % 2, w % 2
                        if w >= 2:
                            pe.wait_ge(s_rf, w - 1)
                        for rot in range(2):
                            for k in range(KT):
                                ins = nc.tensor.matmul(scores[:, w % 2, rot * 512:rot * 512 + T],
                                                       wqk[:, 2 * c + rot, k, mt * P:(mt + 1) * P],
                                                       xnT[:, k, half * T:(half + 1) * T],
                                                       start=(k == 0), stop=(k == KT - 1))
                        ins.then_inc(s_pj, 1)

                    for w in range(2):
                        project(w)
                    for t in range(NT):
                        if t >= 2:
                            pe.wait_ge(s_vc, t - 1)
                        for k in range(KT):
                            ins = nc.tensor.matmul(misc[:, t % 2, 0:D + H], xnT[:, k, t * P:(t + 1) * P],
                                                   wvb[:, k, :], start=(k == 0), stop=(k == KT - 1))
                        ins.then_inc(s_v, 1)
                    pe.wait_ge(s_rf, 2)
                    pe.wait_ge(s_vc, NT)
                    pe.wait_ge(s_ones, 1)
                    pe.wait_ge(s_cb, 1)

                    def turn_maxima(u, c):
                        pe.wait_ge(s_nms, 2 * u + c + 1)
                        if u:
                            pe.wait_ge(s_g, u)
                        nc.tensor.transpose(misc[0:96, c, 0:64].bitcast(BF16),
                                            nms[:, c, :, :].rearrange("p a b -> p (a b)"), identb
                                            ).then_inc(s_mt, 1)

                    def row_scores(u, m, slot):
                        c, h = "kq"[m // 8], m % 8
                        for it in range(NI):
                            w = (it + 1) * P
                            o = ROWAT[it]
                            nc.tensor.matmul(scores[:, slot, o:o + w],
                                             stk[c][0:KR, u % 2, h, it * P:w], stk["B"][0:KR, u % 2, h, 0:w],
                                             start=True, stop=False)
                            ins = nc.tensor.matmul(scores[:, slot, o + w - P:o + w], identb,
                                                   mask[c, it], start=False, stop=True)
                        ins.then_inc(s_sa, 1)

                    def transposed_scores(u, c, h):
                        k = use(c, u) + h
                        if k >= 2:
                            pe.wait_ge(s_fa, k - 1)
                        for jt in range(NI):
                            o = OFF[jt]
                            ins = nc.tensor.matmul(scores[:, k % 2, o:o + T - jt * P],
                                                   stk["B"][0:KR + 3, u % 2, h, jt * P:(jt + 1) * P],
                                                   stk["kq"[c]][0:KR + 3, u % 2, h, jt * P:T],
                                                   start=True, stop=True)
                        ins.then_inc(s_sc, 1)

                    def key_scores(u, heads):
                        pe.wait_ge(s_ml, 96 * u + 96)
                        pe.wait_ge(s_fd, 16 * (u + 1))
                        if u:
                            pe.wait_ge(s_lv, 8 * u)
                        for h in heads:
                            transposed_scores(u, 0, h)

                    def key_softmax(u):
                        key_scores(u, range(4 if u else 0, GH))
                        pe.wait_ge(s_mr, 2 * u + 2)
                        if u:
                            pe.wait_ge(s_uv, 4 * u)
                        pe.wait_ge(s_dk, GH * (u + 1))
                        for hh in range(2):
                            for jt in range(NI):
                                for g in range(4):
                                    o = OFF[jt]
                                    ins = nc.tensor.matmul(misc[32 * g:32 * g + 32, 0, jt * P:T], ones2[:, 32 * hh:32 * hh + 32],
                                                           E[:, 4 * hh + g, o:o + T - jt * P],
                                                           start=(hh == 0 and jt == 0), stop=(hh == 1 and jt == NI - 1),
                                                           skip_group_check=True)
                        ins.then_inc(s_den, 1)
                        pe.wait_ge(s_dc, u + 1)
                        for it in range(NI):
                            ins = nc.tensor.transpose(misc[:, 1, it * P:(it + 1) * P], bankT[:, it * P:(it + 1) * P], identf)
                        ins.then_inc(s_dt, 1)
                        pe.wait_ge(s_ng, u + 1)
                        nc.tensor.transpose(misc[0:GH * NI, 1, 0:P], ng[:], identf).then_inc(s_gt, 1)

                    def sums(u, q):
                        li, it = q // NI, q % NI
                        g = 8 * u + q
                        if q:
                            pe.wait_ge(s_t1, g)
                        if q >= 4:
                            pe.wait_ge(s_lv, g - 3)
                        for h in range(GH):
                            e, x = blk(E, h, it, it), h * NI + it
                            if li == 1:
                                ins = nc.tensor.matmul(scores[64:128, 1, 64 * h:64 * h + 64], e[0:64, 64:128],
                                                       XR[0:64, x, :], start=True, stop=True)
                                continue
                            for lo, hi in PAIRS:
                                ins = nc.tensor.matmul(scores[hi, 1, 32 * h:32 * h + 32], e[lo, hi], XR[lo, x, 0:32],
                                                       start=True, stop=True, skip_group_check=True,
                                                       tile_position=(lo.start, hi.start))
                        ins.then_inc(s_tt, 1)

                    def join(u, q):
                        li, it = q // NI, q % NI
                        n = LEVELS[li]
                        g = 8 * u + q
                        pe.wait_ge(s_t1, g + 1)
                        if q:
                            pe.wait_ge(s_lv, g)
                        for h in range(GH):
                            x = h * NI + it
                            if li == 1:
                                ins = nc.tensor.matmul(scores[0:64, 1, 1024 + 64 * h:1088 + 64 * h], T1[64:128, li, h, :],
                                                       XT[64:128, x, 64:128], start=True, stop=True)
                                continue
                            for lo, hi in PAIRS:
                                if lo.start == 0:
                                    nc.tensor.matmul(scores[hi, 1, 512 + 32 * h:544 + 32 * h], XT[hi, x, hi],
                                                     T1[hi, li, h, 0:32], start=True, stop=True, skip_group_check=True,
                                                     tile_position=(hi.start, hi.start))
                                ins = nc.tensor.matmul(scores[lo, 1, 1024 + 32 * h:1056 + 32 * h], T1[hi, li, h, 0:32],
                                                       XT[hi, x, hi], start=True, stop=True, skip_group_check=True,
                                                       tile_position=(hi.start, lo.start))
                        ins.then_inc(s_pq, 1)

                    def solve(u):
                        for it in range(NI):
                            if it:
                                pe.wait_ge(s_uv, 4 * u + it)
                                for hh in range(2):
                                    for jt in range(it):
                                        for g in range(4):
                                            h = 4 * hh + g
                                            ins = nc.tensor.matmul(misc[32 * g:32 * g + 32, 0, hh * P:(hh + 1) * P],
                                                                   U[:, jt, h, :], blk(E, h, jt, it),
                                                                   start=(jt == 0), stop=(jt == it - 1),
                                                                   skip_group_check=True)
                                ins.then_inc(s_s, 1)
                                pe.wait_ge(s_sn, 3 * u + it)
                                for hh in range(2):
                                    ins = nc.tensor.transpose(misc[:, 0, hh * P:(hh + 1) * P],
                                                              bankT[:, hh * P:(hh + 1) * P], identf)
                                ins.then_inc(s_st1, 1)
                            pe.wait_ge(s_r, 4 * u + it + 1)
                            for hh in range(2):
                                for g in range(4):
                                    h = 4 * hh + g
                                    ins = nc.tensor.matmul(misc[32 * g:32 * g + 32, 1, hh * P:(hh + 1) * P],
                                                           R[:, h, :], XT[:, h * NI + it, :], start=True, stop=True,
                                                           skip_group_check=True)
                            ins.then_inc(s_us, 1)
                            if u + 1 < UNITS and it >= NI - 2:
                                key_scores(u + 1, range(2 * (it - NI + 2), 2 * (it - NI + 2) + 2))
                            pe.wait_ge(s_un, 4 * u + it + 1)
                            for hh in range(2):
                                ins = nc.tensor.transpose(misc[:, 1, hh * P:(hh + 1) * P],
                                                          bankT[:, 256 + hh * P:256 + (hh + 1) * P], identf)
                            ins.then_inc(s_ut, 1)

                    def attend(u, hh):
                        pe.wait_ge(s_dq, GH * u + 4 * (hh + 1))
                        for jt in range(NI):
                            for g in range(4):
                                h, o = 4 * hh + g, OFF[jt]
                                ins = nc.tensor.matmul(misc[32 * g:32 * g + 32, hh, jt * P:T], U[:, jt, h, :],
                                                       EQ(h)[:, o:o + T - jt * P], start=(jt == 0),
                                                       stop=(jt == NI - 1), skip_group_check=True)
                        ins.then_inc(s_o, 1)

                    def turn_outputs(u, hh):
                        pe.wait_ge(s_oc, 2 * u + hh + 1)
                        for it in range(NI):
                            ins = nc.tensor.transpose(misc[:, hh, it * P:(it + 1) * P], bankT[:, it * P:(it + 1) * P], identf)
                        ins.then_inc(s_ot, 1)

                    def stacks_loaded(u, which):
                        for c in which:
                            pe.wait_ge((s_stq if c == "q" else s_stk)[u % 2], 16 * (6 if c == "q" else 12) * (u // 2 + 1))

                    stacks_loaded(0, "kq")
                    for m in range(16):
                        if m >= 2:
                            pe.wait_ge(s_fd, m - 1)
                        row_scores(0, m, m % 2)
                    turn_maxima(0, 0)
                    turn_maxima(0, 1)
                    key_softmax(0)
                    pe.wait_ge(s_fa, 8)
                    for w in range(2, 8):
                        project(w)
                    pe.wait_ge(s_rf, 8)
                    for u in range(UNITS):
                        last = u + 1 == UNITS
                        pe.wait_ge(s_xt, 16 * 4 * (u + 1))
                        pe.wait_ge(s_xr, 16 * 3 * (u + 1))
                        pe.wait_ge(s_fa, 16 * u + 8)
                        for q in range(8):
                            sums(u, q)
                            if q:
                                join(u, q - 1)
                            if not last:
                                if q == 1:
                                    stacks_loaded(u + 1, "kq")
                                for m in maxima_due(u + 1, q):
                                    pe.wait_ge(s_fd, 16 * (u + 1) + m)
                                    row_scores(u + 1, m, 0)
                        join(u, 7)
                        if not last:
                            turn_maxima(u + 1, 0)
                            turn_maxima(u + 1, 1)
                            pe.wait_ge(s_mr, 2 * u + 4)
                        pe.wait_ge(s_lv, 8 * (u + 1))
                        pe.wait_ge(s_g, u + 1)
                        solve(u)
                        if not last:
                            key_softmax(u + 1)
                            pe.wait_ge(s_g, u + 2)
                        else:
                            pe.wait_ge(s_uv, 4 * (u + 1))
                        for h in range(GH):
                            transposed_scores(u, 1, h)
                            if h == 4:
                                attend(u, 0)
                            if h == 6:
                                turn_outputs(u, 0)
                        attend(u, 1)
                        turn_outputs(u, 1)
                        if u + 2 < UNITS:
                            stacks_loaded(u + 2, "k")
                            pe.wait_ge(s_fa, use(1, u) + GH)
                            for m in range(ahead(u + 2)):
                                if m >= 2:
                                    pe.wait_ge(s_fd, 16 * (u + 2) + m - 1)
                                row_scores(u + 2, m, m % 2)
                            pe.wait_ge(s_fd, 16 * (u + 2) + ahead(u + 2))
                        pe.wait_ge(s_ao, 2 * (u + 1))
                    pe_transposes(pe, 1, AO, lambda p: pe.wait_ge(s_ao, 2 * UNITS))
                    pe.wait_ge(s_xnT, 8)
                    for t in range(NT):
                        if t >= 2:
                            pe.wait_ge(s_xw, t - 1)
                        for k in range(KT):
                            ins = nc.tensor.matmul(misc[:, t % 2, 0:D], xnT[:, k, t * P:(t + 1) * P],
                                                   wo0[:, k, :], start=(k == 0), stop=(k == KT - 1))
                        ins.then_inc(s_wo, 1)

                @block.vector
                def _(dve):
                    link = chain(dve, s_dv)
                    nc.vector.memset(eps[:], EPS).then_inc(s_eps, 1)
                    link(nc.vector.memset(U[:], 0.0))
                    link(nc.vector.memset(U[:, :, :, HD:HD + 1], 1.0))
                    link(nc.vector.memset(R[:], 0.0))
                    dve.wait_ge(s_x, 16)
                    dve_norm(dve, link, 0, AO)
                    dve.wait_ge(s_w, 16 * 9)
                    link(nc.vector.tensor_copy(cb[:], E[:, 0, 0:a["cb"].shape[1]]))
                    nc.vector.sem_inc(s_cb, 1)
                    def rotate_and_split(w):
                        dve.wait_ge(s_pj, w + 1)
                        if w >= 2:
                            dve.wait_ge(s_pw[w % 2], 16 * (w // 2))
                        a0, a1 = ropes[:, 0, :], ropes[:, 1, :]
                        nc.vector.tensor_tensor(a0, scores[:, w % 2, 0:T], cosT, ALU.mult)
                        ins = nc.vector.tensor_tensor(a1, scores[:, w % 2, 512:512 + T], sinT, ALU.mult)
                        link(ins)
                        nc.vector.sem_inc(s_rf, 1)
                        link(nc.vector.tensor_tensor(a0, a0, a1, ALU.add))
                        link(nc.vector.tensor_copy(parts[:, w % 2, 0, :], a0))
                        link(nc.vector.tensor_tensor(a0, a0, parts[:, w % 2, 0, :], ALU.subtract))
                        link(nc.vector.tensor_copy(parts[:, w % 2, 1, :], a0))
                        link(nc.vector.tensor_tensor(parts[:, w % 2, 2, :], a0, parts[:, w % 2, 1, :],
                                                     ALU.subtract))
                        nc.vector.sem_inc(s_parts, 1)

                    rotate_and_split(0)
                    rotate_and_split(1)
                    dve.wait_ge(s_vc, NT)
                    bcol = VB[:, :, D:D + H]
                    link(nc.vector.tensor_tensor(bcol, bcol, bb[:].unsqueeze(1).to_broadcast([P, NT, H]), ALU.add))

                    def maxima(u, m, slot):
                        c, h = m // 8, m % 8
                        dve.wait_ge(s_sa, 16 * u + m + 1)
                        for it in range(NI):
                            o = ROWAT[it]
                            ins = nc.vector.tensor_reduce(nm[:, c, NI * h + it:NI * h + it + 1],
                                                          scores[:, slot, o:o + (it + 1) * P],
                                                          AX.X, ALU.max, negate=True)
                        ins.then_inc(s_fd, 1)
                        if h < GH - 1:
                            return
                        dve.wait_ge(s_fd, 16 * u + 8 * (c + 1))
                        if u:
                            dve.wait_ge(s_mt, 2 * (u - 1) + c + 1)
                        link(nc.vector.tensor_copy(nms[:, c, 0, :], nm[:, c, :]))
                        link(nc.vector.tensor_tensor(nmr[:], nm[:, c, :], nms[:, c, 0, :], ALU.subtract))
                        link(nc.vector.tensor_copy(nms[:, c, 1, :], nmr[:]))
                        link(nc.vector.tensor_tensor(nms[:, c, 2, :], nmr[:], nms[:, c, 1, :], ALU.subtract))
                        nc.vector.sem_inc(s_nms, 1)

                    def scale(u):
                        hg, b = u // 2, u % 2
                        dve.wait_ge(s_dt, u + 1)
                        link(nc.vector.tensor_scalar(
                            den[:].rearrange("p (a g i) -> p a g i", a=2, g=4),
                            misc[:, 1, :].rearrange("p (i g a) -> p a g i", i=NI, g=4)[:, 0:2], 1e-30, None, ALU.max))
                        link(nc.vector.reciprocal(den[:], den[:]))
                        beta = VB[:, b * NI:(b + 1) * NI, D + hg * GH:D + (hg + 1) * GH].rearrange("p i h -> p h i")
                        link(nc.vector.scalar_tensor_tensor(
                            out=ng[:].rearrange("p (h i) -> p h i", i=NI),
                            in0=den[:].rearrange("p (h i) -> p h i", i=NI), scalar=-1.0, in1=beta,
                            op0=ALU.mult, op1=ALU.mult))
                        nc.vector.sem_inc(s_ng, 1)
                        dve.wait_ge(s_gt, u + 1)
                        for s4 in range(4):
                            ins = nc.vector.tensor_copy(G[32 * s4:32 * s4 + 32, :],
                                                        misc[0:32, 1, 32 * s4:32 * s4 + 32])
                        link(ins)
                        nc.vector.sem_inc(s_g, 1)

                    inverted = [0]

                    def invert(u):
                        if u:
                            dve.wait_ge(s_ys, 32 * u)
                        flat = Y[:].rearrange("p c i -> p (c i)")
                        link(nc.vector.memset(Y[:], 0.0))
                        nc.vector.memset(flat[:, 0:SB * SB - 1].rearrange("p (a b) -> p a b", b=SB + 1)[:, :, 0], 1.0)
                        nc.vector.memset(flat[:, SB * SB - 1:SB * SB], 1.0)
                        dve.wait_ge(s_lb, 16 * 4 * (u + 1))
                        link(nc.vector.tensor_tensor(
                            LB[:], LB[:], G[:].unsqueeze(1).to_broadcast([P, SB, SB]), ALU.mult))
                        Yc = Y[:].rearrange("p (c two) i -> p two c i", two=2)
                        done = {0: inverted[0], 1: inverted[0]}
                        for k in range(SB - 1):
                            w = SB - 1 - k
                            parities = [(x, (k - x) // 2 + 1) for x in range(2) if k >= x]
                            products = {}
                            for x, n in parities:
                                part = tmp[:, x, 0:n * w].rearrange("p (c i) -> p c i", i=w)
                                if done[x]:
                                    dve.wait_ge(s_inv, done[x])
                                nc.vector.tensor_tensor(
                                    part, Yc[:, x, 0:n, k:k + 1].to_broadcast([P, n, w]),
                                    LB[:, k:k + 1, k + 1:SB].to_broadcast([P, n, w]), ALU.mult).then_inc(s_inv, 1)
                                inverted[0] += 1
                                products[x] = part, inverted[0]
                            for x, n in parities:
                                part, made = products[x]
                                below = Yc[:, x, 0:n, k + 1:SB]
                                dve.wait_ge(s_inv, made)
                                nc.vector.tensor_tensor(below, below, part, ALU.add).then_inc(s_inv, 1)
                                inverted[0] += 1
                                done[x] = inverted[0]
                        dve.wait_ge(s_inv, inverted[0])
                        link(nc.vector.tensor_copy(YT[:], Y[:].rearrange("p c i -> p i c")))
                        nc.vector.sem_inc(s_y, 1)

                    def joined(u, q):
                        li, it = q // NI, q % NI
                        n = LEVELS[li]
                        dve.wait_ge(s_pq, 8 * u + q + 1)
                        xt = XT[:].rearrange("p (h i) c -> p h i c", i=NI)[:, :, it, :]
                        xr = XR[:].rearrange("p (h i) c -> p h i c", i=NI)[:, :, it, :]
                        if li == 1:
                            ins = nc.vector.tensor_copy(xt[0:64, :, 64:128],
                                                        scores[0:64, 1, 1024:1536].rearrange("p (h n) -> p h n", h=GH))
                        else:
                            nc.vector.tensor_copy(xr[32:64, :, 0:32],
                                                  scores[32:64, 1, 512:768].rearrange("p (h n) -> p h n", h=GH))
                            for lo, hi in PAIRS:
                                ins = nc.vector.tensor_copy(xt[lo, :, hi],
                                                            scores[lo, 1, 1024:1280].rearrange("p (h n) -> p h n", h=GH))
                        ins.then_inc(s_lv, 1)

                    def scaled_sums(u, q):
                        li, it = q // NI, q % NI
                        n = LEVELS[li]
                        dve.wait_ge(s_tt, 8 * u + q + 1)
                        g_ = ng[:].rearrange("p (h i) -> p h i", i=NI)[:, :, it].unsqueeze(2)
                        for hi in (slice(64, 128),) if li else (PAIRS[0][1], PAIRS[1][1]):
                            ins = nc.vector.tensor_tensor(
                                T1[hi, li, :, 0:n], scores[hi, 1, 0:GH * n].rearrange("p (h n) -> p h n", h=GH),
                                g_[hi].to_broadcast([hi.stop - hi.start, GH, n]), ALU.mult)
                        ins.then_inc(s_t1, 1)

                    def solved(u):
                        hg, b = u // 2, u % 2
                        for it in range(NI):
                            v = VB[:, b * NI + it, hg * P:(hg + 1) * P].rearrange("p (h d) -> p h d", d=HD)
                            g_ = ng[:].rearrange("p (h i) -> p h i", i=NI)[:, :, it].unsqueeze(2).to_broadcast([P, GH, HD])
                            r = R[:, :, 0:HD]
                            if it:
                                dve.wait_ge(s_st1, 3 * u + it)
                                link(nc.vector.tensor_tensor(
                                    r, misc[:, 0, 0:2 * P].rearrange("p (h d) -> p h d", d=32)[:, :, 0:HD], g_, ALU.mult))
                                nc.vector.tensor_tensor(r, r, v, ALU.add).then_inc(s_r, 1)
                            else:
                                nc.vector.tensor_copy(r, v).then_inc(s_r, 1)
                            dve.wait_ge(s_ut, 4 * u + it + 1)
                            nc.vector.tensor_copy(U[:, it, :, 0:HD],
                                                  misc[:, 1, 0:2 * P].rearrange("p (h d) -> p h d", d=32)[:, :, 0:HD]
                                                  ).then_inc(s_uv, 1)

                    def outputs(u):
                        hg, b = u // 2, u % 2
                        for hh in range(2):
                            dve.wait_ge(s_ot, 2 * u + hh + 1)
                            o4 = misc[:, hh, :].rearrange("p (i g d) -> p i g d", i=NI, g=4)
                            if u or hh:
                                dve.wait_ge(s_ao, 2 * u + hh)
                            link(nc.vector.reciprocal(rec[:], o4[:, :, :, HD]))
                            c = (hg * GH + hh * 4) * HD
                            nc.vector.tensor_tensor(
                                AO[:, b * NI:(b + 1) * NI, c:c + 4 * HD].rearrange("p i (g d) -> p i g d", g=4),
                                o4[:, :, :, 0:HD], rec[:].unsqueeze(3).to_broadcast([P, NI, 4, HD]),
                                ALU.mult).then_inc(s_ao, 1)

                    for m in range(16):
                        maxima(0, m, m % 2)
                    scale(0)
                    for w in range(2, 4):
                        rotate_and_split(w)
                    invert(0)
                    for w in range(4, 8):
                        rotate_and_split(w)
                    for u in range(UNITS):
                        last = u + 1 == UNITS
                        dve.wait_ge(s_xt, 16 * 4 * (u + 1))
                        dve.wait_ge(s_xr, 16 * 3 * (u + 1))
                        for q in range(8):
                            if q:
                                joined(u, q - 1)
                            scaled_sums(u, q)
                            if not last:
                                for m in maxima_due(u + 1, q):
                                    maxima(u + 1, m, 0)
                        joined(u, 7)
                        solved(u)
                        if not last:
                            scale(u + 1)
                            invert(u + 1)
                        outputs(u)
                        if u + 2 < UNITS:
                            for m in range(ahead(u + 2)):
                                maxima(u + 2, m, m % 2)
                    for t in range(NT):
                        dve.wait_ge(s_wo, t + 1)
                        nc.vector.tensor_tensor(X[:, t, :], misc[:, t % 2, 0:D], X[:, t, :], ALU.add).then_inc(s_xw, 1)
                    dve.wait_ge(s_xw, NT)

                @block.scalar
                def _(act):
                    act.wait_ge(s_eps, 1)
                    act_std(act, 0)
                    act_transposes(act, 0)
                    for t in range(NT):
                        act.wait_ge(s_v, t + 1)
                        nc.scalar.copy(VB[:, t, :], misc[:, t % 2, 0:D + H]).then_inc(s_vc, 1)

                    def rows(u, c):
                        act.wait_ge(s_mt, 2 * u + c + 1)
                        if u:
                            act.wait_ge(s_ml, 96 * (u - 1) + 48 * (c + 1))
                        nc.scalar.copy(mrow[:, c, :], misc[0:96, c, 0:64].bitcast(BF16)).then_inc(s_mr, 1)

                    def exps(u, c, h):
                        k = use(c, u) + h
                        act.wait_ge(s_sc, k + 1)
                        if c and h == 4:
                            act.wait_ge(s_o, 2 * u + 1)
                        nc.scalar.activation(EQ(h) if c else E[:, h, :], scores[:, k % 2, 0:WIDE], ACT.Exp,
                                             scale=SCALE).then_inc(s_fa, 1)

                    def key_softmax(u):
                        for h in range(2 if u else 0, GH):
                            exps(u, 0, h)
                        act.wait_ge(s_den, u + 1)
                        nc.scalar.copy(bankT[:], misc[:, 0, :]).then_inc(s_dc, 1)

                    def copy_outputs(u, hh):
                        act.wait_ge(s_o, 2 * u + hh + 1)
                        if hh:
                            act.wait_ge(s_ot, 2 * u + 1)
                        else:
                            act.wait_ge(s_dt, min(u + 2, UNITS))
                        nc.scalar.copy(bankT[:], misc[:, hh, :]).then_inc(s_oc, 1)

                    rows(0, 0)
                    rows(0, 1)
                    key_softmax(0)
                    for w in range(2, 8):
                        store_parts(act, w)
                        if w == 3:
                            load_stacks(act, 1)
                    for u in range(UNITS):
                        for z in range(NZ // UNITS):
                            if z == 0:
                                act.wait_ge(s_ones, 2)
                                act.wait_ge(s_xt, 16 * 4 * (u + 1))
                            act.dma_start(xb_z[u * (NZ // UNITS) + z], zero[:]).then_inc(s_zf, 16)
                        for z in range(NZ1 if u + 1 == UNITS else 0):
                            n = min(4, TL - 4 * z)
                            act.dma_start(xs[4 * z * P:(4 * z + n) * P, :].rearrange("(p n) d -> p (n d)", n=n),
                                          zero[:, 0:n * D]).then_inc(s_zf1, 16)
                        if u + 1 < UNITS:
                            rows(u + 1, 0)
                            rows(u + 1, 1)
                        for it in range(NI):
                            if it:
                                act.wait_ge(s_s, 3 * u + it)
                                nc.scalar.copy(bankT[:, 0:256], misc[:, 0, 0:256]).then_inc(s_sn, 1)
                            if it == NI - 1 and u + 1 < UNITS:
                                exps(u + 1, 0, 0)
                                exps(u + 1, 0, 1)
                            act.wait_ge(s_us, 4 * u + it + 1)
                            nc.scalar.copy(bankT[:, 256:512], misc[:, 1, 0:256]).then_inc(s_un, 1)
                        if u + 1 < UNITS:
                            key_softmax(u + 1)
                        act.wait_ge(s_pw[0], 64)
                        act.wait_ge(s_pw[1], 64)
                        if u + 2 < UNITS:
                            act.wait_ge(s_fa, use(0, u) + GH)
                            load_stack(act, u + 2, "k")
                        for h in range(GH):
                            exps(u, 1, h)
                            if h == 5:
                                copy_outputs(u, 0)
                        if u + 2 < UNITS:
                            act.wait_ge(s_fa, use(1, u) + GH)
                            load_stack(act, u + 2, "B")
                        copy_outputs(u, 1)
                        if u + 2 < UNITS:
                            load_stack(act, u + 2, "q")
                    act_transposes(act, 1)

                @block.gpsimd
                def _(pool):
                    link = chain(pool, s_po)
                    for c in range(2):
                        link(nc.gpsimd.memset(stk["B"][96:99, c], 1.0))
                    nc.gpsimd.sem_inc(s_ones, 1)
                    link(nc.gpsimd.memset(zero[:], 0.0))
                    nc.gpsimd.sem_inc(s_ones, 1)
                    link(nc.gpsimd.memset(XT[:], 0.0))
                    nc.gpsimd.sem_inc(s_z, 1)
                    link(nc.gpsimd.memset(XR[:], 0.0))
                    nc.gpsimd.sem_inc(s_z2, 1)

                    def select(u, c):
                        for h in range(GH):
                            pool.wait_ge(s_fa, use(c, u) + h + 1)
                            e = EQ(h) if c else E[:, h, :]
                            for d in (e[:, 0:1024].rearrange("p (a n) -> p a n", a=2)[:, :, 0:P],
                                      e[:, 896:1152].rearrange("p (a n) -> p a n", a=2)):
                                ins = nc.gpsimd.affine_select(
                                    out=d, in_=d, pattern=[[0, 2], [1, P]], base=0, channel_multiplier=-1,
                                    compare_op=ALU.is_ge if c else ALU.is_gt, fill=0.0)
                            ins.then_inc(s_dq if c else s_dk, 1)

                    select(0, 0)
                    for u in range(UNITS):
                        if u + 1 < UNITS:
                            select(u + 1, 0)
                            pool.wait_ge(s_dk, GH * (u + 2))
                            pool.wait_ge(s_us, 4 * (u + 1))
                            link(nc.gpsimd.memset(XT[:], 0.0))
                            nc.gpsimd.sem_inc(s_z, 1)
                            link(nc.gpsimd.memset(XR[:], 0.0))
                            nc.gpsimd.sem_inc(s_z2, 1)
                        select(u, 1)

                @block.sync
                def _(sp):
                    sp.dma_start(X[:], a["x"].rearrange("(t p) d -> p t d", p=P)).then_inc(s_x, 16)
                    sp.dma_start(cf[:], a["cf"]).then_inc(s_w, 16)
                    sp.dma_start(E[:, 0, 0:a["cb"].shape[1]], a["cb"]).then_inc(s_w, 16)
                    for i, name in enumerate(("wk0", "wk0r", "wq0", "wq0r")):
                        sp.dma_start(wqk[:, i], a[name].rearrange("(k p) n -> p k n", p=P)).then_inc(s_w, 16)
                    sp.dma_start(wvb[:], a["wvb0"].rearrange("(k p) n -> p k n", p=P)).then_inc(s_w, 16)
                    sp.dma_start(wo0[:], a["wo0"].rearrange("(k p) n -> p k n", p=P)).then_inc(s_w, 16)
                    sp.dma_start(bb[:], a["bb"].partition_broadcast(P)).then_inc(s_w, 16)

                    store_parts(sp, 0)
                    store_parts(sp, 1)
                    load_stacks(sp, 0)
                    for u in range(UNITS):
                        for c in range(2):
                            sp.wait_ge(s_mr, 2 * u + c + 1)
                            for part in range(3):
                                sp.dma_start(stk["kq"[c]][KR + part:KR + part + 1, u % 2].rearrange("p h n -> p (h n)"),
                                             mrow[32 * part:32 * part + 32, c, :]).then_inc(s_ml, 16)
                        sp.wait_ge(s_dk, GH * (u + 1))
                        for it in range(NI):
                            sp.dma_start(edd[u % 2].rearrange("(h i) j q -> i j h q", i=NI)[it],
                                         E[:, :, OFF[it]:OFF[it] + P]).then_inc(s_ed, 16)
                        sp.wait_ge(s_ed, 16 * 4 * (u + 1))
                        if u:
                            sp.wait_ge(s_ys, 32 * u)
                        for s in range(P // SB):
                            sp.dma_start(LB[32 * s:32 * s + 32],
                                         edd[u % 2, :, SB * s:SB * (s + 1), SB * s:SB * (s + 1)]).then_inc(s_lb, 16)
                        sp.wait_ge(s_y, u + 1)
                        sp.dma_start(xsd[u % 2, 0], Y[:]).then_inc(s_ys, 16)
                        sp.dma_start(xsd[u % 2, 1], YT[:]).then_inc(s_ys, 16)
                        sp.wait_ge(s_ys, 32 * (u + 1))
                        for x, (dst, zeroed, loaded) in enumerate(((XT, s_z, s_xt), (XR, s_z2, s_xr))):
                            sp.wait_ge(zeroed, u + 1)
                            for s in range(P // SB - x):
                                c = SB * (s % 2 if x else s)
                                sp.dma_start(dst[SB * s:SB * (s + 1), :, c:c + SB],
                                             xsd[u % 2, x, 32 * s:32 * s + 32]
                                             .rearrange("e c i -> c e i")).then_inc(loaded, 16)

        w13 = sb("w13", [P, E1, KT, 2 * F1])
        w2 = sb("w2", [P, E1, FT, D])
        w1 = sb("w_lin", [P, 4, KT, D])
        bias = sb("bias_lin", [P, 3, KT])
        bo = sb("bo", [P, D])
        s_lw = sem("lin_weights")
        ig = sb("gather_slots", [P, NT, K0], U32)
        w8 = sb("w8", [P, NT, K0])
        NG = 16
        gb = sb("gb", [P, NG, D])
        s_gb = [sem(f"gathered{j}") for j in range(NG)]
        s_acc0 = sem("row_added")

        with ExitStack() as moe:
            def sbm(name, shape, dt=F32):
                return moe.enter_context(nc.sbuf_tensor(name, shape, dt))

            xn = sbm("xn_moe", [P, NT, D])
            gate0 = sbm("gate0", [P, KT, E0])
            pr = sbm("probs", [P, NT, E0])
            sel = sbm("sel", [P, NT, E0])
            selb = sbm("selb", [P, NT, E0], BF16)
            val = sbm("val", [P, NT, E0])
            slot = sbm("slot", [P, NT, E0])
            Vg = sbm("Vg", [P, NT, E0])
            Vs = sbm("Vs", [P, NT, E0])
            pick = sbm("pick", [P, 2, E0])
            mx = sbm("mx", [P, NT])
            m8 = sbm("m8", [P, NT, K0])
            V8g = sbm("V8g", [P, NT, K0])
            V8s = sbm("V8s", [P, NT, K0])
            isc = sbm("scatter_slots", [P, NT, K0], U32)
            NB = 4
            xg = sbm("xg", [P, NB, 2, D])
            wgu = sbm("wgu", [P, NB, KT, 2 * F0])
            wd = sbm("wd", [F0, NB, D])
            xgT = sbm("xgT", [P, 2, KT, CAP])
            sg = sbm("sg", [F0, 2, CAP])
            hT = sbm("hT", [F0, 2, CAP])
            yb = sbm("yb", [P, NB, 2, D])

            s_gw, s_lg, s_sub, s_ex = sem("gate_loaded"), sem("logits"), sem("logits_shifted"), sem("logits_exp")
            s_sel, s_rk, s_idx, s_sc0, s_w8 = (sem("selected"), sem("ranks"), sem("slots_ready"), sem("rows_scattered"),
                                              sem("weights_ready"))
            s_ld = [sem(f"expert_loaded{j}") for j in range(NB)]
            s_t, s_xt0, s_gu, s_sl = sem("rows_turned"), sem("rows_copied"), sem("gate_up"), sem("silu_done")
            s_h, s_y0, s_yv = sem("hidden_ready"), sem("down_done"), sem("down_copied")
            s_st = [sem(f"y_stored{j}") for j in range(NB)]

            def steps(fori, total, body):
                body(0, True, False)
                body(1, False, False)
                with fori(2, total - 1) as i:
                    body(i, False, False)
                body(total - 1, False, True)

            with nc.Block() as block:
                @block.tensor
                def _(pe):
                    pe_transposes(pe, 2, xn, xn_ready(pe, 1))
                    pe.wait_ge(s_xnT, 12)
                    pe.wait_ge(s_gw, 16)
                    for t in range(NT):
                        for k in range(KT):
                            ins = nc.tensor.matmul(scores[:, 0, t * E0:(t + 1) * E0], xnT[:, k, t * P:(t + 1) * P],
                                                   gate0[:, k, :], start=(k == 0), stop=(k == KT - 1))
                    ins.then_inc(s_lg, 1)
                    pe.wait_ge(s_sel, 1)
                    for t in range(NT):
                        for q in range(t + 1):
                            ins = nc.tensor.matmul(scores[:, 1, t * E0:(t + 1) * E0], triu if q == t else onesb,
                                                   selb[:, q, :], start=(q == 0), stop=(q == t))
                    ins.then_inc(s_rk, 1)
                    pe.wait_ge(s_w8, 1)

                    def turn(j, i):
                        pe.wait_ge(s_ld[j], (i + 1) * 48)
                        for k in range(KT):
                            for t in range(2):
                                c = (2 * k + t) * P
                                ins = nc.tensor.transpose(misc[:, j % 2, c:c + P], xg[:, j, t, k * P:(k + 1) * P], identf)
                        ins.then_inc(s_t, 1)

                    def down(j, e, wait):
                        pe.wait_ge(s_h, e + 1)
                        if wait:
                            pe.wait_ge(s_yv, e - 1)
                        for t in range(2):
                            ins = nc.tensor.matmul(scores[:, j % 2, 512 + t * D:512 + (t + 1) * D],
                                                   hT[:, j % 2, t * P:(t + 1) * P], wd[:, j, :], start=True, stop=True)
                        ins.then_inc(s_y0, 1)

                    def body(i, first, last):
                        for j in range(NB):
                            e = NB * i + j
                            if not (last and j == NB - 1):
                                turn((j + 1) % NB, i + (j + 1) // NB)
                            pe.wait_ge(s_xt0, e + 1)
                            for g in range(2):
                                for k in range(KT):
                                    ins = nc.tensor.matmul(scores[0:F0, j % 2, g * CAP:(g + 1) * CAP],
                                                           wgu[:, j, k, g * F0:(g + 1) * F0], xgT[:, j % 2, k, :],
                                                           start=(k == 0), stop=(k == KT - 1))
                            ins.then_inc(s_gu, 1)
                            if not (first and j == 0):
                                down((j - 1) % NB, e - 1, not (first and j < 3))

                    turn(0, 0)
                    steps(pe.Fori, E0 // NB, body)
                    down(NB - 1, E0 - 1, True)

                @block.vector
                def _(dve):
                    link = chain(dve, s_dv2)
                    dve_norm(dve, link, 1, xn)
                    dve.wait_ge(s_lg, 1)
                    lg = scores[:, 0, 0:512].rearrange("p (t e) -> p t e", e=E0)
                    bc = [P, NT, E0]
                    link(nc.vector.tensor_reduce(mx[:], lg, AX.X, ALU.max))
                    nc.vector.tensor_tensor(pr[:], lg, mx[:].unsqueeze(2).to_broadcast(bc), ALU.subtract).then_inc(s_sub, 1)
                    dve.wait_ge(s_ex, 1)
                    link(nc.vector.tensor_reduce(mx[:], pr[:], AX.X, ALU.add))
                    link(nc.vector.reciprocal(mx[:], mx[:]))
                    link(nc.vector.tensor_tensor(pr[:], pr[:], mx[:].unsqueeze(2).to_broadcast(bc), ALU.mult))
                    for t in range(NT):
                        ins = nc.vector.max(m8[:, t, :], pr[:, t, :])
                    link(ins)
                    for t in range(NT):
                        ins = nc.vector.match_replace(sel[:, t, :], m8[:, t, :], pr[:, t, :], -1.0)
                    link(ins)
                    nc.vector.tensor_scalar(selb[:], sel[:], 0.0, None, ALU.is_lt).then_inc(s_sel, 1)
                    dve.wait_ge(s_sel, 1)
                    dve.wait_ge(s_rk, 1)
                    rk = scores[:, 1, 0:512].rearrange("p (t e) -> p t e", e=E0)
                    link(nc.vector.tensor_scalar(slot[:], rk, float(CAP), -1.0, ALU.min, ALU.add))
                    link(nc.vector.tensor_scalar(val[:], rk, float(CAP), None, ALU.is_le))
                    link(nc.vector.tensor_tensor(slot[:], slot[:], base0.unsqueeze(1).to_broadcast(bc), ALU.add))
                    link(nc.vector.tensor_scalar(slot[:], slot[:], -1.0, BIG, ALU.mult, ALU.add))
                    link(nc.vector.tensor_tensor(Vg[:], slot[:], selb[:], ALU.mult))
                    link(nc.vector.tensor_tensor(Vs[:], Vg[:], val[:], ALU.mult))
                    for t in range(NT):
                        nc.vector.max(V8s[:, t, :], Vs[:, t, :])
                        ins = nc.vector.max(V8g[:, t, :], Vg[:, t, :])
                    link(ins)
                    nc.vector.tensor_scalar(isc[:], V8s[:], -1.0, BIG, ALU.mult, ALU.add).then_inc(s_idx, 1)
                    nc.vector.tensor_scalar(ig[:], V8g[:], -1.0, BIG, ALU.mult, ALU.add).then_inc(s_idx, 1)
                    link(nc.vector.tensor_tensor(pr[:], pr[:], val[:], ALU.mult))
                    for g in range(NT * K0):
                        t, k = g // K0, g % K0
                        if g >= 2:
                            dve.wait_ge(s_pk, g - 1)
                        nc.vector.scalar_tensor_tensor(
                            out=pick[:, g % 2, :], in0=Vg[:, t, :], scalar=V8g[:, t, k:k + 1], in1=pr[:, t, :],
                            op0=ALU.is_equal, op1=ALU.mult, accum_out=w8[:, t, k:k + 1]).then_inc(s_pk, 1)
                    dve.wait_ge(s_pk, NT * K0)
                    nc.vector.sem_inc(s_w8, 1)

                    def copy_down(j, e, n):
                        dve.wait_ge(s_y0, e + 1)
                        if n is not None:
                            dve.wait_ge(s_st[j], n * 16)
                        nc.vector.tensor_copy(yb[:, j].rearrange("p t d -> p (t d)"),
                                              scores[:, j % 2, 512:1024]).then_inc(s_yv, 1)

                    def body(i, first, last):
                        for j in range(NB):
                            e = NB * i + j
                            dve.wait_ge(s_sl, e + 1)
                            nc.vector.tensor_tensor(hT[:, j % 2, :], sg[:, j % 2, :], scores[0:F0, j % 2, CAP:2 * CAP],
                                                    ALU.mult).then_inc(s_h, 1)
                            if j:
                                copy_down(j - 1, e - 1, None if first else i)
                            elif not first:
                                copy_down(NB - 1, e - 1, None if isinstance(i, int) and i == 1 else i - 1)

                    steps(dve.Fori, E0 // NB, body)
                    copy_down(NB - 1, E0 - 1, E0 // NB - 1)

                @block.scalar
                def _(act):
                    act_std(act, 1)
                    act_transposes(act, 2)
                    act.wait_ge(s_sub, 1)
                    nc.scalar.activation(pr[:], pr[:], ACT.Exp).then_inc(s_ex, 1)
                    for i, name in enumerate(("wk1", "wv1", "wq1", "wo1")):
                        act.dma_start(w1[:, i], a[name].rearrange("(k p) n -> p k n", p=P)).then_inc(s_lw, 16)
                    for i, name in enumerate(("bk1", "bv1", "bq1")):
                        act.dma_start(bias[:, i, :], a[name].rearrange("(k p) -> p k", p=P),
                                     allow_slow_non_contiguous=True).then_inc(s_lw, 16)
                    act.dma_start(bo[:], a["bo1"].partition_broadcast(P)).then_inc(s_lw, 16)
                    for e in range(E1):
                        act.dma_start(w13[:, e], a["w13"][e].rearrange("p (k n) -> p k n", k=KT)).then_inc(s_w1, 16)
                        act.dma_start(w2[:, e], a["w2"][e].rearrange("p (k n) -> p k n", k=FT)).then_inc(s_w1, 16)

                    def copy_rows(j, e):
                        act.wait_ge(s_t, e + 1)
                        nc.scalar.copy(xgT[:, j % 2].rearrange("p k n -> p (k n)"), misc[:, j % 2, :]).then_inc(s_xt0, 1)

                    def body(i, first, last):
                        for j in range(NB):
                            e = NB * i + j
                            if not (last and j == NB - 1):
                                copy_rows(j + 1, e + 1)
                            act.wait_ge(s_gu, e + 1)
                            nc.scalar.activation(sg[:, j % 2, :], scores[0:F0, j % 2, 0:CAP], ACT.Silu).then_inc(s_sl, 1)

                    copy_rows(0, 0)
                    steps(act.Fori, E0 // NB, body)

                @block.gpsimd
                def _(pool):
                    pool.wait_ge(s_idx, 2)
                    pool.wait_ge(s_zf, 16 * NZ)
                    for t in range(NT):
                        for k in range(K0):
                            pool.indirect_dma_start(
                                out=xbuf, out_offset=bass.IndirectOffsetOnAxis(ap=isc[:, t, k:k + 1], axis=0),
                                in_=xn[:, t, :], in_offset=None, bounds_check=E0 * CAP - 1,
                                oob_is_err=False).then_inc(s_sc0, 16)

                @block.sync
                def _(sp):
                    sp.dma_start(gate0[:], a["gate0"].rearrange("(k p) n -> p k n", p=P)).then_inc(s_gw, 16)

                    def load_weights(j, e):
                        sp.dma_start(wgu[:, j], a["wgu0"][e].rearrange("p (k n) -> p k n", k=KT)).then_inc(s_ld[j], 16)
                        sp.dma_start(wd[:, j], a["wd0"][e]).then_inc(s_ld[j], 16)

                    def load_rows(j, e):
                        sp.dma_start(xg[:, j], xb_v[e].rearrange("(t p) d -> p t d", p=P)).then_inc(s_ld[j], 16)

                    for e in range(3):
                        load_weights(e, e)
                    sp.wait_ge(s_sc0, 16 * NT * K0)
                    for e in range(3):
                        load_rows(e, e)

                    def body(i, first, last):
                        for j in range(NB):
                            e = NB * i + j
                            if not (first and j == 0):
                                sp.wait_ge(s_y0, e)
                            if not (last and j > 0):
                                load_weights((j + 3) % NB, e + 3)
                                load_rows((j + 3) % NB, e + 3)
                            if not (first and j == 0):
                                jj = (j - 1) % NB
                                sp.wait_ge(s_yv, e)
                                sp.dma_start(yb_v[e - 1].rearrange("(t p) d -> p t d", p=P), yb[:, jj]).then_inc(s_st[jj], 16)

                    steps(sp.Fori, E0 // NB, body)
                    sp.wait_ge(s_yv, E0)
                    sp.dma_start(yb_v[E0 - 1].rearrange("(t p) d -> p t d", p=P), yb[:, NB - 1]).then_inc(s_st[NB - 1], 16)
                    for j in range(NB):
                        sp.wait_ge(s_st[j], 16 * (E0 // NB))

        with ExitStack() as lin:
            def sbl(name, shape, dt=F32):
                return lin.enter_context(nc.sbuf_tensor(name, shape, dt))

            xn = sbl("xn_lin", [P, NT, D])
            low = sbl("low", [P, 2, 2, T])
            relu = sbl("relu", [P, 2, 2, T])
            kv = sbl("kv", [P, 2, T])
            cum = sbl("cum", [P, 2, T])
            ctxT = sbl("ctxT", [P, KT, N])
            s_re = sem("lin_relu")
            s_pr, s_lo, s_ph, s_cx, s_oo, s_xl, s_kvr = (
                sem("lin_projected"), sem("lin_low"), sem("lin_phi"), sem("lin_context"),
                sem("lin_out"), sem("lin_added"), sem("lin_chain"))

            with nc.Block() as block:
                @block.gpsimd
                def _(pool):
                    for g in range(NT * K0):
                        t, k = g // K0, g % K0
                        if g >= NG:
                            pool.wait_ge(s_acc0, g - NG + 1)
                        pool.indirect_dma_start(
                            out=gb[:, g % NG, :], out_offset=None, in_=ybuf,
                            in_offset=bass.IndirectOffsetOnAxis(ap=ig[:, t, k:k + 1], axis=0),
                            bounds_check=E0 * CAP - 1, oob_is_err=True).then_inc(s_gb[g % NG], 16)

                @block.tensor
                def _(pe):
                    pe.wait_ge(s_lw, 16 * 8)
                    for half in range(2):
                        pe_transposes(pe, 3, xn, xn_ready(pe, 2), range(2 * half, 2 * half + 2))
                        pe.wait_ge(s_xnT, 14 + 2 * half)
                        for mt in range(KT):
                            w = 2 * half + mt
                            if w >= 2:
                                pe.wait_ge(s_cx, w - 1)
                            for c in range(3):
                                for k in range(KT):
                                    ins = nc.tensor.matmul(scores[:, w % 2, c * T:(c + 1) * T],
                                                           w1[:, c, k, mt * P:(mt + 1) * P],
                                                           xnT[:, k, half * T:(half + 1) * T],
                                                           start=(k == 0), stop=(k == KT - 1))
                            ins.then_inc(s_pr, 1)
                    for half in range(2):
                        pe.wait_ge(s_cx, 2 * half + 2)
                        for t in range(HT * half, HT * (half + 1)):
                            if t >= 2:
                                pe.wait_ge(s_xl, t - 1)
                            for k in range(KT):
                                ins = nc.tensor.matmul(misc[:, t % 2, 0:D], ctxT[:, k, t * P:(t + 1) * P], w1[:, 3, k, :],
                                                       start=(k == 0), stop=(k == KT - 1))
                            ins.then_inc(s_oo, 1)

                @block.scalar
                def _(act):
                    for half in range(2):
                        act_std(act, 2 + half, range(HT * half, HT * (half + 1)))
                        act_transposes(act, 3, range(2 * half, 2 * half + 2))
                        for mt in range(KT):
                            w, r = 2 * half + mt, mt
                            act.wait_ge(s_pr, w + 1)
                            for x, c in ((0, 0), (1, 2)):
                                ins = nc.scalar.activation(relu[:, r, x, :], scores[:, r, c * T:(c + 1) * T], ACT.Relu,
                                                           bias=bias[:, c, mt:mt + 1])
                            ins.then_inc(s_re, 1)
                            act.wait_ge(s_lo, w + 1)
                            nc.scalar.activation(low[:, r], low[:, r], ACT.Exp).then_inc(s_ph, 1)

                @block.vector
                def _(dve):
                    link = chain(dve, s_kvr)

                    def gathered(t):
                        for k in range(K0):
                            g = t * K0 + k
                            dve.wait_ge(s_gb[g % NG], 16 * (g // NG + 1))
                            if k:
                                dve.wait_ge(s_acc0, g)
                            nc.vector.scalar_tensor_tensor(out=X[:, t, :], in0=gb[:, g % NG, :], scalar=w8[:, t, k:k + 1],
                                                           in1=X[:, t, :], op0=ALU.mult, op1=ALU.add).then_inc(s_acc0, 1)

                    def window(half, mt):
                        w, r = 2 * half + mt, mt
                        dve.wait_ge(s_re, w + 1)
                        for x, c in ((0, 0), (1, 2)):
                            ins = nc.vector.tensor_scalar(low[:, r, x, :], scores[:, r, c * T:(c + 1) * T],
                                                          bias[:, c, mt:mt + 1], 0.0, ALU.add, ALU.min)
                        ins.then_inc(s_lo, 1)
                        dve.wait_ge(s_ph, w + 1)
                        link(nc.vector.tensor_tensor(relu[:, r], relu[:, r], low[:, r], ALU.add))
                        link(nc.vector.scalar_tensor_tensor(out=kv[:, r, :], in0=scores[:, r, T:2 * T],
                                                            scalar=bias[:, 1, mt:mt + 1], in1=relu[:, r, 0, :],
                                                            op0=ALU.add, op1=ALU.mult))
                        link(nc.vector.tensor_tensor_scan(cum[:, r, :], onesf.to_broadcast([P, T]), kv[:, r, :],
                                                          0.0, ALU.mult, ALU.add))
                        nc.vector.scalar_tensor_tensor(out=ctxT[:, mt, half * T:(half + 1) * T], in0=cum[:, r, :],
                                                       scalar=SCALE, in1=relu[:, r, 1, :], op0=ALU.mult,
                                                       op1=ALU.mult).then_inc(s_cx, 1)

                    def add_outputs(half):
                        x = X[:, HT * half:HT * (half + 1), :]
                        link(nc.vector.tensor_tensor(x, x, bo[:].unsqueeze(1).to_broadcast([P, HT, D]), ALU.add))
                        for t in range(HT * half, HT * (half + 1)):
                            dve.wait_ge(s_oo, t + 1)
                            nc.vector.tensor_tensor(X[:, t, :], misc[:, t % 2, 0:D], X[:, t, :], ALU.add).then_inc(s_xl, 1)

                    for t in range(HT):
                        gathered(t)
                    dve.wait_ge(s_acc0, HT * K0)
                    dve.wait_ge(s_lw, 16 * 8)
                    dve_norm(dve, link, 2, xn, range(HT))
                    gathered(HT)
                    gathered(HT + 1)
                    window(0, 0)
                    gathered(HT + 2)
                    window(0, 1)
                    gathered(HT + 3)
                    dve.wait_ge(s_acc0, NT * K0)
                    dve_norm(dve, link, 3, xn, range(HT, NT))
                    window(1, 0)
                    window(1, 1)
                    add_outputs(0)
                    add_outputs(1)
                    dve.wait_ge(s_xl, NT)

        with ExitStack() as ffn:
            def sbf(name, shape, dt=F32):
                return ffn.enter_context(nc.sbuf_tensor(name, shape, dt))

            xn = sbf("xn_ffn", [P, NT, D])
            gate1 = sbf("gate1", [P, KT, E1])
            bc = [P, NT, E1]
            pr = sbf("probs1", bc)
            mx = sbf("mx1", [P, NT])
            m8 = sbf("m81", bc)
            i8 = sbf("i81", bc, U32)
            f8 = sbf("f81", bc)
            den2 = sbf("den2", [P, NT])
            wt = sbf("wt1", [P, NT, K1])
            one = sbf("one1", [P, K1, NT, E1])
            selb = sbf("selb1", bc, BF16)
            cnt = sbf("counts1", [P, E1])
            over = sbf("over1", [P, E1, E1])
            tiles = sbf("tiles1", [P, E1])
            ends = sbf("ends1", [P, E1])
            first_slot = sbf("first_slot1", [P, E1])
            past = sbf("past1", [1, TL, E1])
            owner_f = sbf("owner_f", [1, TL])
            owner = sbf("owner", [1, TL], I32)
            pos = sbf("pos1", bc)
            at_k = sbf("at_k1", [P, K1, NT, E1])
            slot_f = sbf("slot_f1", [P, K1, NT])
            slots = sbf("slots1", [P, K1, NT], U32)
            xg = sbf("xg1", [P, 2, D])
            xgT = sbf("xgT1", [P, 2, KT, P])
            sg = sbf("sg1", [P, 2, F1])
            hid = sbf("hid1", [P, 2, F1])
            hT = sbf("hT1", [P, 2, F1])
            yb = sbf("yb1", [P, 2, D])
            gb = sbf("gb1", [P, K1 * NT, D])
            s_gw, s_lg, s_sub, s_ex = sem("gate1_loaded"), sem("logits1"), sem("shifted1"), sem("exp1")
            s_lnk, s_sel, s_rk = sem("chain1"), sem("selected1"), sem("ranks1")
            s_own, s_sl1, s_sc = sem("owners_ready"), sem("slots1_ready"), sem("rows_scattered1")
            s_ld = [sem("rows_loaded0"), sem("rows_loaded1")]
            s_xt, s_xc, s_g, s_u = sem("rows_turned1"), sem("rows_copied1"), sem("gate1_done"), sem("up1_done")
            s_sl, s_h, s_th, s_hc = sem("silu1"), sem("hidden1"), sem("hidden_turned1"), sem("hidden_copied1")
            s_y, s_yc = sem("down1"), sem("down1_copied")
            s_st = [sem("y1_stored0"), sem("y1_stored1")]
            assert K1 * NT == NG
            s_acc = sem("added1")

            def pairs_of_tiles(fori, body):
                body(0, 0)
                body(1, 1)
                body(2, 0)
                body(3, 1)
                with fori(2, TL // 2) as i:
                    body(2 * i, 0)
                    body(2 * i + 1, 1)
                body(TL - 1, (TL - 1) % 2)

            with nc.Block() as block:
                @block.sync
                def _(sp):
                    sp.dma_start(gate1[:], a["gate1"].rearrange("(k p) n -> p k n", p=P)).then_inc(s_gw, 16)

                    def load(t, j):
                        sp.dma_start(xg[:, j, :], xs_v[t]).then_inc(s_ld[j], 16)

                    def store(t, j):
                        sp.wait_ge(s_yc, t + 1)
                        sp.dma_start(ys_v[t], yb[:, j, :]).then_inc(s_st[j], 16)

                    sp.wait_ge(s_sc, 16 * K1 * NT)
                    load(0, 0)
                    load(1, 1)

                    def body(t, j):
                        if not (isinstance(t, int) and t + 2 >= TL):
                            sp.wait_ge(s_xt, t + 1)
                            load(t + 2, j)
                        if not (isinstance(t, int) and t == 0):
                            store(t - 1, 1 - j)

                    for t in range(4):
                        body(t, t % 2)
                    with sp.Fori(2, TL // 2 - 1) as i:
                        body(2 * i, 0)
                        body(2 * i + 1, 1)
                    for t in range(TL - 3, TL):
                        body(t, t % 2)
                    store(TL - 1, (TL - 1) % 2)
                    sp.wait_ge(s_acc, NT * K1)
                    sp.dma_start(out.rearrange("(t p) d -> p t d", p=P), X[:]).then_inc(s_out, 16)
                    sp.wait_ge(s_out, 16)

                @block.tensor
                def _(pe):
                    pe_transposes(pe, 4, xn, xn_ready(pe, 3))
                    pe.wait_ge(s_xnT, 20)
                    pe.wait_ge(s_gw, 16)
                    for t in range(NT):
                        for k in range(KT):
                            ins = nc.tensor.matmul(misc[:, 0, t * E1:(t + 1) * E1], xnT[:, k, t * P:(t + 1) * P],
                                                   gate1[:, k, :], start=(k == 0), stop=(k == KT - 1))
                    ins.then_inc(s_lg, 1)
                    pe.wait_ge(s_sel, 1)
                    for q in range(NT):
                        nc.tensor.matmul(scores[:, 0, T:T + E1], onesb, selb[:, q, :], start=(q == 0), stop=(q == NT - 1))
                    for t in range(NT):
                        for q in range(t + 1):
                            ins = nc.tensor.matmul(scores[:, 0, t * E1:(t + 1) * E1], triu if q == t else onesb,
                                                   selb[:, q, :], start=(q == 0), stop=(q == t))
                    ins.then_inc(s_rk, 1)
                    pe.wait_ge(s_own, 1)
                    pe.wait_ge(s_sl1, 1)
                    pe.wait_ge(s_w1, 16 * 2 * E1)

                    def turn_x(t, j):
                        if isinstance(t, int):
                            pe.wait_ge(s_ld[j], 16 * (t // 2 + 1))
                        else:
                            pe.wait_ge(s_ld[j], 8 * (t - j) + 16)
                        if not (isinstance(t, int) and t == 0):
                            pe.wait_ge(s_xc, t)
                        for k in range(KT):
                            ins = nc.tensor.transpose(misc[:, 1, k * P:(k + 1) * P], xg[:, j, k * P:(k + 1) * P], identf)
                        ins.then_inc(s_xt, 1)

                    def project(t, j, e, g, s):
                        for k in range(KT):
                            ins = nc.tensor.matmul(scores[:, j, g * F1:(g + 1) * F1], xgT[:, j, k, :],
                                                   w13[:, bass.ds(e, 1), k, g * F1:(g + 1) * F1].rearrange("p e n -> p (e n)"),
                                                   start=(k == 0), stop=(k == KT - 1))
                        ins.then_inc(s, 1)

                    def turn_h(t, j):
                        pe.wait_ge(s_h, t + 1)
                        if not (isinstance(t, int) and t < 2):
                            pe.wait_ge(s_hc, t - 1)
                        for f in range(FT):
                            ins = nc.tensor.transpose(scores[:, j, 2 * F1 + f * P:2 * F1 + (f + 1) * P],
                                                      hid[:, j, f * P:(f + 1) * P], identf)
                        ins.then_inc(s_th, 1)

                    def down(t, j, e):
                        pe.wait_ge(s_hc, t + 1)
                        if not (isinstance(t, int) and t == 0):
                            pe.wait_ge(s_yc, t)
                        for f in range(FT):
                            ins = nc.tensor.matmul(misc[:, 0, 0:D], hT[:, j, f * P:(f + 1) * P],
                                                   w2[:, bass.ds(e, 1), f, :].rearrange("p e n -> p (e n)"),
                                                   start=(f == 0), stop=(f == FT - 1))
                        ins.then_inc(s_y, 1)

                    def expert(t):
                        return pe.value_load(owner[0:1, bass.ds(t, 1)], min_val=0, max_val=E1 - 1)

                    def body(t, j):
                        if not (isinstance(t, int) and t + 1 == TL):
                            turn_x(t + 1, 1 - j)
                        pe.wait_ge(s_xc, t + 1)
                        if not (isinstance(t, int) and t < 2):
                            pe.wait_ge(s_sl, t - 1)
                        e = expert(t)
                        project(t, j, e, 0, s_g)
                        if not (isinstance(t, int) and t == 0):
                            turn_h(t - 1, 1 - j)
                        project(t, j, e, 1, s_u)
                        if not (isinstance(t, int) and t == 0):
                            down(t - 1, 1 - j, expert(t - 1))

                    turn_x(0, 0)
                    pairs_of_tiles(pe.Fori, body)
                    turn_h(TL - 1, (TL - 1) % 2)
                    down(TL - 1, (TL - 1) % 2, expert(TL - 1))

                @block.scalar
                def _(act):
                    act_std(act, 4)
                    act_transposes(act, 4)
                    act.wait_ge(s_sub, 1)
                    nc.scalar.activation(pr[:], pr[:], ACT.Exp).then_inc(s_ex, 1)

                    def copy_x(t, j):
                        act.wait_ge(s_xt, t + 1)
                        if not (isinstance(t, int) and t < 2):
                            act.wait_ge(s_u, t - 1)
                        nc.scalar.copy(xgT[:, j].rearrange("p k n -> p (k n)"), misc[:, 1, 0:KT * P]).then_inc(s_xc, 1)

                    def body(t, j):
                        if not (isinstance(t, int) and t + 1 == TL):
                            copy_x(t + 1, 1 - j)
                        act.wait_ge(s_g, t + 1)
                        if not (isinstance(t, int) and t < 2):
                            act.wait_ge(s_h, t - 1)
                        nc.scalar.activation(sg[:, j, :], scores[:, j, 0:F1], ACT.Silu).then_inc(s_sl, 1)

                    copy_x(0, 0)
                    pairs_of_tiles(act.Fori, body)

                @block.vector
                def _(dve):
                    link = chain(dve, s_lnk)
                    dve_norm(dve, link, 4, xn)
                    dve.wait_ge(s_lg, 1)
                    lg = misc[:, 0, 0:NT * E1].rearrange("p (t e) -> p t e", e=E1)
                    link(nc.vector.tensor_reduce(mx[:], lg, AX.X, ALU.max))
                    nc.vector.tensor_tensor(pr[:], lg, mx[:].unsqueeze(2).to_broadcast(bc), ALU.subtract).then_inc(s_sub, 1)
                    dve.wait_ge(s_ex, 1)
                    link(nc.vector.tensor_reduce(mx[:], pr[:], AX.X, ALU.add))
                    link(nc.vector.reciprocal(mx[:], mx[:]))
                    link(nc.vector.tensor_tensor(pr[:], pr[:], mx[:].unsqueeze(2).to_broadcast(bc), ALU.mult))
                    for t in range(NT):
                        ins = nc.vector.max(m8[:, t, :], pr[:, t, :])
                    link(ins)
                    for t in range(NT):
                        ins = nc.vector.max_index(i8[:, t, :], m8[:, t, :], pr[:, t, :])
                    link(ins)
                    link(nc.vector.tensor_copy(f8[:], i8[:]))
                    for k in range(K1):
                        ins = nc.vector.tensor_tensor(one[:, k], iota8.unsqueeze(1).to_broadcast(bc),
                                                      f8[:, :, k].unsqueeze(2).to_broadcast(bc), ALU.is_equal)
                    link(ins)
                    nc.vector.tensor_tensor(selb[:], one[:, 0], one[:, 1], ALU.add).then_inc(s_sel, 1)
                    link(nc.vector.tensor_tensor(den2[:], m8[:, :, 0], m8[:, :, 1], ALU.add))
                    link(nc.vector.reciprocal(den2[:], den2[:]))
                    link(nc.vector.tensor_tensor(wt[:], m8[:, :, 0:K1], den2[:].unsqueeze(2).to_broadcast([P, NT, K1]), ALU.mult))
                    dve.wait_ge(s_rk, 1)
                    steps_of = base0[:, 0:E1]
                    sq = [P, E1, E1]
                    link(nc.vector.tensor_scalar(cnt[:], scores[:, 0, T:T + E1], float(CAP // P), None, ALU.mult))
                    link(nc.vector.tensor_tensor(over[:], cnt[:].unsqueeze(2).to_broadcast(sq),
                                                 steps_of.unsqueeze(1).to_broadcast(sq), ALU.is_gt))
                    link(nc.vector.tensor_reduce(tiles[:], over[:], AX.X, ALU.add))
                    link(nc.vector.tensor_tensor_scan(ends[:], onesf.to_broadcast([P, E1]), tiles[:], 0.0, ALU.mult, ALU.add))
                    link(nc.vector.tensor_tensor(first_slot[:], ends[:], tiles[:], ALU.subtract))
                    link(nc.vector.tensor_scalar(first_slot[:], first_slot[:], float(P), -1.0, ALU.mult, ALU.add))
                    rk = scores[:, 0, 0:NT * E1].rearrange("p (t e) -> p t e", e=E1)
                    link(nc.vector.tensor_tensor(pos[:], rk, first_slot[:].unsqueeze(1).to_broadcast(bc), ALU.add))
                    for k in range(K1):
                        ins = nc.vector.tensor_tensor(at_k[:, k], pos[:], one[:, k], ALU.mult)
                    link(ins)
                    link(nc.vector.tensor_reduce(slot_f[:], at_k[:], AX.X, ALU.add))
                    nc.vector.tensor_copy(slots[:], slot_f[:]).then_inc(s_sl1, 1)
                    link(nc.vector.tensor_scalar(cnt[:], ends[:], float(CAP), None, ALU.mult))
                    tq = [1, TL, E1]
                    link(nc.vector.tensor_tensor(past[:], base0[0:1, 0:TL].unsqueeze(2).to_broadcast(tq),
                                                 cnt[0:1, :].unsqueeze(1).to_broadcast(tq), ALU.is_ge))
                    link(nc.vector.tensor_reduce(owner_f[:], past[:], AX.X, ALU.add))
                    nc.vector.tensor_scalar(owner[:], owner_f[:], float(E1 - 1), None, ALU.min).then_inc(s_own, 1)

                    def copy_h(t, j):
                        dve.wait_ge(s_th, t + 1)
                        nc.vector.tensor_copy(hT[:, j, :], scores[:, j, 2 * F1:3 * F1]).then_inc(s_hc, 1)

                    def copy_y(t, j):
                        dve.wait_ge(s_y, t + 1)
                        if not (isinstance(t, int) and t < 2):
                            dve.wait_ge(s_st[j], 16 * (t // 2) if isinstance(t, int) else 8 * (t - j))
                        nc.vector.tensor_copy(yb[:, j, :], misc[:, 0, 0:D]).then_inc(s_yc, 1)

                    def body(t, j):
                        if not (isinstance(t, int) and t == 0):
                            copy_h(t - 1, 1 - j)
                        dve.wait_ge(s_sl, t + 1)
                        dve.wait_ge(s_u, t + 1)
                        nc.vector.tensor_tensor(hid[:, j, :], sg[:, j, :], scores[:, j, F1:2 * F1], ALU.mult).then_inc(s_h, 1)
                        if not (isinstance(t, int) and t == 0):
                            copy_y(t - 1, 1 - j)

                    pairs_of_tiles(dve.Fori, body)
                    copy_h(TL - 1, (TL - 1) % 2)
                    copy_y(TL - 1, (TL - 1) % 2)
                    for k in range(K1):
                        for t in range(NT):
                            dve.wait_ge(s_gb[k * NT + t], 16 * (NT * K0 // NG + 1))
                            if k:
                                dve.wait_ge(s_acc, t + 1)
                            nc.vector.scalar_tensor_tensor(out=X[:, t, :], in0=gb[:, k * NT + t, :], scalar=wt[:, t, k:k + 1],
                                                           in1=X[:, t, :], op0=ALU.mult, op1=ALU.add).then_inc(s_acc, 1)

                @block.gpsimd
                def _(pool):
                    pool.wait_ge(s_sl1, 1)
                    pool.wait_ge(s_zf1, 16 * NZ1)
                    for k in range(K1):
                        for t in range(NT):
                            pool.indirect_dma_start(
                                out=xs, out_offset=bass.IndirectOffsetOnAxis(ap=slots[:, k, t:t + 1], axis=0),
                                in_=xn[:, t, :], in_offset=None, bounds_check=TL * P - 1,
                                oob_is_err=True).then_inc(s_sc, 16)
                    pool.wait_ge(s_st[0], 16 * ((TL + 1) // 2))
                    pool.wait_ge(s_st[1], 16 * (TL // 2))
                    for k in range(K1):
                        for t in range(NT):
                            pool.indirect_dma_start(
                                out=gb[:, k * NT + t, :], out_offset=None, in_=ys,
                                in_offset=bass.IndirectOffsetOnAxis(ap=slots[:, k, t:t + 1], axis=0),
                                bounds_check=TL * P - 1, oob_is_err=True).then_inc(s_gb[k * NT + t], 16)




def shape_constants():
    r = np.arange(P)
    half = HD // 2
    inv = (np.float32(1.0) / np.power(np.float32(10000.0), np.arange(half, dtype=np.float32) / np.float32(half))).astype(np.float32)
    ang = (np.arange(T, dtype=np.float32)[:, None] * inv[None, :]).astype(np.float32)
    cos, sin = np.cos(ang).astype(np.float32), np.sin(ang).astype(np.float32)
    d = r % HD
    C = cos[:, d % half].T
    S = np.where(d[:, None] < half, -1.0, 1.0) * sin[:, d % half].T
    ones2 = np.zeros((P, 64))
    ones2[:, [0, 33]] = 1
    cf = np.concatenate([np.eye(P), C, S,
                         np.tile(np.arange(E1), (P, 1)), np.ones((P, 1)), np.tile(np.arange(E0) * CAP, (P, 1)), ones2], 1).astype(np.float32)
    neg = -1e30
    causal = np.where(r[None, :] > r[:, None], neg, 0)
    strict = np.where(r[None, :] >= r[:, None], neg, 0)
    first = strict.copy()
    first[0, 0] = 0
    cb = np.concatenate([np.eye(P), causal, strict, first, r[:, None] <= r[None, :], np.ones((P, P))], 1)
    return cf, cb.astype(np.float32)


def kernel(**inputs):
    import concourse.bacc as _bacc
    from concourse.bass_utils import run_bass_kernel_spmd as _run

    g = {k: np.asarray(v) for k, v in inputs.items()}
    swap = np.arange(D).reshape(H, 2, HD // 2)[:, ::-1].reshape(-1)
    wq, wk = g["L0_attn_Wq"], g["L0_attn_Wk"]
    cf, cb = shape_constants()
    data = {
        "x": g["L0_attn_hidden_states"].reshape(N, D), "cf": cf, "cb": cb,
        "wk0": wk, "wk0r": wk[:, swap], "wq0": wq, "wq0r": wq[:, swap],
        "wvb0": np.concatenate([g["L0_attn_Wv"], g["L0_attn_Wb"]], 1), "wo0": g["L0_attn_Wo"],
        "bb": g["L0_attn_bb"], "gate0": g["L0_ffn_gate_w"].T,
        "wgu0": np.concatenate([g["L0_ffn_w_gate"], g["L0_ffn_w_up"]], 1).reshape(E0, 2 * F0, KT, P)
        .transpose(0, 3, 2, 1).reshape(E0, P, KT * 2 * F0),
        "wd0": g["L0_ffn_w_down"].transpose(0, 2, 1),
        "wk1": g["L1_attn_Wk"].T, "wv1": g["L1_attn_Wv"].T, "wq1": g["L1_attn_Wq"].T, "wo1": g["L1_attn_Wo"].T,
        "bk1": g["L1_attn_bk"], "bv1": g["L1_attn_bv"], "bq1": g["L1_attn_bq"], "bo1": g["L1_attn_bo"],
        "gate1": g["L1_ffn_gate_w"].T,
        "w13": np.concatenate([g["L1_ffn_w1"], g["L1_ffn_w3"]], 1).reshape(E1, 2 * F1, KT, P)
        .transpose(0, 3, 2, 1).reshape(E1, P, KT * 2 * F1),
        "w2": g["L1_ffn_w2"].reshape(E1, D, F1 // P, P).transpose(0, 3, 2, 1).reshape(E1, P, F1 // P * D),
    }
    nc = _bacc.Bacc("TRN2", target_bir_lowering=False, num_devices=1)
    arrays, aps = {}, {}
    for name, x in data.items():
        x = np.ascontiguousarray(x)
        arrays["in_" + name] = x
        aps[name] = nc.dram_tensor("in_" + name, x.shape, mybir.dt.from_np(x.dtype), kind="ExternalInput").ap()
    out = nc.dram_tensor("out_0", (N, D), F32, kind="ExternalOutput").ap()
    build_kernel(nc, aps, out)
    r = _run(nc, [arrays], core_ids=[0])
    return r.results[0]["out_0"].reshape(2, T, D)
```
